# Optimizing a Trainium2 kernel written in Bass

```python
import numpy as np
import jax
import jax.numpy as jnp

def _softmax(x, axis=-1):
    return jax.nn.softmax(x, axis=axis)

def _gelu(x):
    return jax.nn.gelu(x, approximate=True)

def _silu(x):
    return jax.nn.silu(x)

def _sigmoid(x):
    return jax.nn.sigmoid(x)

def _layernorm(x, axis=-1, eps=1e-05):
    m = jnp.mean(x, axis=axis, keepdims=True)
    v = jnp.var(x, axis=axis, keepdims=True)
    return (x - m) / jnp.sqrt(v + eps)

def _scatter_add(tgt, idx, src, axis=0):
    return tgt.at[idx].add(src)

def _segment_sum(src, seg, n):
    return jax.ops.segment_sum(src, seg, n)
kernel_name = 'mk_macaron_d2_jaxref_r8_882214'

def setup_inputs(seed: int=0):
    np.random.seed(seed)
    _w = jnp.asarray

    def _L0_attn_setup():
        import math
        import jax, jax.numpy as jnp
        import numpy as np
        N_HEAD = 16
        X_INT = -100.0
        Y_INT = 1.0
        POWER = 2
        DIVISOR = 1000.0

        def polymax(x):
            m = Y_INT / X_INT
            lin_cond = (x >= X_INT) & (x <= 0)
            x_lin = jnp.where(lin_cond, x, 0.0)
            lin = jnp.where(lin_cond, m * x_lin + Y_INT, 0.0)
            pos_cond = x > 0
            x_pos = jnp.where(pos_cond, x, 0.0)
            poly = jnp.where(pos_cond, x_pos ** POWER + Y_INT, 0.0)
            return (poly + lin) / DIVISOR
        key = jax.random.key(seed)
        k1, k2, k3 = jax.random.split(key, 3)
        B, T, C = (2, 256, 128)
        x = jax.random.normal(k1, (B, T, C), dtype=jnp.float32)
        W_attn = jax.random.normal(k2, (C, 3 * C), dtype=jnp.float32) * (1.0 / math.sqrt(C))
        W_proj = jax.random.normal(k3, (C, C), dtype=jnp.float32) * (1.0 / math.sqrt(C))
        return {'x': x, 'W_attn': W_attn, 'W_proj': W_proj}
    _L0_attn_in = _L0_attn_setup()

    def _L0_ffn_setup():
        import jax, jax.numpy as jnp
        import numpy as np
        H = 128
        I = 512
        E = 8
        K = 2
        B, S = (2, 256)

        def _moe_linear(x, router_w, expert_w):
            n_exp = router_w.shape[0]
            logits = x @ router_w.T
            vals, idx = jax.lax.top_k(logits, K)
            probs = jax.nn.softmax(vals, axis=-1)
            onehot = jax.nn.one_hot(idx, n_exp, dtype=x.dtype)
            combine = jnp.einsum('tk,tke->te', probs, onehot)
            out = jnp.zeros((x.shape[0], expert_w.shape[1]), x.dtype)
            for e in range(n_exp):
                out = out + combine[:, e:e + 1] * (x @ expert_w[e].T)
            return out
        key = jax.random.key(seed)
        ks = jax.random.split(key, 7)
        init = lambda k, shape, fan_in: jax.random.normal(k, shape, jnp.float32) / np.float32(np.sqrt(fan_in))
        return {'x': jax.random.normal(ks[0], (B, S, H), jnp.float32), 'router_gate': init(ks[1], (E, H), H), 'w_gate': init(ks[2], (E, I, H), H), 'router_up': init(ks[3], (E, H), H), 'w_up': init(ks[4], (E, I, H), H), 'router_down': init(ks[5], (E, I), I), 'w_down': init(ks[6], (E, H, I), I)}
    _L0_ffn_in = _L0_ffn_setup()

    def _L1_attn_setup():
        import jax, jax.numpy as jnp
        import numpy as np
        B, T, C = (2, 256, 128)
        H, L = (16, 36)
        D_HEAD = C // H
        key = jax.random.key(seed)
        ks = jax.random.split(key, 7)
        s = 0.02
        return {'x': jax.random.normal(ks[0], (B, T, C), dtype=jnp.float32), 'latent_w': jax.random.normal(ks[1], (C, L), dtype=jnp.float32) * s, 'latent_b': jax.random.normal(ks[2], (L,), dtype=jnp.float32) * s, 'Wd_w': jax.random.normal(ks[3], (H, C, L), dtype=jnp.float32) * s, 'Wd_b': jax.random.normal(ks[4], (H, L), dtype=jnp.float32) * s, 'out_w': jax.random.normal(ks[5], (H * L, C), dtype=jnp.float32) * s, 'out_b': jax.random.normal(ks[6], (C,), dtype=jnp.float32) * s}
    _L1_attn_in = _L1_attn_setup()

    def _L1_ffn_setup():
        import jax, jax.numpy as jnp
        import numpy as np
        LORA_DIM = 16
        LORA_TOKEN_INDEX = 1
        B, S, D, H = (4, 256, 128, 512)
        key = jax.random.key(seed)
        ks = jax.random.split(key, 6)
        x = jax.random.normal(ks[0], (B, S, D), dtype=jnp.float32)
        W1 = jax.random.normal(ks[1], (H, D), dtype=jnp.float32) * 0.02
        b1 = jnp.zeros((H,), dtype=jnp.float32)
        W2 = jax.random.normal(ks[2], (D, H), dtype=jnp.float32) * 0.02
        b2 = jnp.zeros((D,), dtype=jnp.float32)
        scale = jnp.asarray(0.001, dtype=jnp.float32)
        return {'x': x, 'W1': W1, 'b1': b1, 'W2': W2, 'b2': b2, 'scale': scale}
    _L1_ffn_in = _L1_ffn_setup()
    _d = {'L0_attn_x': _L0_attn_in['x'], 'L0_attn_W_attn': _L0_attn_in['W_attn'], 'L0_attn_W_proj': _L0_attn_in['W_proj'], 'L0_ffn_router_gate': _L0_ffn_in['router_gate'], 'L0_ffn_w_gate': _L0_ffn_in['w_gate'], 'L0_ffn_router_up': _L0_ffn_in['router_up'], 'L0_ffn_w_up': _L0_ffn_in['w_up'], 'L0_ffn_router_down': _L0_ffn_in['router_down'], 'L0_ffn_w_down': _L0_ffn_in['w_down'], 'L1_attn_latent_w': _L1_attn_in['latent_w'], 'L1_attn_latent_b': _L1_attn_in['latent_b'], 'L1_attn_Wd_w': _L1_attn_in['Wd_w'], 'L1_attn_Wd_b': _L1_attn_in['Wd_b'], 'L1_attn_out_w': _L1_attn_in['out_w'], 'L1_attn_out_b': _L1_attn_in['out_b'], 'L1_ffn_W1': _L1_ffn_in['W1'], 'L1_ffn_b1': _L1_ffn_in['b1'], 'L1_ffn_W2': _L1_ffn_in['W2'], 'L1_ffn_b2': _L1_ffn_in['b2'], 'L1_ffn_scale': _L1_ffn_in['scale']}
    _x0 = _d['L0_attn_x']
    _d['L0_attn_x'] = jax.random.normal(jax.random.fold_in(jax.random.key(seed), 1), (4, 1024, 128), dtype=_x0.dtype)
    del _x0
    return _d

def reference(L0_attn_x, L0_attn_W_attn, L0_attn_W_proj, L0_ffn_router_gate, L0_ffn_w_gate, L0_ffn_router_up, L0_ffn_w_up, L0_ffn_router_down, L0_ffn_w_down, L1_attn_latent_w, L1_attn_latent_b, L1_attn_Wd_w, L1_attn_Wd_b, L1_attn_out_w, L1_attn_out_b, L1_ffn_W1, L1_ffn_b1, L1_ffn_W2, L1_ffn_b2, L1_ffn_scale):

    def _L0_attn_ref(x, W_attn, W_proj):
        import math
        import jax, jax.numpy as jnp
        import numpy as np
        N_HEAD = 16
        X_INT = -100.0
        Y_INT = 1.0
        POWER = 2
        DIVISOR = 1000.0

        def polymax(x):
            m = Y_INT / X_INT
            lin_cond = (x >= X_INT) & (x <= 0)
            x_lin = jnp.where(lin_cond, x, 0.0)
            lin = jnp.where(lin_cond, m * x_lin + Y_INT, 0.0)
            pos_cond = x > 0
            x_pos = jnp.where(pos_cond, x, 0.0)
            poly = jnp.where(pos_cond, x_pos ** POWER + Y_INT, 0.0)
            return (poly + lin) / DIVISOR
        B, T, C = x.shape
        H = N_HEAD
        hd = C // H
        qkv = x @ W_attn
        q, k, v = jnp.split(qkv, 3, axis=-1)
        q = q.reshape(B, T, H, hd).transpose(0, 2, 1, 3)
        k = k.reshape(B, T, H, hd).transpose(0, 2, 1, 3)
        v = v.reshape(B, T, H, hd).transpose(0, 2, 1, 3)
        att = jnp.einsum('bhid,bhjd->bhij', q, k) * (1.0 / math.sqrt(hd))
        causal = jnp.tril(jnp.ones((T, T), dtype=bool))
        att = jnp.where(causal[None, None], att, -jnp.inf)
        att = polymax(att)
        y = jnp.einsum('bhij,bhjd->bhid', att, v)
        y = y.transpose(0, 2, 1, 3).reshape(B, T, C)
        return y @ W_proj

    def _L0_ffn_ref(x, router_gate, w_gate, router_up, w_up, router_down, w_down):
        import jax, jax.numpy as jnp
        import numpy as np
        H = 128
        I = 512
        E = 8
        K = 2
        B, S = (2, 256)

        def _moe_linear(x, router_w, expert_w):
            n_exp = router_w.shape[0]
            logits = x @ router_w.T
            vals, idx = jax.lax.top_k(logits, K)
            probs = jax.nn.softmax(vals, axis=-1)
            onehot = jax.nn.one_hot(idx, n_exp, dtype=x.dtype)
            combine = jnp.einsum('tk,tke->te', probs, onehot)
            out = jnp.zeros((x.shape[0], expert_w.shape[1]), x.dtype)
            for e in range(n_exp):
                out = out + combine[:, e:e + 1] * (x @ expert_w[e].T)
            return out
        b, s, h = x.shape
        xt = x.reshape(b * s, h)
        g = _moe_linear(xt, router_gate, w_gate)
        u = _moe_linear(xt, router_up, w_up)
        inter = jax.nn.silu(g) * u
        d = _moe_linear(inter, router_down, w_down)
        return d.reshape(b, s, h)

    def _L1_attn_ref(x, latent_w, latent_b, Wd_w, Wd_b, out_w, out_b):
        import jax, jax.numpy as jnp
        import numpy as np
        B, T, C = (2, 256, 128)
        H, L = (16, 36)
        D_HEAD = C // H
        b, t, c = x.shape
        h = Wd_w.shape[0]
        d_head = c // h
        Wdkv = x @ latent_w + latent_b
        q = jnp.einsum('btc,hcl->bhtl', x, Wd_w) + Wd_b[None, :, None, :]
        scores = jnp.einsum('bhtl,bsl->bhts', q, Wdkv) / jnp.asarray(np.sqrt(d_head), dtype=x.dtype)
        causal = jnp.tril(jnp.ones((t, t), dtype=bool))
        scores = jnp.where(causal[None, None, :, :], scores, -jnp.inf)
        attn = jax.nn.softmax(scores, axis=-1)
        y = jnp.einsum('bhts,bsl->bhtl', attn, Wdkv)
        z = jnp.transpose(y, (0, 2, 1, 3)).reshape(b, t, h * Wdkv.shape[-1])
        return z @ out_w + out_b

    def _L1_ffn_ref(x, W1, b1, W2, b2, scale):
        import jax, jax.numpy as jnp
        import numpy as np
        LORA_DIM = 16
        LORA_TOKEN_INDEX = 1
        B, S, D, H = (4, 256, 128, 512)
        Bx, Sx, Dx = x.shape
        Hx = W1.shape[0]
        lt = jax.lax.dynamic_slice_in_dim(x, LORA_TOKEN_INDEX, LORA_DIM, axis=1)
        even = lt[:, ::2, :]
        odd = lt[:, 1::2, :]
        m1 = (even[:, :4, :, None] * odd[:, :4, None, :]).reshape(Bx, Hx, Dx)
        m2 = (even[:, 4:, :, None] * odd[:, 4:, None, :]).reshape(Bx, Dx, Hx)
        h = jnp.einsum('bsd,hd->bsh', x, W1) + scale * jnp.einsum('bsd,bhd->bsh', x, m1) + b1
        h = jax.nn.gelu(h, approximate=False)
        out = jnp.einsum('bsh,oh->bso', h, W2) + scale * jnp.einsum('bsh,boh->bso', h, m2) + b2
        return out
    x = L0_attn_x
    x = x + 0.5 * _L0_ffn_ref(_layernorm(x, axis=-1), L0_ffn_router_gate, L0_ffn_w_gate, L0_ffn_router_up, L0_ffn_w_up, L0_ffn_router_down, L0_ffn_w_down)
    x = x + _L0_attn_ref(_layernorm(x, axis=-1), L0_attn_W_attn, L0_attn_W_proj)
    x = x + 0.5 * _L0_ffn_ref(_layernorm(x, axis=-1), L0_ffn_router_gate, L0_ffn_w_gate, L0_ffn_router_up, L0_ffn_w_up, L0_ffn_router_down, L0_ffn_w_down)
    x = x + 0.5 * _L1_ffn_ref(_layernorm(x, axis=-1), L1_ffn_W1, L1_ffn_b1, L1_ffn_W2, L1_ffn_b2, L1_ffn_scale)
    x = x + _L1_attn_ref(_layernorm(x, axis=-1), L1_attn_latent_w, L1_attn_latent_b, L1_attn_Wd_w, L1_attn_Wd_b, L1_attn_out_w, L1_attn_out_b)
    x = x + 0.5 * _L1_ffn_ref(_layernorm(x, axis=-1), L1_ffn_W1, L1_ffn_b1, L1_ffn_W2, L1_ffn_b2, L1_ffn_scale)
    return x

_drawn_inputs = setup_inputs


def setup_inputs(seed=0):
    import zlib

    import numpy as np

    out = dict(_drawn_inputs(seed))
    spreads = {'L1_ffn_b1': (0.0, 0.345), 'L1_ffn_b2': (0.0, 0.1)}
    factors = {'L1_attn_latent_w': 5.057,
     'L1_attn_latent_b': 7.275,
     'L1_attn_Wd_w': 8.0,
     'L1_attn_Wd_b': 8.0,
     'L1_attn_out_w': 3.94,
     'L1_attn_out_b': 2.729}
    for name, (base, spread) in spreads.items():
        noise = np.random.default_rng([zlib.crc32(name.encode()), seed]).standard_normal(out[name].shape)
        drawn = base * np.exp(spread * noise) if base else spread * noise
        out[name] = jnp.asarray(drawn.astype(out[name].dtype))
    for name, factor in factors.items():
        out[name] = (out[name] * factor).astype(out[name].dtype)
    return out
```

```python
import concourse.bass as bass
from concourse import mybir
from contextlib import ExitStack

F32 = mybir.dt.float32
F32R = mybir.dt.float32r
BF16 = mybir.dt.bfloat16
U32 = mybir.dt.uint32
ALU = mybir.AluOpType
ACT = mybir.ActivationFunctionType
AX = mybir.AxisListType

P = 128
BATCH, SEQ, DIM = 4, 1024, 128
TILES = BATCH * SEQ // P
BT = SEQ // P
EXPERTS, INNER = 8, 512
KC = INNER // P
HALF = 512
HEADS, HD = 16, 8
GROUPS, GH = 4, 4
LAT = 36
EPS = 1e-5
SCORE_SCALE = HD ** -0.5

LEAD = 64


def after(n):
    return n + 1 + LEAD


def at(t):
    return bass.ds(t, 1)


def f32(ap):
    return ap.bitcast(F32)


class Links:

    def __init__(self, eng, sem, per):
        self.eng, self.sem, self.per = eng, sem, per
        self.item, self.k = 0, per

    def start(self, item):
        assert self.k == self.per, (self.k, self.per)
        self.item, self.k = item, 0

    def link(self, ins):
        ins.then_inc(self.sem, 1)
        self.eng.wait_ge(self.sem, self.item * self.per + (self.k + 1 + LEAD))
        self.k += 1


def layernorm_scales(act, dve, nc, t, sqrt_ready):
    if act is not None:
        act.activation(t.rstd[:, :], t.stats[:, :, 1], ACT.Sqrt, bias=t.consts[:, 0:1]).then_inc(sqrt_ready, 1)
    if dve is not None:
        dve.wait_ge(sqrt_ready, 1)
        dve.reciprocal(t.rstd[:, :], t.rstd[:, :]).then_inc(sqrt_ready, 1)
        dve.wait_ge(sqrt_ready, 2)


class Semaphores:

    def __init__(self, ctx, nc, tag):
        self.ctx, self.nc, self.tag, self.all = ctx, nc, tag, []

    def __call__(self, name):
        s = self.ctx.enter_context(self.nc.semaphore(f"{self.tag}_{name}"))
        self.all.append(s)
        return s

    def clear(self):
        with self.nc.Block() as block:
            @block.sync
            def _(sp):
                for s in self.all:
                    sp.sem_clear(s)


class ResidualAdd:

    def __init__(self, ctx, nc, sem, t, tag, tiles):
        self.t, self.tiles = t, tiles
        self.xo = ctx.enter_context(nc.sbuf_tensor(f"{tag}_xo", [P, 2, tiles, DIM], F32))
        self.stat6 = ctx.enter_context(nc.sbuf_tensor(f"{tag}_stat6", [P, 2, tiles, 6], F32))
        self.aggr = ctx.enter_context(nc.sbuf_tensor(f"{tag}_aggr", [P, 2, tiles, 2], F32))
        self.xo_ready, self.stat_ready, self.pause = sem("xo_ready"), sem("stat_ready"), sem("dve_pause")

    def prime(self, dve):
        dve.sem_inc(self.xo_ready, LEAD)
        dve.sem_inc(self.stat_ready, LEAD)

    def add(self, dve, item, q, tile, bank):
        t, some = self.t, bass.ds(tile, self.tiles)
        dve.tensor_tensor(self.xo[:, q, :, :], bank.rearrange("p (j c) -> p j c", c=DIM), t.X[:, some, :],
                          ALU.add).then_inc(self.xo_ready, 1)
        dve.wait_ge(self.xo_ready, after(item))
        dve.sem_inc(self.pause, 1)
        dve.tensor_copy(t.X[:, some, :], self.xo[:, q, :, :])
        for j in range(self.tiles):
            ins = dve.bn_stats(self.stat6[:, q, j, :], self.xo[:, q, j, :])
        ins.then_inc(self.stat_ready, 1)
        dve.wait_ge(self.stat_ready, after(item * 2))
        dve.sem_inc(self.pause, 1)
        for j in range(self.tiles):
            ins = dve.bn_aggr(self.aggr[:, q, j, :], self.stat6[:, q, j, :])
        ins.then_inc(self.stat_ready, 1)
        dve.wait_ge(self.stat_ready, after(item * 2 + 1))
        dve.sem_inc(self.pause, 1)
        dve.tensor_copy(t.stats[:, some, :], self.aggr[:, q, :, :])


class Shared:
    pass


def load_input(nc, t, d):
    with ExitStack() as ctx:
        stat6 = ctx.enter_context(nc.sbuf_tensor("stat6", [P, TILES, 6], F32))
        sem = Semaphores(ctx, nc, "in")
        x_in, c_in, stat_ready = [sem(f"x_in{i}") for i in range(2)], sem("const_in"), sem("stat_ready")
        with nc.Block() as block:
            @block.sync
            def _(sp):
                for i in range(2):
                    sp.dma_start(t.X[:, 16 * i:16 * i + 16, :],
                                 d["x"].rearrange("(n p) c -> p n c", p=P)[:, 16 * i:16 * i + 16, :]).then_inc(x_in[i], 16)
                sp.dma_start(t.consts[:, :], d["consts"]).then_inc(c_in, 16)

            @block.vector
            def _(dve):
                for i in range(TILES):
                    if i % 16 == 0:
                        dve.wait_ge(x_in[i // 16], 16)
                    dve.bn_stats(stat6[:, i, :], t.X[:, i, :]).then_inc(stat_ready, 1)
                for i in range(TILES):
                    dve.wait_ge(stat_ready, i + 1)
                    dve.bn_aggr(t.stats[:, i, :], stat6[:, i, :])
                dve.wait_ge(c_in, 16)
                dve.tensor_copy(t.bconsts[:, :], t.consts[:, C_IDENT:CONSTS])
        sem.clear()


def load_experts(nc, t, d, tag):
    with ExitStack() as ctx:
        stage = [ctx.enter_context(nc.sbuf_tensor(f"{tag}_stage{i}", [P, EXPERTS * INNER], F32)) for i in range(3)]
        rstage = ctx.enter_context(nc.sbuf_tensor(f"{tag}_rstage", [P, 2 * EXPERTS + KC * EXPERTS], F32))
        sem = Semaphores(ctx, nc, f"{tag}_load")
        w_in, high_ready = [sem(f"w_in{i}") for i in range(4)], sem("high_ready")
        with nc.Block() as block:
            @block.sync
            def _(sp):
                sp.dma_start(rstage[:, :], d["routers"]).then_inc(w_in[3], 16)
                for i, name in enumerate(("w_gate", "w_up", "w_down")):
                    sp.dma_start(stage[i][:, :], d[name]).then_inc(w_in[i], 16)

            @block.scalar
            def _(act):
                act.wait_ge(w_in[3], 16)
                act.activation(t.rout[0][:, :], rstage[:, :], ACT.Copy).then_inc(high_ready, 1)
                for i in range(3):
                    act.wait_ge(w_in[i], 16)
                    act.activation(t.W[i][0][:, :], stage[i][:, :], ACT.Copy).then_inc(high_ready, 1)

            @block.vector
            def _(dve):
                dve.wait_ge(high_ready, 1)
                dve.tensor_tensor(t.rout[1][:, :], rstage[:, :], f32(t.rout[0][:, :]), ALU.subtract)
                for i in range(3):
                    dve.wait_ge(high_ready, i + 2)
                    dve.tensor_tensor(t.W[i][1][:, :], stage[i][:, :], f32(t.W[i][0][:, :]), ALU.subtract)
        sem.clear()


def moe_phase(nc, t, tag):
    with ExitStack() as ctx:
        def sb(name, shape, dt=F32):
            return ctx.enter_context(nc.sbuf_tensor(f"{tag}_{name}", shape, dt))

        sem = Semaphores(ctx, nc, tag)

        xn = sb("xn", [P, 2, DIM])
        xh = [sb(f"xh{i}", [P, P], F32R) for i in range(2)]
        xl = [sb(f"xl{i}", [P, P], F32R) for i in range(2)]
        logits = sb("logits", [P, 2, 16])
        top = sb("top", [P, 2, 2, 8])
        topi = sb("topi", [P, 2, 2, 8], U32)
        pick = sb("pick", [P, 2, 2, 2])
        gap = sb("gap", [P, 2, 2])
        prob = sb("prob", [P, 2, 2, 2])
        part = sb("part", [P, 2, 2, 2, EXPERTS])
        comb = sb("comb", [P, 2, 2, EXPERTS])
        dlogits = sb("dlogits", [P, 2, 8])
        dtop = sb("dtop", [P, 2, 8])
        dtopi = sb("dtopi", [P, 2, 8], U32)
        dpick = sb("dpick", [P, 2, 2])
        dgap = sb("dgap", [P, 2, 1])
        dprob = sb("dprob", [P, 2, 2])
        dhalf = sb("dhalf", [P, 2, 2])
        dpart = sb("dpart", [P, 2, 2, EXPERTS])
        dcomb = sb("dcomb", [P, 2, EXPERTS])
        acc = sb("acc", [P, 2, 2, INNER])
        sig = sb("sig", [P, 2, INNER])
        gated = sb("gated", [P, 2, INNER])
        inter = sb("inter", [P, 2, INNER])
        ih = [sb(f"ih{i}", [P, INNER], F32R) for i in range(2)]
        il = [sb(f"il{i}", [P, INNER], F32R) for i in range(2)]
        yacc = sb("yacc", [P, 2, DIM])
        stat6 = sb("stat6", [P, 2, 6])

        ps = [ctx.enter_context(nc.psum_tensor(f"{tag}_ps{i}", [P, HALF], F32)) for i in range(8)]
        expert_bank, a_bank, t_bank, y_bank = ps[0:4], ps[4], ps[5], ps[6:8]

        rstd_ready = sem("rstd_ready")
        xn_ready, xt_ready, xh_ready, xl_ready = sem("xn_ready"), sem("xt_ready"), sem("xh_ready"), sem("xl_ready")
        lg_ready, lg_copied, gap_ready, prob_ready, comb_ready = (
            sem("lg_ready"), sem("lg_copied"), sem("gap_ready"), sem("prob_ready"), sem("comb_ready"))
        prod_ready, first_used, prod_used = sem("prod_ready"), sem("first_used"), sem("prod_used")
        sig_ready, gated_ready, inter_ready = sem("sig_ready"), sem("gated_ready"), sem("inter_ready")
        it_ready, ih_ready, il_ready = sem("it_ready"), sem("ih_ready"), sem("il_ready")
        dlg_ready, dlg_copied, dgap_ready, dprob_ready, dcomb_ready = (
            sem("dlg_ready"), sem("dlg_copied"), sem("dgap_ready"), sem("dprob_ready"), sem("dcomb_ready"))
        y_ready, y_used = sem("y_ready"), sem("y_used")
        dve_a, dve_c, dve_y = sem("dve_a"), sem("dve_c"), sem("dve_y")
        pool_a, pool_c = sem("pool_a"), sem("pool_c")
        dve_pause, pool_pause = sem("dve_pause"), sem("pool_pause")
        aggr = sb("aggr", [P, 2, 2])

        ND = 2 * EXPERTS - 2
        wg, wu, wd = t.W

        def steps(eng, body, first, last):
            body(0, 0)
            body(1, 1)
            with eng.Fori(0, (TILES - 4) // 2) as i:
                for q in range(2):
                    body(i * 2 + (2 + q), q)
            body(TILES - 2, 0)
            body(TILES - 1, 1)

        with nc.Block() as block:
            @block.tensor
            def _(pe):
                for s in (xt_ready, lg_ready, prod_ready, it_ready, dlg_ready, y_ready):
                    pe.sem_inc(s, LEAD)

                def transpose_x(n, q):
                    pe.wait_ge(xn_ready, after(n))
                    pe.wait_ge(lg_copied, after(n - 1))
                    pe.transpose(a_bank[:, 0:P], xn[:, q, :], t.ident).then_inc(xt_ready, 1)

                def route_gu(n, q):
                    pe.wait_ge(xh_ready, after(n))
                    pe.wait_ge(xl_ready, after(n))
                    for k, (a, b) in enumerate(((xh, 0), (xh, 1), (xl, 0))):
                        last = pe.matmul(a_bank[:, P:P + 16], a[q][:, :], t.rout[b][:, 0:16], start=k == 0, stop=k == 2)
                    last.then_inc(lg_ready, 1)

                def product(n, q, j):
                    if j < 4:
                        pe.wait_ge(prod_used, after(n * ND + (j - 4)))
                    elif j < 6:
                        pe.wait_ge(first_used, after(n * 2 + (j - 4)))
                    else:
                        pe.wait_ge(prod_used, after(n * ND + (j - 6)))
                    w, e = (wg, wu)[j % 2], j // 2
                    cols = slice(e * INNER, (e + 1) * INNER)
                    for k, (a, b) in enumerate(((xh, 0), (xh, 1), (xl, 0))):
                        last = pe.matmul(expert_bank[j % 4][:, :], a[q][:, :], w[b][:, cols], start=k == 0, stop=k == 2)
                    last.then_inc(prod_ready, 1)

                def transpose_inter(n, q):
                    pe.wait_ge(inter_ready, after(n))
                    pe.wait_ge(dlg_copied, after(n - 1))
                    for c in range(KC):
                        last = pe.transpose(t_bank[:, c * P:(c + 1) * P], inter[:, q, c * P:(c + 1) * P], t.ident)
                    last.then_inc(it_ready, 1)

                def route_down(n, q):
                    pe.wait_ge(ih_ready, after(n))
                    pe.wait_ge(il_ready, after(n))
                    k = 0
                    for c in range(KC):
                        rows = slice(c * P, (c + 1) * P)
                        rcol = slice(16 + c * EXPERTS, 16 + (c + 1) * EXPERTS)
                        for a, b in ((ih, 0), (ih, 1), (il, 0)):
                            last = pe.matmul(t_bank[:, 0:EXPERTS], a[q][:, rows], t.rout[b][:, rcol], start=k == 0, stop=k == 11)
                            k += 1
                    last.then_inc(dlg_ready, 1)

                def down(n, q):
                    for h in range(2):
                        pe.wait_ge(y_used, after((n - 1) * 2 + h))
                        k = 0
                        for c in range(KC):
                            rows = slice(c * P, (c + 1) * P)
                            cols = slice(c * 1024 + h * HALF, c * 1024 + (h + 1) * HALF)
                            for a, b in ((ih, 0), (ih, 1), (il, 0)):
                                last = pe.matmul(y_bank[h][:, :], a[q][:, rows], wd[b][:, cols], start=k == 0, stop=k == 11)
                                k += 1
                        last.then_inc(y_ready, 1)

                def body(n, q):
                    nxt = not (isinstance(n, int) and n == TILES - 1)
                    bef = not (isinstance(n, int) and n == 0)
                    if nxt:
                        transpose_x(n + 1, 1 - q)
                    for j in range(0, 6):
                        product(n, q, j)
                    if bef:
                        transpose_inter(n - 1, 1 - q)
                    for j in range(6, 10):
                        product(n, q, j)
                    if nxt:
                        route_gu(n + 1, 1 - q)
                    for j in range(10, 12):
                        product(n, q, j)
                    if bef:
                        route_down(n - 1, 1 - q)
                    for j in range(12, 16):
                        product(n, q, j)
                    if bef:
                        down(n - 1, 1 - q)

                transpose_x(0, 0)
                route_gu(0, 0)
                steps(pe, body, None, None)
                transpose_inter(TILES - 1, 1)
                route_down(TILES - 1, 1)
                down(TILES - 1, 1)

            @block.scalar
            def _(act):
                layernorm_scales(act, None, nc, t, rstd_ready)
                for s in (xh_ready, prob_ready, first_used, sig_ready, ih_ready, dprob_ready):
                    act.sem_inc(s, LEAD)

                def high_x(n, q):
                    act.wait_ge(xt_ready, after(n))
                    act.wait_ge(prod_ready, after((n - 2) * 16 + 15))
                    act.activation(xh[q][:, :], a_bank[:, 0:P], ACT.Copy).then_inc(xh_ready, 1)

                def probs(n, q):
                    act.wait_ge(gap_ready, after(n * 2 + 1))
                    act.wait_ge(comb_ready, after(n - 2))
                    act.activation(prob[:, q, :, 0], gap[:, q, :], ACT.Sigmoid)
                    act.activation(prob[:, q, :, 1], gap[:, q, :], ACT.Sigmoid, scale=-1.0).then_inc(prob_ready, 1)

                def first(n, q):
                    act.wait_ge(comb_ready, after(n))
                    act.wait_ge(inter_ready, after(n - 2))
                    for j in range(2):
                        act.wait_ge(prod_ready, after(n * 16 + j))
                        act.activation(acc[:, q, j, :], expert_bank[j][:, :], ACT.Copy,
                                       scale=comb[:, q, j, 0:1]).then_inc(first_used, 1)

                def sigmoid(n, q):
                    act.wait_ge(prod_used, after(n * ND + (ND - 2)))
                    act.wait_ge(gated_ready, after(n - 2))
                    act.activation(sig[:, q, :], acc[:, q, 0, :], ACT.Sigmoid).then_inc(sig_ready, 1)

                def high_inter(n, q):
                    act.wait_ge(it_ready, after(n))
                    act.wait_ge(y_ready, after((n - 2) * 2 + 1))
                    act.activation(ih[q][:, :], t_bank[:, :], ACT.Copy).then_inc(ih_ready, 1)

                def dprobs(n, q):
                    act.wait_ge(dgap_ready, after(n * 2 + 1))
                    act.wait_ge(dcomb_ready, after(n - 2))
                    act.activation(dprob[:, q, 0:1], dgap[:, q, :], ACT.Sigmoid)
                    act.activation(dprob[:, q, 1:2], dgap[:, q, :], ACT.Sigmoid, scale=-1.0).then_inc(dprob_ready, 1)

                def body(n, q):
                    nxt = not (isinstance(n, int) and n == TILES - 1)
                    bef = not (isinstance(n, int) and n == 0)
                    if nxt:
                        high_x(n + 1, 1 - q)
                    first(n, q)
                    if bef:
                        high_inter(n - 1, 1 - q)
                    if nxt:
                        probs(n + 1, 1 - q)
                    if bef:
                        dprobs(n - 1, 1 - q)
                    sigmoid(n, q)

                high_x(0, 0)
                probs(0, 0)
                steps(act, body, None, None)
                high_inter(TILES - 1, 1)
                dprobs(TILES - 1, 1)

            @block.gpsimd
            def _(pool):
                for s in (comb_ready, gated_ready, inter_ready, dcomb_ready, pool_a, pool_c):
                    pool.sem_inc(s, LEAD)
                own_a, own_c = Links(pool, pool_a, 1), Links(pool, pool_c, 2)

                def combine(n, q):
                    own_a.start(n)
                    pool.wait_ge(prob_ready, after(n))
                    pool.wait_ge(prod_used, after((n - 2) * ND + (ND - 1)))
                    pool.wait_ge(first_used, after((n - 2) * 2 + 1))
                    pool.sem_inc(pool_pause, 1)
                    for r in range(2):
                        for k in range(2):
                            ins = pool.tensor_scalar(part[:, q, r, k, :], t.iota8, pick[:, q, r, k:k + 1],
                                                     prob[:, q, r, k:k + 1], ALU.is_equal, ALU.mult)
                    own_a.link(ins)
                    pool.tensor_tensor(comb[:, q, :, :], part[:, q, :, 0, :], part[:, q, :, 1, :], ALU.add).then_inc(comb_ready, 1)

                def dcombine(n, q):
                    own_c.start(n)
                    pool.wait_ge(dprob_ready, after(n))
                    pool.wait_ge(y_used, after((n - 2) * 2 + 1))
                    pool.sem_inc(pool_pause, 1)
                    own_c.link(pool.tensor_scalar(dhalf[:, q, :], dprob[:, q, :], 0.5, None, ALU.mult))
                    pool.sem_inc(pool_pause, 1)
                    for k in range(2):
                        ins = pool.tensor_scalar(dpart[:, q, k, :], t.iota8, dpick[:, q, k:k + 1],
                                                 dhalf[:, q, k:k + 1], ALU.is_equal, ALU.mult)
                    own_c.link(ins)
                    pool.tensor_tensor(dcomb[:, q, :], dpart[:, q, 0, :], dpart[:, q, 1, :], ALU.add).then_inc(dcomb_ready, 1)

                def gate(n, q):
                    pool.wait_ge(sig_ready, after(n))
                    pool.tensor_tensor(gated[:, q, :], acc[:, q, 0, :], sig[:, q, :], ALU.mult).then_inc(gated_ready, 1)
                    pool.wait_ge(gated_ready, after(n))
                    pool.wait_ge(prod_used, after(n * ND + (ND - 1)))
                    pool.wait_ge(it_ready, after(n - 2))
                    pool.tensor_tensor(inter[:, q, :], gated[:, q, :], acc[:, q, 1, :], ALU.mult).then_inc(inter_ready, 1)

                def body(n, q):
                    nxt = not (isinstance(n, int) and n == TILES - 1)
                    bef = not (isinstance(n, int) and n == 0)
                    if nxt:
                        combine(n + 1, 1 - q)
                    if bef:
                        dcombine(n - 1, 1 - q)
                    gate(n, q)

                combine(0, 0)
                steps(pool, body, None, None)
                dcombine(TILES - 1, 1)

            @block.vector
            def _(dve):
                layernorm_scales(None, dve, nc, t, rstd_ready)
                for s in (xn_ready, xl_ready, lg_copied, gap_ready, prod_used, il_ready, dlg_copied, dgap_ready,
                          y_used, dve_a, dve_c, dve_y):
                    dve.sem_inc(s, LEAD)
                own_a, own_c, own_y = Links(dve, dve_a, 1), Links(dve, dve_c, 1), Links(dve, dve_y, EXPERTS)

                def normalise(n, q):
                    dve.wait_ge(xt_ready, after(n - 2))
                    dve.tensor_scalar(xn[:, q, :], t.X[:, at(n), :], t.stats[:, at(n), 0], t.rstd[:, at(n)],
                                      ALU.subtract, ALU.mult).then_inc(xn_ready, 1)

                def low_x(n, q):
                    dve.wait_ge(xh_ready, after(n))
                    dve.tensor_tensor(xl[q][:, :], a_bank[:, 0:P], f32(xh[q][:, :]), ALU.subtract).then_inc(xl_ready, 1)

                def best_gu(n, q):
                    own_a.start(n)
                    dve.wait_ge(lg_ready, after(n))
                    dve.tensor_copy(logits[:, q, :], a_bank[:, P:P + 16]).then_inc(lg_copied, 1)
                    dve.wait_ge(lg_copied, after(n))
                    dve.sem_inc(dve_pause, 1)
                    for r in range(2):
                        ins = dve.max(top[:, q, r, :], logits[:, q, 8 * r:8 * r + 8])
                    own_a.link(ins)
                    dve.wait_ge(comb_ready, after(n - 2))
                    dve.sem_inc(dve_pause, 1)
                    for r in range(2):
                        ins = dve.max_index(topi[:, q, r, :], top[:, q, r, :], logits[:, q, 8 * r:8 * r + 8])
                    ins.then_inc(gap_ready, 1)
                    dve.wait_ge(gap_ready, after(n * 2))
                    dve.tensor_copy(pick[:, q, :, :], topi[:, q, :, 0:2])
                    dve.tensor_tensor(gap[:, q, :], top[:, q, :, 0], top[:, q, :, 1], ALU.subtract).then_inc(gap_ready, 1)

                def add(n, q, j):
                    dve.wait_ge(prod_ready, after(n * 16 + j))
                    if j < 4:
                        dve.wait_ge(first_used, after(n * 2 + (j - 2)))
                    else:
                        dve.wait_ge(prod_used, after(n * ND + (j - 4)))
                    r, e = j % 2, j // 2
                    dve.scalar_tensor_tensor(acc[:, q, r, :], expert_bank[j % 4][:, :], comb[:, q, r, e:e + 1],
                                             acc[:, q, r, :], ALU.mult, ALU.add).then_inc(prod_used, 1)

                def low_inter(n, q):
                    dve.wait_ge(ih_ready, after(n))
                    dve.tensor_tensor(il[q][:, :], t_bank[:, :], f32(ih[q][:, :]), ALU.subtract).then_inc(il_ready, 1)

                def best_down(n, q):
                    own_c.start(n)
                    dve.wait_ge(dlg_ready, after(n))
                    dve.tensor_copy(dlogits[:, q, :], t_bank[:, 0:EXPERTS]).then_inc(dlg_copied, 1)
                    dve.wait_ge(dlg_copied, after(n))
                    dve.sem_inc(dve_pause, 1)
                    own_c.link(dve.max(dtop[:, q, :], dlogits[:, q, :]))
                    dve.wait_ge(dcomb_ready, after(n - 2))
                    dve.sem_inc(dve_pause, 1)
                    dve.max_index(dtopi[:, q, :], dtop[:, q, :], dlogits[:, q, :]).then_inc(dgap_ready, 1)
                    dve.wait_ge(dgap_ready, after(n * 2))
                    dve.tensor_copy(dpick[:, q, :], dtopi[:, q, 0:2])
                    dve.tensor_tensor(dgap[:, q, :], dtop[:, q, 0:1], dtop[:, q, 1:2], ALU.subtract).then_inc(dgap_ready, 1)

                def add_down(n, q, h):
                    if h == 0:
                        own_y.start(n)
                        dve.wait_ge(dcomb_ready, after(n))
                    dve.wait_ge(y_ready, after(n * 2 + h))
                    for e in range(4 * h, 4 * h + 4):
                        src = t.X[:, at(n), :] if e == 0 else yacc[:, q, :]
                        dst = t.X[:, at(n), :] if e == EXPERTS - 1 else yacc[:, q, :]
                        ins = dve.scalar_tensor_tensor(dst, y_bank[h][:, (e % 4) * P:(e % 4 + 1) * P],
                                                       dcomb[:, q, e:e + 1], src, ALU.mult, ALU.add)
                        if e % 4 == 3:
                            ins.then_inc(y_used, 1)
                            dve.wait_ge(y_used, after(n * 2 + h))
                        else:
                            own_y.link(ins)
                    if h == 1:
                        dve.sem_inc(dve_pause, 1)
                        own_y.link(dve.bn_stats(stat6[:, q, :], t.X[:, at(n), :]))
                        dve.sem_inc(dve_pause, 1)
                        own_y.link(dve.bn_aggr(aggr[:, q, :], stat6[:, q, :]))
                        dve.sem_inc(dve_pause, 1)
                        dve.tensor_copy(t.stats[:, at(n), :], aggr[:, q, :])

                def body(n, q):
                    nxt = not (isinstance(n, int) and n == TILES - 1)
                    nx2 = not (isinstance(n, int) and n >= TILES - 2)
                    bef = not (isinstance(n, int) and n == 0)
                    be2 = not (isinstance(n, int) and n <= 1)
                    for j in range(2, 5):
                        add(n, q, j)
                    if be2:
                        add_down(n - 2, q, 0)
                    add(n, q, 5)
                    if nxt:
                        low_x(n + 1, 1 - q)
                    for j in range(6, 8):
                        add(n, q, j)
                    if be2:
                        add_down(n - 2, q, 1)
                    for j in range(8, 10):
                        add(n, q, j)
                    if bef:
                        low_inter(n - 1, 1 - q)
                    for j in range(10, 12):
                        add(n, q, j)
                    if nxt:
                        best_gu(n + 1, 1 - q)
                    for j in range(12, 14):
                        add(n, q, j)
                    if bef:
                        best_down(n - 1, 1 - q)
                    for j in range(14, 16):
                        add(n, q, j)
                    if nx2:
                        normalise(n + 2, q)

                normalise(0, 0)
                normalise(1, 1)
                low_x(0, 0)
                best_gu(0, 0)
                steps(dve, body, None, None)
                for h in range(2):
                    add_down(TILES - 2, 0, h)
                low_inter(TILES - 1, 1)
                best_down(TILES - 1, 1)
                for h in range(2):
                    add_down(TILES - 1, 1, h)
        sem.clear()


def ffn_phase(nc, t, d, tag, out):
    with ExitStack() as ctx:
        def sb(name, shape, dt=F32):
            return ctx.enter_context(nc.sbuf_tensor(f"{tag}_{name}", shape, dt))

        sem = Semaphores(ctx, nc, tag)

        w1 = sb("w1", [P, INNER])
        w2 = sb("w2", [P, INNER])
        small = sb("small", [P, FFN_SMALL])
        b1, b2, scale = small[:, 0:4], small[:, 4:5], small[0:8, 5:6]
        first_half, second_half = small[0:8, 8:12], small[0:8, 12:16]
        b2h = sb("b2h", [P, 1])
        xn = sb("xn", [P, BT, DIM])
        xT = sb("xT", [P, SEQ])
        even = sb("even", [8, DIM])
        odd = sb("odd", [8, DIM])
        evens = sb("evens", [8, DIM])
        odds = sb("odds", [8, KC, DIM])
        evenm = sb("evenm", [8, 4, 4, 32])
        w1e = sb("w1e", [P, INNER])
        w2e = sb("w2e", [P, INNER])
        hid = sb("hid", [P, 2, KC, HALF])
        oT = sb("oT", [P, 2, HALF])
        xo = sb("xo", [P, 2, KC, DIM])
        stat6 = sb("stat6", [P, 2, KC, 6])
        aggr = sb("aggr", [P, 2, KC, 2])
        ps = [ctx.enter_context(nc.psum_tensor(f"{tag}_ps{i}", [P, HALF], F32)) for i in range(8)]
        x_bank, w_bank, h_bank, o_bank = ps[0:2], ps[2], ps[3:7], ps[7]

        w_in, s_in, rstd_ready, b2h_ready = sem("w_in"), sem("s_in"), sem("rstd_ready"), sem("b2h_ready")
        xn_ready, rows_in, pairs_ready = sem("xn_ready"), sem("rows_in"), sem("pairs_ready")
        xt_ready, xt_copied, wp_ready, we_ready = sem("xt_ready"), sem("xt_copied"), sem("wp_ready"), sem("we_ready")
        h_ready, hid_ready, o_ready, o_copied = sem("h_ready"), sem("hid_ready"), sem("o_ready"), sem("o_copied")
        ot_ready, xo_ready, stat_ready = sem("ot_ready"), sem("xo_ready"), sem("stat_ready")
        dve_pause = sem("dve_pause")

        with nc.Block() as block:
            @block.sync
            def _(sp):
                sp.dma_start(w1[:, :], d["w1"]).then_inc(w_in, 16)
                sp.dma_start(w2[:, :], d["w2"]).then_inc(w_in, 16)
                sp.dma_start(small[:, :], d["ffn_small"]).then_inc(s_in, 16)
                with sp.Fori(0, BATCH) as b:
                    sp.wait_ge(xn_ready, after(b * BT))
                    sp.wait_ge(we_ready, after((b - 1) * 2 + 1))
                    sp.dma_start(even[:, :], xn[1:16:2, 0, :]).then_inc(rows_in, 16)
                    sp.dma_start(odd[:, :], xn[2:17:2, 0, :]).then_inc(rows_in, 16)

            @block.tensor
            def _(pe):
                for s in (xt_ready, wp_ready, h_ready, o_ready, ot_ready):
                    pe.sem_inc(s, LEAD)
                with pe.Fori(0, BATCH) as b:
                    for s in range(2):
                        pe.wait_ge(xn_ready, after(b * BT + 4 * s + 3))
                        pe.wait_ge(xo_ready, after((b - 1) * 2 + s))
                        for j in range(4):
                            last = pe.transpose(x_bank[s][:, j * P:(j + 1) * P], xn[:, 4 * s + j, :], t.ident)
                        last.then_inc(xt_ready, 1)
                    pe.wait_ge(pairs_ready, after(b * 3 + 2))
                    for p in range(KC):
                        last = pe.matmul(w_bank[:, p * P:(p + 1) * P], odds[:, p, :], even[:, :], start=True, stop=True)
                    last.then_inc(wp_ready, 1)
                    pe.wait_ge(we_ready, after(b * 2))
                    for c in range(KC):
                        last = pe.matmul(w_bank[:, c * P:(c + 1) * P], odd[:, :], evenm[:, c, :, :], start=True, stop=True)
                    last.then_inc(wp_ready, 1)
                    for s in range(2):
                        pe.wait_ge(xt_copied, after(b * 2 + s))
                        for c in range(KC):
                            pe.wait_ge(hid_ready, after((b * 2 + s - 1) * KC + c))
                            pe.matmul(h_bank[c][:, :], w1e[:, c * P:(c + 1) * P], xT[:, s * HALF:(s + 1) * HALF],
                                      start=True, stop=True).then_inc(h_ready, 1)
                    pe.wait_ge(we_ready, after(b * 2 + 1))
                    for s in range(2):
                        pe.wait_ge(o_copied, after(b * 2 + s - 1))
                        for c in range(KC):
                            pe.wait_ge(hid_ready, after((b * 2 + s) * KC + c))
                            last = pe.matmul(o_bank[:, :], w2e[:, c * P:(c + 1) * P], hid[:, s, c, :], start=c == 0, stop=c == KC - 1)
                        last.then_inc(o_ready, 1)
                    for s in range(2):
                        pe.wait_ge(o_copied, after(b * 2 + s))
                        for j in range(4):
                            last = pe.transpose(x_bank[s][:, j * P:(j + 1) * P], oT[:, s, j * P:(j + 1) * P], t.ident)
                        last.then_inc(ot_ready, 1)

            @block.scalar
            def _(act):
                layernorm_scales(act, None, nc, t, rstd_ready)
                for s in (xt_copied, hid_ready, o_copied):
                    act.sem_inc(s, LEAD)
                act.wait_ge(b2h_ready, 1)
                with act.Fori(0, BATCH) as b:
                    for s in range(2):
                        act.wait_ge(xt_ready, after(b * 2 + s))
                        act.wait_ge(h_ready, after((b - 1) * 2 * KC + (s + 1) * KC - 1))
                        act.activation(xT[:, s * HALF:(s + 1) * HALF], x_bank[s][:, :], ACT.Copy).then_inc(xt_copied, 1)
                    for s in range(2):
                        for c in range(KC):
                            act.wait_ge(h_ready, after((b * 2 + s) * KC + c))
                            act.wait_ge(o_ready, after((b - 1) * 2 + s))
                            act.activation(hid[:, s, c, :], h_bank[c][:, :], ACT.Gelu, bias=b1[:, c:c + 1]).then_inc(hid_ready, 1)
                    for s in range(2):
                        act.wait_ge(o_ready, after(b * 2 + s))
                        act.wait_ge(ot_ready, after((b - 1) * 2 + s))
                        act.activation(oT[:, s, :], o_bank[:, :], ACT.Identity, bias=b2h[:, :], scale=0.5).then_inc(o_copied, 1)

            @block.vector
            def _(dve):
                layernorm_scales(None, dve, nc, t, rstd_ready)
                for s in (xn_ready, pairs_ready, we_ready, xo_ready, stat_ready):
                    dve.sem_inc(s, LEAD)
                dve.wait_ge(s_in, 16)
                dve.tensor_scalar(b2h[:, :], b2, 0.5, None, ALU.mult).then_inc(b2h_ready, 1)
                dve.wait_ge(w_in, 32)
                with dve.Fori(0, BATCH) as b:
                    for j in range(BT):
                        if j % 4 == 0:
                            dve.wait_ge(xt_ready, after((b - 1) * 2 + j // 4))
                            if j == 0:
                                dve.wait_ge(pairs_ready, after((b - 1) * 3 + 2))
                        n = b * BT + j
                        dve.tensor_scalar(xn[:, j, :], t.X[:, at(n), :], t.stats[:, at(n), 0], t.rstd[:, at(n)],
                                          ALU.subtract, ALU.mult).then_inc(xn_ready, 1)
                    dve.wait_ge(rows_in, (b + 1) * 32)
                    dve.scalar_tensor_tensor(odds[:, :, :], odd[:, :].unsqueeze(1).to_broadcast([8, KC, DIM]), scale,
                                             first_half.unsqueeze(2).to_broadcast([8, KC, DIM]), ALU.mult, ALU.mult).then_inc(pairs_ready, 1)
                    dve.tensor_scalar(evens[:, :], even[:, :], scale, None, ALU.mult).then_inc(pairs_ready, 1)
                    dve.wait_ge(pairs_ready, after(b * 3 + 1))
                    ev = evens[:, :].rearrange("k (i r) -> k r i", r=4).unsqueeze(2).to_broadcast([8, 4, 4, 32])
                    sh = second_half.unsqueeze(1).unsqueeze(3).to_broadcast([8, 4, 4, 32])
                    dve.tensor_tensor(evenm[:, :, :, :], ev, sh, ALU.mult).then_inc(pairs_ready, 1)
                    for k, (we, w) in enumerate(((w1e, w1), (w2e, w2))):
                        dve.wait_ge(wp_ready, after(b * 2 + k))
                        dve.tensor_tensor(we[:, :], w_bank[:, :], w[:, :], ALU.add).then_inc(we_ready, 1)
                    for s in range(2):
                        dve.wait_ge(ot_ready, after(b * 2 + s))
                        half = bass.ds(b * BT + 4 * s, 4)
                        dve.tensor_tensor(xo[:, s, :, :], x_bank[s][:, :].rearrange("p (j c) -> p j c", c=DIM), t.X[:, half, :],
                                          ALU.add).then_inc(xo_ready, 1)
                        dve.wait_ge(xo_ready, after(b * 2 + s))
                        dve.sem_inc(dve_pause, 1)
                        dve.tensor_copy(t.X[:, half, :], xo[:, s, :, :])
                        for j in range(4):
                            ins = dve.bn_stats(stat6[:, s, j, :], xo[:, s, j, :])
                        ins.then_inc(stat_ready, 1)
                        dve.wait_ge(stat_ready, after(b * 4 + 2 * s))
                        dve.sem_inc(dve_pause, 1)
                        for j in range(4):
                            ins = dve.bn_aggr(aggr[:, s, j, :], stat6[:, s, j, :])
                        ins.then_inc(stat_ready, 1)
                        dve.wait_ge(stat_ready, after(b * 4 + 2 * s + 1))
                        dve.sem_inc(dve_pause, 1)
                        dve.tensor_copy(t.stats[:, half, :], aggr[:, s, :, :])
        sem.clear()


FFN_SMALL = 16


def ffn_laid_out(np, a, r):
    r["w1"] = a["L1_ffn_W1"].T
    r["w2"] = a["L1_ffn_W2"].reshape(DIM, KC, P).transpose(2, 1, 0).reshape(P, INNER)
    small = np.zeros((P, FFN_SMALL), np.float32)
    small[:, 0:4] = a["L1_ffn_b1"].reshape(KC, P).T
    small[:, 4] = a["L1_ffn_b2"]
    small[:, 5] = a["L1_ffn_scale"]
    small[0:4, 8:12] = np.eye(4)
    small[4:8, 12:16] = np.eye(4)
    r["ffn_small"] = small


GW = 3 * P
ROW = 32
SLOPE, SHIFT, DIVISOR = -0.01, 100.0, 1000.0
BOUND = 99.0


def attn0_phase(nc, t, d, tag):
    with ExitStack() as ctx:
        def sb(name, shape, dt=F32):
            return ctx.enter_context(nc.sbuf_tensor(f"{tag}_{name}", shape, dt))

        sem = Semaphores(ctx, nc, tag)

        w32 = sb("w32", [P, GROUPS, GW])
        w = [sb(f"w{i}", [P, GROUPS, GW], F32R) for i in range(2)]
        wp = sb("wp", [P, GROUPS * DIM])
        small = sb("small", [P, A0_SMALL])
        k_low, q_low, q_ones, head_mask = small[:, 0:1], small[:, 1:2], small[:, 2:3], small[:, 4:8]
        first_rows = small[:, 3:4]
        state_mask, kv_ones, seen = small[:, 8:136], small[:, 136:392], small[:, 392:904]
        xn = sb("xn", [P, BT, DIM])
        xT = [sb(f"xT{i}", [P, SEQ], F32R) for i in range(2)]
        low = sb("low", [P, 2, HALF], F32R)
        kS = sb("kS", [P, SEQ], F32R)
        kM = [sb(f"kM{q}", [P, GH, SEQ], F32R) for q in range(2)]
        qS = [sb(f"qS{q}", [P, SEQ], F32R) for q in range(2)]
        KV = [sb(f"KV{q}", [P, BT, 2 * P]) for q in range(2)]
        run = sb("run", [P, BT, P])
        runm = sb("runm", [P, BT, P])
        runl = sb("runl", [P, BT, P], F32R)
        S = [sb(f"S{q}", [P, BT, P], F32R) for q in range(2)]
        R = sb("R", [P, 2, GH, HALF])
        L = sb("L", [P, GH, HALF])
        yS = sb("yS", [P, GROUPS, SEQ])
        bound = sb("bound", [P, 2, 3])
        peak = sb("peak", [1, 2])
        flag = sb("flag", [1, 2], mybir.dt.int32)
        res = ResidualAdd(ctx, nc, sem, t, tag, 4)
        ps = [ctx.enter_context(nc.psum_tensor(f"{tag}_ps{i}", [P, HALF], F32)) for i in range(8)]
        e_bank, a_bank, y_bank, x_bank = ps[0:4], ps[4:6], ps[6], ps[7]

        w_in, w_high, w_low, rstd_ready, zero_ready = sem("w_in"), sem("w_high"), sem("w_low"), sem("rstd_ready"), sem("zero_ready")
        xn_ready, xt_ready, xh_ready, xl_ready = sem("xn_ready"), sem("xt_ready"), sem("xh_ready"), sem("xl_ready")
        ap_ready, t_ready, av_ready, run_ready = sem("ap_ready"), sem("t_ready"), sem("av_ready"), sem("run_ready")
        km_ready, runm_ready, runl_ready, S_ready = sem("km_ready"), sem("runm_ready"), sem("runl_ready"), sem("S_ready")
        s_ready, r_ready, u_ready, l_ready, g_ready = (
            sem("s_ready"), sem("r_ready"), sem("u_ready"), sem("l_ready"), sem("g_ready"))
        pv_ready, y_ready, yc_ready, o_ready = sem("pv_ready"), sem("y_ready"), sem("yc_ready"), sem("o_ready")
        pe_pause, act_pause, dve_pause, pool_pause = sem("pe_pause"), sem("act_pause"), sem("vector_pause"), sem("pool_pause")
        bound_ready, peak_ready, top_ready, flag_ready = sem("bound_ready"), sem("peak_ready"), sem("top_ready"), sem("flag_ready")
        cs_ready, cl_ready, cm_ready, cc_ready, cv_ready, cy_ready = (
            sem("cs_ready"), sem("cl_ready"), sem("cm_ready"), sem("cc_ready"), sem("cv_ready"), sem("cy_ready"))

        units = [(s, u) for s in range(2) for u in key_units(s)]
        NU, NQ0 = len(units), len(key_units(0))
        US = NU * GH
        PRODUCTS = ((0, 0), (1, 0), (0, 1))
        PREP = [("k", 0), ("k", 1), ("kv", 0), ("kv", 1), ("kv", 2), ("kv", 3), ("q", 0), ("q", 1), ("run", 0), ("run", 1)]
        LOWS = {0: 0, 1: 1, 6: 2, 7: 3}

        def width(u):
            pieces = units[u][1]
            return pieces[0][3] if len(pieces) == 1 else HALF

        def correct(eng, pause, m, q, body, totals):
            eng.wait_ge(flag_ready, after(m))
            eng.sem_inc(pause, 1)
            may_be_low = eng.value_load(flag[0:1, q:q + 1], min_val=0, max_val=1)
            with eng.If(may_be_low):
                nc.disable_value_cache = True
                body()
                nc.disable_value_cache = False
            with eng.Else():
                for s, n in totals:
                    eng.sem_inc(s, n)

        def pipeline(eng, stage0, prepare, attend, stage3):
            with eng.Fori(0, BATCH) as b:
                stage0(b)
                for k in range(NU):
                    prepare(b * GROUPS, 0, k)
                for g in range(GROUPS):
                    nxt = (lambda k, g=g: prepare(b * GROUPS + (g + 1), g + 1, k)) if g + 1 < GROUPS else (lambda k: None)
                    attend(b * GROUPS + g, g, nxt)
                stage3(b)

        with nc.Block() as block:
            @block.sync
            def _(sp):
                sp.dma_start(w32[:, :, :], d["wqkv"].rearrange("p (g n) -> p g n", g=GROUPS)).then_inc(w_in, 16)
                sp.dma_start(wp[:, :], d["wproj"]).then_inc(w_in, 16)
                sp.dma_start(small[:, :], d["attn0_small"]).then_inc(w_in, 16)

            @block.gpsimd
            def _(pool):
                for s in (km_ready, runm_ready, runl_ready, S_ready, g_ready):
                    pool.sem_inc(s, LEAD)
                pool.memset(run[:, 0, :], 0.0).then_inc(zero_ready, 1)
                pool.wait_ge(w_in, 48)

                def prepare(m, g, k):
                    q = g % 2
                    if k == 1:
                        pool.wait_ge(av_ready, after(m * NU + 1))
                        pool.wait_ge(s_ready, after((m - 1) * US - 1))
                        pool.sem_inc(pool_pause, 1)
                        for j in range(GH):
                            ins = pool.tensor_scalar(kM[q][:, j, :], f32(kS[:, :]), head_mask[:, j:j + 1], None, ALU.mult)
                        ins.then_inc(km_ready, 1)
                    if k == NU - 1:
                        pool.wait_ge(av_ready, after(m * NU + NU - 1))
                        pool.wait_ge(y_ready, after((m - 1) * 2 - 1))
                        pool.tensor_tensor(runm[:, :, :], run[:, :, :], state_mask.unsqueeze(1).to_broadcast([P, BT, P]),
                                           ALU.mult).then_inc(runm_ready, 1)
                        pool.wait_ge(runm_ready, after(m))
                        pool.sem_inc(pool_pause, 1)
                        pool.tensor_scalar(runl[:, :, :], runm[:, :, :], k_low, None, ALU.mult).then_inc(runl_ready, 1)
                        pool.wait_ge(runl_ready, after(m))
                        pool.tensor_tensor(S[q][:, :, :], runm[:, :, :], f32(runl[:, :, :]), ALU.subtract).then_inc(S_ready, 1)

                def attend(m, g, nxt):
                    for u in range(NU):
                        if units[u][1][0][4]:
                            for j in range(GH):
                                n = m * 2 * GH + (GH if u else 0) + j
                                pool.wait_ge(l_ready, after(n))
                                pool.tensor_tensor(L[:, j, :], L[:, j, :], seen, ALU.mult).then_inc(g_ready, 1)
                        nxt(u)

                pipeline(pool, lambda b: None, prepare, attend, lambda b: None)

            @block.tensor
            def _(pe):
                for s in (xt_ready, ap_ready, s_ready, pv_ready, y_ready, o_ready, peak_ready, cs_ready, cv_ready):
                    pe.sem_inc(s, LEAD)
                pe.wait_ge(w_in, 48)
                pe.wait_ge(w_low, 1)

                def stage0(b):
                    for s in range(2):
                        pe.wait_ge(xn_ready, after(b * BT + 4 * s + 3))
                        pe.wait_ge(r_ready, after(b * GROUPS * US - 1))
                        for j in range(4):
                            last = pe.transpose(e_bank[s][:, j * P:(j + 1) * P], xn[:, 4 * s + j, :], t.ident)
                        last.then_inc(xt_ready, 1)
                    pe.wait_ge(xl_ready, after(b * 2 + 1))
                    pe.wait_ge(res.xo_ready, after(b * 2 - 1))

                def prepare(m, g, k):
                    q = g % 2
                    kind, i = PREP[k]
                    bank = a_bank[k % 2]
                    pe.wait_ge(av_ready, after(m * NU + k - 2))
                    if kind in "kq":
                        off = P if kind == "k" else 0
                        for n, (a, b_) in enumerate(PRODUCTS):
                            last = pe.matmul(bank[:, :], w[b_][:, g, off:off + P], xT[a][:, i * HALF:(i + 1) * HALF],
                                             start=n == 0, stop=n == 2)
                    elif kind == "kv":
                        for h in range(2):
                            j = 2 * i + h
                            for n, (a, b_) in enumerate(PRODUCTS):
                                last = pe.matmul(bank[:, h * 2 * P:(h + 1) * 2 * P], xT[a][:, j * P:(j + 1) * P], w[b_][:, g, P:GW],
                                                 start=n == 0, stop=n == 2)
                    else:
                        pe.wait_ge(av_ready, after(m * NU + 5))
                        if i == 0:
                            pe.wait_ge(bound_ready, after(m * 3 + 2))
                            pe.wait_ge(flag_ready, after(m - 1))
                            pe.matmul(x_bank[0:1, 0:GH], bound[:, q, 2:3], head_mask, start=True, stop=True).then_inc(peak_ready, 1)
                        for h in range(4 if i == 0 else 3):
                            j = 4 * i + h
                            last = pe.matmul(bank[:, h * P:(h + 1) * P], KV[q][:, j, 0:P], KV[q][:, j, P:2 * P], start=True, stop=True)
                    last.then_inc(ap_ready, 1)

                def scores(m, g, u):
                    q = g % 2
                    s, pieces = units[u]
                    for j in range(GH):
                        pe.wait_ge(r_ready, after(m * US + (u - 1) * GH + j))
                        diagonal = pieces[0][4]
                        for k, (kt, at_, qc, n, _) in enumerate(pieces):
                            last = pe.matmul(e_bank[j][:, at_:at_ + n], kM[q][:, j, kt * P:(kt + 1) * P],
                                             qS[q][:, s * HALF + qc:s * HALF + qc + n], start=not diagonal or k == 0,
                                             stop=not diagonal, skip_group_check=diagonal)
                        if diagonal:
                            last = pe.matmul(e_bank[j][:, :], t.identb, t.neg_kq, start=False, stop=True, skip_group_check=True)
                        last.then_inc(s_ready, 1)

                def values(m, g, u):
                    q = g % 2
                    s, pieces = units[u]
                    first, end = u in (0, NQ0), u in (NQ0 - 1, NU - 1)
                    if first:
                        pe.wait_ge(yc_ready, after(m * 2 + s - 1))
                    pe.wait_ge(u_ready, after(m * US + u * GH + GH - 1))
                    for k, (kt, at_, qc, n, diagonal) in enumerate(pieces):
                        for j in range(GH):
                            rows = slice(j * ROW, (j + 1) * ROW)
                            last = pe.matmul(y_bank[rows, qc:qc + n], KV[q][:, kt, P + j * ROW:P + (j + 1) * ROW],
                                             R[:, u % 2, j, at_:at_ + n], start=first and k == 0, stop=False, skip_group_check=True)
                    if first:
                        pe.wait_ge(g_ready, after((m * 2 + s) * GH + GH - 1))
                        for k, (kt, at_, qc, n, _) in enumerate(pieces):
                            for j in range(GH):
                                rows = slice(j * ROW, (j + 1) * ROW)
                                last = pe.matmul(y_bank[rows, qc:qc + n], KV[q][:, kt, P + j * ROW:P + (j + 1) * ROW],
                                                 L[:, j, at_:at_ + n], start=False, stop=False, skip_group_check=True)
                    last.then_inc(pv_ready, 1)
                    if end:
                        pe.wait_ge(S_ready, after(m))
                        chunks = [c for c in range(4 * s, 4 * s + 4) if c]
                        for c in chunks:
                            last = pe.matmul(y_bank[:, (c % 4) * P:(c % 4 + 1) * P], S[q][:, c, :], qS[q][:, c * P:(c + 1) * P],
                                             start=False, stop=c == chunks[-1], skip_group_check=True)
                        last.then_inc(y_ready, 1)

                def attend(m, g, nxt):
                    pe.wait_ge(km_ready, after(m))
                    pe.wait_ge(av_ready, after(m * NU + NU - 1))
                    for u in range(NU):
                        scores(m, g, u)
                        nxt(u)
                        if u >= 1:
                            values(m, g, u - 1)
                    values(m, g, NU - 1)
                    correct(pe, pe_pause, m, g % 2, lambda: low_scores(m, g), ((cs_ready, US), (cv_ready, NU)))

                def low_scores(m, g):
                    q = g % 2
                    for u in range(NU):
                        s, pieces = units[u]
                        for j in range(GH):
                            pe.wait_ge(cc_ready, after(m * US + (u - 1) * GH + j))
                            for kt, at_, qc, n, _ in pieces:
                                last = pe.matmul(e_bank[j][:, at_:at_ + n], kM[q][:, j, kt * P:(kt + 1) * P],
                                                 qS[q][:, s * HALF + qc:s * HALF + qc + n], start=True, stop=True)
                            last.then_inc(cs_ready, 1)
                        if u == 0:
                            pe.wait_ge(yc_ready, after(m * 2 + 1))
                        if u == NQ0:
                            pe.wait_ge(cy_ready, after(m * 2))
                        pe.wait_ge(cc_ready, after(m * US + u * GH + GH - 1))
                        for k, (kt, at_, qc, n, _) in enumerate(pieces):
                            for j in range(GH):
                                rows = slice(j * ROW, (j + 1) * ROW)
                                last = pe.matmul(y_bank[rows, qc:qc + n], KV[q][:, kt, P + j * ROW:P + (j + 1) * ROW],
                                                 R[:, 0, j, at_:at_ + n], start=u in (0, NQ0) and k == 0,
                                                 stop=u in (NQ0 - 1, NU - 1), skip_group_check=True)
                        last.then_inc(cv_ready, 1)
                    pe.wait_ge(cy_ready, after(m * 2 + 1))

                def stage3(b):
                    pe.wait_ge(yc_ready, after((b + 1) * GROUPS * 2 - 1))
                    pe.wait_ge(cy_ready, after((b + 1) * GROUPS * 2 - 1))
                    pe.wait_ge(av_ready, after((b + 1) * GROUPS * NU - 1))
                    for s in range(2):
                        for j in range(4):
                            for g in range(GROUPS):
                                c = s * HALF + j * P
                                last = pe.matmul(a_bank[s][:, j * P:(j + 1) * P], yS[:, g, c:c + P], wp[:, g * DIM:(g + 1) * DIM],
                                                 start=g == 0, stop=g == GROUPS - 1)
                        last.then_inc(o_ready, 1)

                pipeline(pe, stage0, prepare, attend, stage3)

            @block.scalar
            def _(act):
                layernorm_scales(act, None, nc, t, rstd_ready)
                for s in (xh_ready, t_ready, r_ready, l_ready, cl_ready):
                    act.sem_inc(s, LEAD)
                act.wait_ge(w_in, 48)
                act.activation(w[0][:, :, 0:P], w32[:, :, 0:P], ACT.Copy, scale=SCORE_SCALE)
                act.activation(w[0][:, :, P:GW], w32[:, :, P:GW], ACT.Copy).then_inc(w_high, 1)

                def stage0(b):
                    for s in range(2):
                        act.wait_ge(xt_ready, after(b * 2 + s))
                        act.wait_ge(ap_ready, after(b * GROUPS * NU - 1))
                        act.activation(xT[0][:, s * HALF:(s + 1) * HALF], e_bank[s][:, :], ACT.Copy).then_inc(xh_ready, 1)

                def prepare(m, g, k):
                    if k in LOWS:
                        act.wait_ge(ap_ready, after(m * NU + k))
                        act.wait_ge(av_ready, after(m * NU + k - 2))
                        act.activation(low[:, k % 2, :], a_bank[k % 2][:, :], ACT.Copy,
                                       scale=k_low if PREP[k][0] == "k" else q_low).then_inc(t_ready, 1)

                def attend(m, g, nxt):
                    for u in range(NU):
                        pieces, n = units[u][1], width(u)
                        for j in range(GH):
                            act.wait_ge(s_ready, after(m * US + u * GH + j))
                            if j == 0:
                                act.wait_ge(pv_ready, after(m * NU + u - 2))
                            if pieces[0][4]:
                                act.activation(L[:, j, :], e_bank[j][:, :], ACT.Copy, bias=1.0, scale=SLOPE).then_inc(l_ready, 1)
                            act.activation(R[:, u % 2, j, HALF - n:HALF], e_bank[j][:, HALF - n:HALF], ACT.Relu).then_inc(r_ready, 1)
                        nxt(u)
                    correct(act, act_pause, m, g % 2, lambda: low_terms(m), ((cl_ready, US),))

                def low_terms(m):
                    for u in range(NU):
                        n = width(u)
                        for j in range(GH):
                            act.wait_ge(cs_ready, after(m * US + u * GH + j))
                            act.wait_ge(cc_ready, after(m * US + (u - 1) * GH + j))
                            act.activation(L[:, j, HALF - n:HALF], e_bank[j][:, HALF - n:HALF], ACT.Copy, bias=-1.0,
                                           scale=-SLOPE).then_inc(cl_ready, 1)

                pipeline(act, stage0, prepare, attend, lambda b: None)

            @block.vector
            def _(dve):
                layernorm_scales(None, dve, nc, t, rstd_ready)
                for s in (xn_ready, xl_ready, av_ready, run_ready, u_ready, yc_ready, bound_ready, top_ready,
                          flag_ready, cm_ready, cc_ready, cy_ready):
                    dve.sem_inc(s, LEAD)
                res.prime(dve)
                dve.wait_ge(w_high, 1)
                dve.wait_ge(zero_ready, 1)
                dve.scalar_tensor_tensor(w[1][:, :, 0:P], w32[:, :, 0:P], SCORE_SCALE, f32(w[0][:, :, 0:P]), ALU.mult, ALU.subtract)
                dve.tensor_tensor(w[1][:, :, P:GW], w32[:, :, P:GW], f32(w[0][:, :, P:GW]), ALU.subtract).then_inc(w_low, 1)

                def stage0(b):
                    for j in range(BT):
                        if j % 4 == 0:
                            dve.wait_ge(xt_ready, after((b - 1) * 2 + j // 4))
                        n = b * BT + j
                        dve.tensor_scalar(xn[:, j, :], t.X[:, at(n), :], t.stats[:, at(n), 0], t.rstd[:, at(n)],
                                          ALU.subtract, ALU.mult).then_inc(xn_ready, 1)
                    for s in range(2):
                        half = slice(s * HALF, (s + 1) * HALF)
                        dve.wait_ge(xh_ready, after(b * 2 + s))
                        dve.tensor_tensor(xT[1][:, half], e_bank[s][:, :], f32(xT[0][:, half]), ALU.subtract).then_inc(xl_ready, 1)

                def prepare(m, g, k):
                    q = g % 2
                    kind, i = PREP[k]
                    bank = a_bank[k % 2]
                    half = slice(i * HALF, (i + 1) * HALF)
                    if k in LOWS:
                        dve.wait_ge(t_ready, after(m * 4 + LOWS[k]))
                    else:
                        dve.wait_ge(ap_ready, after(m * NU + k))
                    if kind == "k":
                        dve.wait_ge(km_ready, after(m - 1))
                        ins = dve.tensor_tensor(kS[:, half], bank[:, :], f32(low[:, k % 2, :]), ALU.subtract)
                    elif kind == "q":
                        dve.wait_ge(y_ready, after((m - 1) * 2 - 1))
                        ins = dve.scalar_tensor_tensor(qS[q][:, half], bank[:, :], q_ones, f32(low[:, k % 2, :]), ALU.add, ALU.subtract)
                    elif kind == "kv":
                        dve.wait_ge(y_ready, after((m - 1) * 2 - 1))
                        ins = dve.tensor_tensor(KV[q][:, 2 * i:2 * i + 2, :], bank[:, :].rearrange("p (j n) -> p j n", n=2 * P),
                                                kv_ones.unsqueeze(1).to_broadcast([P, 2, 2 * P]), ALU.add)
                    else:
                        dve.wait_ge(runm_ready, after(m - 1))
                        for h in range(4 if i == 0 else 3):
                            c = 4 * i + h
                            if c == 4:
                                dve.wait_ge(av_ready, after(m * NU + k - 1))
                            elif c:
                                dve.wait_ge(run_ready, after(m * 5 + c - 1 - (c > 4)))
                            ins = dve.tensor_tensor(run[:, c + 1, :], bank[:, h * P:(h + 1) * P], run[:, c, :], ALU.add)
                            if h != (3 if i == 0 else 2):
                                ins.then_inc(run_ready, 1)
                    ins.then_inc(av_ready, 1)
                    if k in (1, 7):
                        dve.wait_ge(av_ready, after(m * NU + k))
                        c = (k == 7) * 1
                        dve.reduce_max(bound[:, q, c:c + 1], f32((qS[q] if c else kS)[:, :]), AX.X,
                                       apply_absolute_value=True).then_inc(bound_ready, 1)
                    if k == 7:
                        dve.wait_ge(bound_ready, after(m * 3 + 1))
                        dve.scalar_tensor_tensor(bound[:, q, 2:3], bound[:, q, 0:1], bound[:, q, 1:2], first_rows,
                                                 ALU.mult, ALU.mult).then_inc(bound_ready, 1)
                    if k == NU - 1:
                        dve.wait_ge(peak_ready, after(m))
                        dve.reduce_max(peak[:, q:q + 1], x_bank[0:1, 0:GH], AX.X).then_inc(top_ready, 1)
                        dve.wait_ge(top_ready, after(m))
                        dve.tensor_scalar(flag[:, q:q + 1], peak[:, q:q + 1], BOUND, None, ALU.is_ge).then_inc(flag_ready, 1)

                def copy_out(m, g, s):
                    dve.wait_ge(y_ready, after(m * 2 + s))
                    dve.tensor_scalar(yS[:, g, s * HALF:(s + 1) * HALF], y_bank[:, :], 1.0 / DIVISOR, None, ALU.mult).then_inc(yc_ready, 1)

                def attend(m, g, nxt):
                    for u in range(NU):
                        pieces, n = units[u][1], width(u)
                        for j in range(GH):
                            dve.wait_ge(r_ready, after(m * US + u * GH + j))
                            r = R[:, u % 2, j, HALF - n:HALF]
                            dve.scalar_tensor_tensor(r, r, -SLOPE, r, ALU.add, ALU.mult).then_inc(u_ready, 1)
                        nxt(u)
                        if u == NQ0:
                            copy_out(m, g, 0)
                    copy_out(m, g, 1)
                    correct(dve, dve_pause, m, g % 2, lambda: low_weights(m, g), ((cc_ready, US), (cm_ready, 2 * GH), (cy_ready, 2)))

                def low_weights(m, g):
                    for u in range(NU):
                        n = width(u)
                        for j in range(GH):
                            dve.wait_ge(cl_ready, after(m * US + u * GH + j))
                            if j == 0:
                                dve.wait_ge(cv_ready, after(m * NU + u - 1))
                            c = R[:, 0, j, HALF - n:HALF]
                            ins = dve.scalar_tensor_tensor(c, e_bank[j][:, HALF - n:HALF], -SHIFT, L[:, j, HALF - n:HALF],
                                                           ALU.is_lt, ALU.mult)
                            if units[u][1][0][4]:
                                ins.then_inc(cm_ready, 1)
                                dve.wait_ge(cm_ready, after(m * 2 * GH + (GH if u else 0) + j))
                                ins = dve.tensor_tensor(c, c, seen, ALU.mult)
                            ins.then_inc(cc_ready, 1)
                        if u in (NQ0 - 1, NU - 1):
                            s = units[u][0]
                            dve.wait_ge(cv_ready, after(m * NU + u))
                            y = yS[:, g, s * HALF:(s + 1) * HALF]
                            dve.scalar_tensor_tensor(y, y_bank[:, :], 1.0 / DIVISOR, y, ALU.mult, ALU.add).then_inc(cy_ready, 1)

                def stage3(b):
                    for s in range(2):
                        dve.wait_ge(o_ready, after(b * 2 + s))
                        res.add(dve, b * 2 + s, s, b * BT + 4 * s, a_bank[s][:, :])

                pipeline(dve, stage0, prepare, attend, stage3)
        sem.clear()


A0_SMALL = 904


def attn0_laid_out(np, a, r):
    wqkv = a["L0_attn_W_attn"].reshape(DIM, 3, GROUPS, GH, HD)
    w = np.zeros((DIM, GROUPS, 3, GH, ROW), np.float32)
    for part in range(3):
        w[:, :, 0:2, :, part * HD:(part + 1) * HD] = wqkv[:, 0:2].transpose(0, 2, 1, 3, 4)
    w[:, :, 2, :, 0:HD] = wqkv[:, 2]
    r["wqkv"] = w.reshape(P, GROUPS * GW)
    wp = np.zeros((GROUPS, GH, ROW, DIM), np.float32)
    wp[:, :, 0:HD] = a["L0_attn_W_proj"].reshape(GROUPS, GH, HD, DIM)
    r["wproj"] = wp.transpose(1, 2, 0, 3).reshape(P, GROUPS * DIM)
    row, col = np.arange(P) % ROW, np.arange(P)
    small = np.zeros((P, A0_SMALL), np.float32)
    small[:, 0] = ((row >= HD) & (row < 2 * HD)) | (row == 25)
    small[:, 1] = (row >= 2 * HD) & (row < 3 * HD)
    small[:, 2] = (row == 24) | (row == 25)
    small[:, 3] = row < HD
    small[:, 4:8] = np.arange(P)[:, None] // ROW == np.arange(GH)
    same = (np.arange(P)[:, None] // ROW) == (col[None, :] // ROW)
    small[:, 8:136] = same * np.where(row < 24, SLOPE, 1.0)[:, None]
    small[:, 136:264] = ((row == 24) | (row == 25))[None, :]
    small[:, 392:904] = np.tile(np.triu(np.ones((P, P))), (1, 4))
    r["attn0_small"] = small


PAIRS = HEADS // 2
STACK = 3 * LAT
KROWS = STACK + 2
ZW = 5 * P
VW = 64
L1_COLS = 2 * LAT + 8 + 4 * HEADS


def key_units(s):
    k = 4 * s
    diagonal = [(k + i, i * P, i * P, P, True) for i in range(4)]
    split = [(k, P, P, 3 * P, False), (k + 2, 0, 3 * P, P, False)]
    half = [(k + 1, 2 * P, 2 * P, 2 * P, False)]
    return [diagonal, split, half] + [[(i, 0, 0, HALF, False)] for i in range(k)]


def attn1_phase(nc, t, d, tag):
    with ExitStack() as ctx:
        def sb(name, shape, dt=F32):
            return ctx.enter_context(nc.sbuf_tensor(f"{tag}_{name}", shape, dt))

        sem = Semaphores(ctx, nc, tag)

        wd32 = sb("wd32", [P, HEADS * STACK])
        wd = [sb(f"wd{i}", [P, HEADS * STACK], F32R) for i in range(2)]
        lat32 = sb("lat32", [P, STACK])
        lat = [sb(f"lat{i}", [P, STACK], F32R) for i in range(2)]
        wo = sb("wo", [P, ZW])
        cols = sb("cols", [P, L1_COLS])
        v_bias, k_bias, k_low, q_low = cols[:, 0:LAT], cols[0:STACK, 36:37], cols[0:STACK, 37:38], cols[0:STACK, 38:39]
        q_bias = cols[0:STACK, 40:40 + HEADS]
        k_lbias = sb("k_lbias", [STACK, 1])
        qb_low = sb("qb_low", [STACK, HEADS])
        xn = sb("xn", [P, BT, DIM])
        xT = [sb(f"xT{i}", [P, SEQ], F32R) for i in range(2)]
        kT = sb("kT", [STACK, 2, HALF], F32R)
        kS = sb("kS", [KROWS, SEQ], F32R)
        V = sb("V", [P, BT, VW])
        wcur = sb("wcur", [P, 2, 2 * STACK], F32R)
        bcur = sb("bcur", [STACK, 2, 2])
        qT = sb("qT", [STACK, 2, HALF], F32R)
        qS = [[sb(f"qS{q}{c}", [KROWS, SEQ], F32R) for c in range(2)] for q in range(2)]
        mx = sb("mx", [P, 2, 16])
        mh = sb("mh", [16, 2, P], F32R)
        ml = sb("ml", [16, 2, P], F32R)
        probs = sb("probs", [P, 2, 2, HALF])
        yT = sb("yT", [P, PAIRS, SEQ])
        rcp = sb("rcp", [P, 2, HEADS])
        z = sb("z", [P, 2, ZW])
        zT = sb("zT", [P, 2, ZW])
        res = ResidualAdd(ctx, nc, sem, t, tag, 1)
        m_all = ctx.enter_context(nc.psum_tensor(f"{tag}_psm", [P, 4 * HALF], F32))
        m_bank = [m_all[:, i * HALF:(i + 1) * HALF] for i in range(4)]
        e_bank = [ctx.enter_context(nc.psum_tensor(f"{tag}_pse{i}", [P, HALF], F32)) for i in range(2)]
        y_bank = ctx.enter_context(nc.psum_tensor(f"{tag}_psy", [P, HALF], F32))
        o_bank = ctx.enter_context(nc.psum_tensor(f"{tag}_pso", [P, HALF], F32))

        w_in, k_in, w_high, w_low, rstd_ready = sem("w_in"), sem("k_in"), sem("w_high"), sem("w_low"), sem("rstd_ready")
        minus = sb("minus", [2, SEQ], F32R)
        const_ready, minus_ready = sem("const_ready"), sem("minus_ready")
        xn_ready, xt_ready, xh_ready, xl_ready = sem("xn_ready"), sem("xt_ready"), sem("xh_ready"), sem("xl_ready")
        kp_ready, kt_ready, ks_ready, vp_ready, v_ready = (
            sem("kp_ready"), sem("kt_ready"), sem("ks_ready"), sem("vp_ready"), sem("v_ready"))
        wq_ready, qp_ready, qt_ready, qs_ready = sem("wq_ready"), sem("qp_ready"), sem("qt_ready"), sem("qs_ready")
        sm_ready, mx_ready, mt_ready, mh_ready, ml_ready, m_in = (
            sem("sm_ready"), sem("mx_ready"), sem("mt_ready"), sem("mh_ready"), sem("ml_ready"), sem("m_in"))
        s_ready, p_ready, pv_ready, y_ready, yc_ready = (
            sem("s_ready"), sem("p_ready"), sem("pv_ready"), sem("y_ready"), sem("yc_ready"))
        zt_ready, r_ready, z_ready, zz_ready, zc_ready, o_ready = (
            sem("zt_ready"), sem("r_ready"), sem("z_ready"), sem("zz_ready"), sem("zc_ready"), sem("o_ready"))
        pool_pause = sem("pool_pause")

        units = [(s, u) for s in range(2) for u in key_units(s)]
        NU = len(units)
        NQ0 = len(key_units(0))
        PRODUCTS = ((0, 0), (1, 0), (0, 1))

        def pipeline(eng, stage0, both, stage3):
            with eng.Fori(0, BATCH) as b:
                stage0(b)
                with eng.Fori(0, PAIRS // 2 - 1) as i:
                    for q in range(2):
                        both(b * PAIRS + i * 2 + q, q, i * 2 + q, True)
                both(b * PAIRS + PAIRS - 2, 0, PAIRS - 2, True)
                both(b * PAIRS + PAIRS - 1, 1, PAIRS - 1, False)
                stage3(b)

        with nc.Block() as block:
            @block.sync
            def _(sp):
                sp.dma_start(wd32[:, :], d["wd"]).then_inc(w_in, 16)
                sp.dma_start(lat32[:, :], d["latent"]).then_inc(w_in, 16)
                sp.dma_start(wo[:, :], d["wo"]).then_inc(w_in, 16)
                sp.dma_start(cols[:, :], d["attn1_small"]).then_inc(w_in, 16)
                sp.wait_ge(minus_ready, 1)
                sp.dma_start(f32(kS[STACK:KROWS, :]), f32(minus[:, :])).then_inc(k_in, 16)

                def maxima(m, q):
                    sp.wait_ge(ml_ready, after(m))
                    for c in range(2):
                        sp.dma_start(f32(qS[q][c][STACK:STACK + 1, :]), f32(mh[8 * c:8 * c + 8, q, :])).then_inc(m_in, 16)
                        sp.dma_start(f32(qS[q][c][STACK + 1:STACK + 2, :]), f32(ml[8 * c:8 * c + 8, q, :])).then_inc(m_in, 16)

                def both(m, q, i, more):
                    if more:
                        maxima(m + 1, 1 - q)

                pipeline(sp, lambda b: maxima(b * PAIRS, 0), both, lambda b: None)

            @block.gpsimd
            def _(pool):
                for s in (wq_ready,):
                    pool.sem_inc(s, LEAD)
                pool.memset(V[:, :, LAT:VW], 0.0)
                pool.memset(z[:, :, HEADS * LAT:ZW], 0.0).then_inc(const_ready, 1)
                pool.wait_ge(const_ready, 1)
                pool.memset(V[:, :, LAT:LAT + 1], 1.0)
                pool.memset(z[:, :, HEADS * LAT:HEADS * LAT + 1], 1.0).then_inc(const_ready, 1)
                pool.wait_ge(w_low, 2)

                def weights(m, i):
                    pool.wait_ge(qs_ready, after(m * 4 - 1))
                    pool.sem_inc(pool_pause, 1)
                    for k in range(2):
                        pool.tensor_copy(wcur[:, k, :], wd[k][:, bass.ds(i * 2 * STACK, 2 * STACK)])
                    pool.tensor_copy(bcur[:, 0, :], q_bias[:, bass.ds(i * 2, 2)])
                    pool.tensor_copy(bcur[:, 1, :], qb_low[:, bass.ds(i * 2, 2)]).then_inc(wq_ready, 1)

                def both(m, q, i, more):
                    if more:
                        weights(m + 1, i + 1)

                pipeline(pool, lambda b: weights(b * PAIRS, 0), both, lambda b: None)

            @block.tensor
            def _(pe):
                for s in (xt_ready, kp_ready, vp_ready, qp_ready, sm_ready, mt_ready, s_ready, pv_ready, y_ready,
                          zt_ready, zz_ready, o_ready):
                    pe.sem_inc(s, LEAD)
                pe.wait_ge(w_in, 64)
                pe.wait_ge(w_low, 2)
                pe.wait_ge(k_in, 16)
                pe.wait_ge(const_ready, 2)

                def stage0(b):
                    for s in range(2):
                        pe.wait_ge(xn_ready, after(b * BT + 4 * s + 3))
                        pe.wait_ge(z_ready, after((b - 1) * BT + BT - 1))
                        for j in range(4):
                            last = pe.transpose(m_bank[s][:, j * P:(j + 1) * P], xn[:, 4 * s + j, :], t.ident)
                        last.then_inc(xt_ready, 1)
                    for s in range(2):
                        pe.wait_ge(xl_ready, after(b * 2 + s))
                        for k, (a, w) in enumerate(PRODUCTS):
                            last = pe.matmul(m_bank[2 + s][0:STACK, :], lat[w][:, :], xT[a][:, s * HALF:(s + 1) * HALF],
                                             start=k == 0, stop=k == 2)
                        last.then_inc(kp_ready, 1)
                    pe.wait_ge(res.xo_ready, after(b * BT - 1))
                    for j in range(BT):
                        for k, (a, w) in enumerate(PRODUCTS):
                            last = pe.matmul(o_bank[:, j * VW:j * VW + LAT], xT[a][:, j * P:(j + 1) * P], lat[w][:, 0:LAT],
                                             start=k == 0, stop=k == 2)
                    last.then_inc(vp_ready, 1)
                    pe.wait_ge(ks_ready, after(b * 2 + 1))
                    for c in range(2):
                        project(b * PAIRS, c)
                    for v in range(16):
                        scores_max(b * PAIRS, 0, v)
                    pe.wait_ge(v_ready, after(b))
                    transpose_max(b * PAIRS, 0)

                def project(m, c):
                    pe.wait_ge(wq_ready, after(m))
                    pe.wait_ge(mx_ready, after((m - 1) * 16 + 15))
                    for s in range(2):
                        for k, (a, w) in enumerate(PRODUCTS):
                            last = pe.matmul(m_bank[2 * c + s][0:STACK, :], wcur[:, w, c * STACK:(c + 1) * STACK],
                                             xT[a][:, s * HALF:(s + 1) * HALF], start=k == 0, stop=k == 2)
                        last.then_inc(qp_ready, 1)

                def scores_max(m, q, v):
                    c, j = v // 8, v % 8
                    if v == 0:
                        pe.wait_ge(qs_ready, after(m * 4 + 3))
                    if v >= 2:
                        pe.wait_ge(mx_ready, after(m * 16 + v - 2))
                    base = (v % 2) * 2 * HALF
                    for lo in range(0, (j + 1) * P, HALF):
                        hi = min(lo + HALF, (j + 1) * P)
                        pe.matmul(m_all[:, base + lo:base + hi], qS[q][c][0:STACK, j * P:(j + 1) * P], kS[0:STACK, lo:hi],
                                  start=True, stop=hi < (j + 1) * P)
                    pe.matmul(m_all[:, base + j * P:base + (j + 1) * P], t.identb, t.neg_qk, start=False, stop=True).then_inc(sm_ready, 1)

                def transpose_max(m, q):
                    pe.wait_ge(mx_ready, after(m * 16 + 15))
                    pe.wait_ge(ml_ready, after(m - 1))
                    pe.transpose(o_bank[0:16, 0:P], mx[:, q, :], t.ident).then_inc(mt_ready, 1)

                def scores(m, q, u):
                    s, pieces = units[u]
                    for c in range(2):
                        pe.wait_ge(p_ready, after(m * 2 * NU + 2 * (u - 1) + c))
                        diagonal = pieces[0][4]
                        for k, (kt, at_, qc, n, _) in enumerate(pieces):
                            last = pe.matmul(e_bank[c][:, at_:at_ + n], kS[:, kt * P:(kt + 1) * P],
                                             qS[q][c][:, s * HALF + qc:s * HALF + qc + n], start=True if not diagonal else k == 0,
                                             stop=not diagonal, skip_group_check=diagonal)
                        if diagonal:
                            last = pe.matmul(e_bank[c][:, :], t.identb, t.neg_kq, start=False, stop=True, skip_group_check=True)
                        last.then_inc(s_ready, 1)

                def values(m, q, u):
                    s, pieces = units[u]
                    first = u in (0, NQ0)
                    if first:
                        pe.wait_ge(yc_ready, after(m * 2 + s - 1))
                    pe.wait_ge(p_ready, after(m * 2 * NU + 2 * u + 1))
                    end = u in (NQ0 - 1, NU - 1)
                    for k, (kt, at_, qc, n, _) in enumerate(pieces):
                        for c in range(2):
                            last = pe.matmul(y_bank[VW * c:VW * (c + 1), qc:qc + n], V[:, kt, :], probs[:, u % 2, c, at_:at_ + n],
                                             start=first and k == 0, stop=end, skip_group_check=True)
                    last.then_inc(y_ready if end else pv_ready, 1)

                def both(m, q, i, more):
                    pe.wait_ge(m_in, (m + 1) * 64)
                    for u in range(NU):
                        scores(m, q, u)
                        if more:
                            if u < 2:
                                project(m + 1, u)
                            for v in ({2: range(0, 3), 3: range(3, 6), 4: range(6, 9), 5: range(9, 12), 6: range(12, 14), 7: range(14, 16)}.get(u, ())):
                                scores_max(m + 1, 1 - q, v)
                            if u == NU - 2:
                                transpose_max(m + 1, 1 - q)
                        if u >= 1:
                            values(m, q, u - 1)
                    values(m, q, NU - 1)

                def stage3(b):
                    def heads_out(j):
                        pe.wait_ge(yc_ready, after((b + 1) * PAIRS * 2 - 1))
                        pe.wait_ge(z_ready, after(b * BT + j - 2))
                        pe.wait_ge(mx_ready, after((b + 1) * PAIRS * 16 - 1))
                        for i in range(PAIRS):
                            last = pe.transpose(m_all[:, (j % 2) * 2 * HALF + i * P:(j % 2) * 2 * HALF + (i + 1) * P],
                                                yT[:, i, j * P:(j + 1) * P], t.ident)
                        last.then_inc(zt_ready, 1)

                    heads_out(0)
                    for j in range(BT):
                        if j + 1 < BT:
                            heads_out(j + 1)
                        pe.wait_ge(z_ready, after(b * BT + j))
                        pe.wait_ge(zc_ready, after((b * BT + j - 1) * 2 + 1))
                        pe.wait_ge(p_ready, after((b + 1) * PAIRS * 2 * NU - 1))
                        for k in range(5):
                            last = pe.transpose(e_bank[k // 4][:, (k % 4) * P:(k % 4 + 1) * P], z[:, j % 2, k * P:(k + 1) * P], t.ident)
                        last.then_inc(zz_ready, 1)
                        pe.wait_ge(zc_ready, after((b * BT + j) * 2 + 1))
                        pe.wait_ge(res.xo_ready, after(b * BT + j - 1))
                        pe.wait_ge(ml_ready, after((b + 1) * PAIRS - 1))
                        for k in range(5):
                            last = pe.matmul(o_bank[:, 0:P], zT[:, j % 2, k * P:(k + 1) * P], wo[:, k * P:(k + 1) * P], start=k == 0, stop=k == 4)
                        last.then_inc(o_ready, 1)

                pipeline(pe, stage0, both, stage3)

            @block.scalar
            def _(act):
                layernorm_scales(act, None, nc, t, rstd_ready)
                for s in (xh_ready, kt_ready, qt_ready, mh_ready, p_ready, zc_ready):
                    act.sem_inc(s, LEAD)
                act.wait_ge(w_in, 64)
                act.activation(wd[0][:, :], wd32[:, :], ACT.Copy)
                act.activation(lat[0][:, :], lat32[:, :], ACT.Copy).then_inc(w_high, 1)
                act.wait_ge(w_low, 2)

                def stage0(b):
                    for s in range(2):
                        act.wait_ge(xt_ready, after(b * 2 + s))
                        act.wait_ge(qp_ready, after(b * PAIRS * 4 - 1))
                        act.activation(xT[0][:, s * HALF:(s + 1) * HALF], m_bank[s], ACT.Copy).then_inc(xh_ready, 1)
                    for s in range(2):
                        act.wait_ge(kp_ready, after(b * 2 + s))
                        act.wait_ge(ks_ready, after((b - 1) * 2 + s))
                        act.activation(kT[:, s, :], m_bank[2 + s][0:STACK, :], ACT.Identity, bias=k_lbias[:, :],
                                       scale=k_low).then_inc(kt_ready, 1)
                    for g in range(4):
                        low_query(b * PAIRS, g)
                    high_max(b * PAIRS, 0)

                def low_query(m, g):
                    act.wait_ge(qp_ready, after(m * 4 + g))
                    act.wait_ge(qs_ready, after(m * 4 + g - 2))
                    act.activation(qT[:, g % 2, :], m_bank[g][0:STACK, :], ACT.Identity, bias=bcur[:, 1, g // 2:g // 2 + 1],
                                   scale=q_low).then_inc(qt_ready, 1)

                def high_max(m, q):
                    act.wait_ge(mt_ready, after(m))
                    act.activation(mh[:, q, :], o_bank[0:16, 0:P], ACT.Copy).then_inc(mh_ready, 1)

                def both(m, q, i, more):
                    for u in range(NU):
                        for c in range(2):
                            act.wait_ge(s_ready, after(m * 2 * NU + 2 * u + c))
                            if c == 0:
                                if u in (0, 1):
                                    act.wait_ge(pv_ready if u == 0 else y_ready, after((m - 1) * (NU - 2) + NU - 3) if u == 0 else after(m * 2 - 1))
                                elif u - 2 == NQ0 - 1:
                                    act.wait_ge(y_ready, after(m * 2))
                                else:
                                    act.wait_ge(pv_ready, after(m * (NU - 2) + (u - 2) - (1 if u - 2 >= NQ0 else 0)))
                            n = 256 if len(units[u][1]) == 1 and units[u][1][0][3] == 256 else HALF
                            act.activation(probs[:, u % 2, c, HALF - n:HALF], e_bank[c][:, HALF - n:HALF], ACT.Exp,
                                           scale=SCORE_SCALE).then_inc(p_ready, 1)
                        if more:
                            if u < 2:
                                low_query(m + 1, 2 * u)
                                low_query(m + 1, 2 * u + 1)
                            if u == NU - 2:
                                high_max(m + 1, 1 - q)

                def stage3(b):
                    for j in range(BT):
                        act.wait_ge(zz_ready, after(b * BT + j))
                        act.wait_ge(o_ready, after(b * BT + j - 2))
                        act.activation(zT[:, j % 2, 0:HALF], e_bank[0][:, :], ACT.Copy).then_inc(zc_ready, 1)
                        act.activation(zT[:, j % 2, HALF:ZW], e_bank[1][:, 0:P], ACT.Copy).then_inc(zc_ready, 1)

                pipeline(act, stage0, both, stage3)

            @block.vector
            def _(dve):
                layernorm_scales(None, dve, nc, t, rstd_ready)
                for s in (xn_ready, xl_ready, ks_ready, v_ready, qs_ready, mx_ready, ml_ready, yc_ready, r_ready, z_ready):
                    dve.sem_inc(s, LEAD)
                res.prime(dve)
                dve.memset(f32(minus[:, :]), -1.0).then_inc(minus_ready, 1)
                dve.wait_ge(w_in, 64)
                dve.tensor_scalar(k_lbias[:, :], k_bias, k_low, None, ALU.mult)
                dve.tensor_scalar(qb_low[:, :], q_bias, q_low, None, ALU.mult).then_inc(w_low, 1)
                dve.wait_ge(w_high, 1)
                dve.tensor_tensor(wd[1][:, :], wd32[:, :], f32(wd[0][:, :]), ALU.subtract)
                dve.tensor_tensor(lat[1][:, :], lat32[:, :], f32(lat[0][:, :]), ALU.subtract).then_inc(w_low, 1)
                dve.wait_ge(k_in, 16)
                dve.wait_ge(const_ready, 2)

                def stage0(b):
                    for j in range(BT):
                        if j % 4 == 0:
                            dve.wait_ge(xt_ready, after((b - 1) * 2 + j // 4))
                        n = b * BT + j
                        dve.tensor_scalar(xn[:, j, :], t.X[:, at(n), :], t.stats[:, at(n), 0], t.rstd[:, at(n)],
                                          ALU.subtract, ALU.mult).then_inc(xn_ready, 1)
                    for s in range(2):
                        half = slice(s * HALF, (s + 1) * HALF)
                        dve.wait_ge(xh_ready, after(b * 2 + s))
                        dve.tensor_tensor(xT[1][:, half], m_bank[s], f32(xT[0][:, half]), ALU.subtract).then_inc(xl_ready, 1)
                    for s in range(2):
                        dve.wait_ge(kt_ready, after(b * 2 + s))
                        dve.scalar_tensor_tensor(kS[0:STACK, s * HALF:(s + 1) * HALF], m_bank[2 + s][0:STACK, :], k_bias,
                                                 f32(kT[:, s, :]), ALU.add, ALU.subtract).then_inc(ks_ready, 1)
                    dve.wait_ge(vp_ready, after(b))
                    dve.tensor_tensor(V[:, :, 0:LAT], o_bank[:, :].rearrange("p (j v) -> p j v", v=VW)[:, :, 0:LAT],
                                      v_bias.unsqueeze(1).to_broadcast([P, BT, LAT]), ALU.add).then_inc(v_ready, 1)
                    for g in range(4):
                        query(b * PAIRS, 0, g)
                    for v in range(16):
                        maximum(b * PAIRS, 0, v)
                    low_max(b * PAIRS, 0)

                def query(m, q, g):
                    c, s = g // 2, g % 2
                    dve.wait_ge(qt_ready, after(m * 4 + g))
                    dve.wait_ge(s_ready, after((m - 1) * 2 * NU - 1))
                    dve.scalar_tensor_tensor(qS[q][c][0:STACK, s * HALF:(s + 1) * HALF], m_bank[g][0:STACK, :],
                                             bcur[:, 0, c:c + 1], f32(qT[:, g % 2, :]), ALU.add, ALU.subtract).then_inc(qs_ready, 1)

                def maximum(m, q, v):
                    dve.wait_ge(sm_ready, after(m * 16 + v))
                    base = (v % 2) * 2 * HALF
                    dve.reduce_max(mx[:, q, v:v + 1], m_all[:, base:base + (v % 8 + 1) * P], AX.X).then_inc(mx_ready, 1)

                def low_max(m, q):
                    dve.wait_ge(mh_ready, after(m))
                    dve.tensor_tensor(ml[:, q, :], o_bank[0:16, 0:P], f32(mh[:, q, :]), ALU.subtract).then_inc(ml_ready, 1)

                def copy_out(m, i, s):
                    dve.wait_ge(y_ready, after(m * 2 + s))
                    dve.tensor_scalar(yT[:, at(i), s * HALF:(s + 1) * HALF], y_bank[:, :], 1.0, None, ALU.mult).then_inc(yc_ready, 1)

                def both(m, q, i, more):
                    if more:
                        for g in range(4):
                            query(m + 1, 1 - q, g)
                        for v in range(6):
                            maximum(m + 1, 1 - q, v)
                    copy_out(m, i, 0)
                    if more:
                        for v in range(6, 16):
                            maximum(m + 1, 1 - q, v)
                        low_max(m + 1, 1 - q)
                    copy_out(m, i, 1)

                def stage3(b):
                    for j in range(BT):
                        n = b * BT + j
                        heads = m_all[:, (j % 2) * 2 * HALF:(j % 2 + 1) * 2 * HALF].rearrange("p (h v) -> p h v", v=VW)
                        dve.wait_ge(zt_ready, after(n))
                        dve.reciprocal(rcp[:, j % 2, :], heads[:, :, LAT]).then_inc(r_ready, 1)
                        dve.wait_ge(r_ready, after(n))
                        dve.wait_ge(zz_ready, after(n - 2))
                        dve.tensor_tensor(z[:, j % 2, 0:HEADS * LAT].rearrange("p (h v) -> p h v", v=LAT), heads[:, :, 0:LAT],
                                          rcp[:, j % 2, :].unsqueeze(2).to_broadcast([P, HEADS, LAT]), ALU.mult).then_inc(z_ready, 1)
                        if j >= 1:
                            dve.wait_ge(o_ready, after(n - 1))
                            res.add(dve, n - 1, (j - 1) % 2, n - 1, o_bank[:, 0:P])
                    dve.wait_ge(o_ready, after(b * BT + BT - 1))
                    res.add(dve, b * BT + BT - 1, 1, b * BT + BT - 1, o_bank[:, 0:P])

                pipeline(dve, stage0, both, stage3)
        sem.clear()





def attn1_laid_out(np, a, r):
    wd = np.repeat(a["L1_attn_Wd_w"].transpose(1, 0, 2)[:, :, None, :], 3, axis=2)
    r["wd"] = wd.reshape(P, HEADS * STACK)
    r["latent"] = np.tile(a["L1_attn_latent_w"], (1, 3))
    wo = np.zeros((ZW, DIM), np.float32)
    wo[0:HEADS * LAT] = a["L1_attn_out_w"]
    wo[HEADS * LAT] = a["L1_attn_out_b"]
    r["wo"] = wo.reshape(5, P, DIM).transpose(1, 0, 2).reshape(P, ZW)
    small = np.zeros((P, L1_COLS), np.float32)
    small[:, 0:LAT] = a["L1_attn_latent_b"]
    small[0:STACK, 36] = np.tile(a["L1_attn_latent_b"], 3)
    small[LAT:2 * LAT, 37] = 1.0
    small[2 * LAT:STACK, 38] = 1.0
    small[0:STACK, 40:40 + HEADS] = np.tile(a["L1_attn_Wd_b"].T, (3, 1))
    r["attn1_small"] = small


def macaron(nc, d, out, phases=("moe", "attn0", "moe", "ffn", "attn1", "ffn")):
    t = Shared()
    with ExitStack() as ctx:
        def sb(name, shape, dt=F32):
            return ctx.enter_context(nc.sbuf_tensor(name, shape, dt))

        t.X = sb("X", [P, TILES, DIM])
        t.stats = sb("stats", [P, TILES, 2])
        t.rstd = sb("rstd", [P, TILES])
        t.consts = sb("consts", [P, CONSTS])
        t.ident = t.consts[:, C_IDENT:C_IDENT + P]
        t.bconsts = sb("bconsts", [P, CONSTS - C_IDENT], BF16)
        t.identb = t.bconsts[:, 0:P]
        t.neg_qk = t.bconsts[:, C_NEG_QK - C_IDENT:C_NEG_KQ - C_IDENT]
        t.neg_kq = t.bconsts[:, C_NEG_KQ - C_IDENT:C_NEG_KQ - C_IDENT + HALF]
        t.iota8 = t.consts[:, C_IOTA:C_IOTA + EXPERTS]
        load_input(nc, t, d)
        for n, name in enumerate(phases):
            if name == "moe":
                with ExitStack() as moe:
                    t.rout = [moe.enter_context(nc.sbuf_tensor(f"m{n}_routers{i}", [P, 2 * EXPERTS + KC * EXPERTS], F32R)) for i in range(2)]
                    t.W = [[moe.enter_context(nc.sbuf_tensor(f"m{n}_W{w}{i}", [P, EXPERTS * INNER], F32R)) for i in range(2)] for w in "gud"]
                    load_experts(nc, t, d, f"m{n}")
                    moe_phase(nc, t, f"m{n}")
            if name == "attn0":
                attn0_phase(nc, t, d, f"a{n}")
            if name == "ffn":
                ffn_phase(nc, t, d, f"f{n}", None)
            if name == "attn1":
                attn1_phase(nc, t, d, f"b{n}")
        store_phase(nc, t, out)


def store_phase(nc, t, out):
    with nc.semaphore("out_done") as out_done, nc.Block() as block:
        @block.sync
        def _(sp):
            sp.dma_start(out.rearrange("(n p) c -> p n c", p=P), t.X[:, :, :]).then_inc(out_done, 16)
            sp.wait_ge(out_done, 16)


C_EPS, C_IOTA, C_IDENT = 0, 8, 16
C_NEG_QK = C_IDENT + P
C_NEG_KQ = C_NEG_QK + P
CONSTS = C_NEG_KQ + HALF
NEG = -1e30


def constants(np):
    c = np.zeros((P, CONSTS), np.float32)
    c[:, C_EPS] = EPS
    c[:, C_IOTA:C_IOTA + EXPERTS] = np.arange(EXPERTS)
    c[:, C_IDENT:C_IDENT + P] = np.eye(P)
    c[:, C_NEG_QK:C_NEG_KQ] = NEG * np.triu(np.ones((P, P)), 1)
    c[:, C_NEG_KQ:] = np.tile(NEG * np.tril(np.ones((P, P)), -1), (1, 4))
    return c


def laid_out(inputs):
    import numpy as np

    a = {k: np.asarray(v) for k, v in inputs.items()}
    r = {}
    r["x"] = a["L0_attn_x"].reshape(BATCH * SEQ, DIM)
    r["w_gate"] = a["L0_ffn_w_gate"].transpose(2, 0, 1).reshape(P, EXPERTS * INNER)
    r["w_up"] = a["L0_ffn_w_up"].transpose(2, 0, 1).reshape(P, EXPERTS * INNER)
    r["w_down"] = a["L0_ffn_w_down"].reshape(EXPERTS, DIM, KC, P).transpose(3, 2, 0, 1).reshape(P, KC * EXPERTS * DIM)
    r["routers"] = np.concatenate([
        a["L0_ffn_router_gate"].T, a["L0_ffn_router_up"].T,
        a["L0_ffn_router_down"].reshape(EXPERTS, KC, P).transpose(2, 1, 0).reshape(P, KC * EXPERTS)], axis=1)
    r["consts"] = constants(np)
    attn0_laid_out(np, a, r)
    ffn_laid_out(np, a, r)
    attn1_laid_out(np, a, r)
    return {k: np.ascontiguousarray(v) for k, v in r.items()}


def kernel(**inputs):
    import concourse.bacc as bacc
    from concourse.bass_utils import run_bass_kernel_spmd

    nc = bacc.Bacc("TRN2", target_bir_lowering=False, num_devices=1)
    arrays = {f"in_{k}": v for k, v in laid_out(inputs).items()}
    d = {k[3:]: nc.dram_tensor(k, v.shape, mybir.dt.from_np(v.dtype), kind="ExternalInput").ap() for k, v in arrays.items()}
    out = nc.dram_tensor("out", (BATCH * SEQ, DIM), F32, kind="ExternalOutput").ap()
    macaron(nc, d, out)
    r = run_bass_kernel_spmd(nc, [arrays], core_ids=[0])
    return r.results[0]["out"].reshape(BATCH, SEQ, DIM)
```

```python
import concourse.bass as bass
from concourse import mybir
from contextlib import ExitStack

F32 = mybir.dt.float32
F32R = mybir.dt.float32r
BF16 = mybir.dt.bfloat16
U32 = mybir.dt.uint32
ALU = mybir.AluOpType
ACT = mybir.ActivationFunctionType
AX = mybir.AxisListType

P = 128
BATCH, SEQ, DIM = 4, 1024, 128
TILES = BATCH * SEQ // P
BT = SEQ // P
EXPERTS, INNER = 8, 512
KC = INNER // P
HALF = 512
HEADS, HD = 16, 8
GROUPS, GH = 4, 4
LAT = 36
EPS = 1e-5
SCORE_SCALE = HD ** -0.5

LEAD = 64


def after(n):
    return n + 1 + LEAD


def at(t):
    return bass.ds(t, 1)


def f32(ap):
    return ap.bitcast(F32)


class Links:

    def __init__(self, eng, sem, per):
        self.eng, self.sem, self.per = eng, sem, per
        self.item, self.k = 0, per

    def start(self, item):
        assert self.k == self.per, (self.k, self.per)
        self.item, self.k = item, 0

    def mark(self, ins):
        ins.then_inc(self.sem, 1)
        self.k += 1

    def wait(self):
        self.eng.wait_ge(self.sem, self.item * self.per + (self.k + LEAD))


def layernorm_scales(act, dve, nc, t, sqrt_ready):
    if act is not None:
        act.activation(t.rstd[:, :], t.stats[:, :, 1], ACT.Sqrt, bias=t.consts[:, 0:1]).then_inc(sqrt_ready, 1)
    if dve is not None:
        dve.wait_ge(sqrt_ready, 1)
        dve.reciprocal(t.rstd[:, :], t.rstd[:, :]).then_inc(sqrt_ready, 1)
        dve.wait_ge(sqrt_ready, 2)


class Semaphores:

    def __init__(self, ctx, nc, tag):
        self.ctx, self.nc, self.tag, self.all = ctx, nc, tag, []

    def __call__(self, name):
        s = self.ctx.enter_context(self.nc.semaphore(f"{self.tag}_{name}"))
        self.all.append(s)
        return s

    def clear(self):
        with self.nc.Block() as block:
            @block.sync
            def _(sp):
                for s in self.all:
                    sp.sem_clear(s)


class ResidualAdd:

    def __init__(self, ctx, nc, sem, t, tag, tiles):
        self.t, self.tiles = t, tiles
        self.xo = ctx.enter_context(nc.sbuf_tensor(f"{tag}_xo", [P, 2, tiles, DIM], F32))
        self.stat6 = ctx.enter_context(nc.sbuf_tensor(f"{tag}_stat6", [P, 2, tiles, 6], F32))
        self.aggr = ctx.enter_context(nc.sbuf_tensor(f"{tag}_aggr", [P, 2, tiles, 2], F32))
        self.xo_ready, self.stat_ready, self.pause = sem("xo_ready"), sem("stat_ready"), sem("dve_pause")

    def prime(self, dve):
        dve.sem_inc(self.xo_ready, LEAD)
        dve.sem_inc(self.stat_ready, LEAD)

    def add(self, dve, item, q, tile, bank):
        t, some = self.t, bass.ds(tile, self.tiles)
        dve.tensor_tensor(self.xo[:, q, :, :], bank.rearrange("p (j c) -> p j c", c=DIM), t.X[:, some, :],
                          ALU.add).then_inc(self.xo_ready, 1)
        dve.wait_ge(self.xo_ready, after(item))
        dve.sem_inc(self.pause, 1)
        dve.tensor_copy(t.X[:, some, :], self.xo[:, q, :, :])
        for j in range(self.tiles):
            ins = dve.bn_stats(self.stat6[:, q, j, :], self.xo[:, q, j, :])
        ins.then_inc(self.stat_ready, 1)
        dve.wait_ge(self.stat_ready, after(item * 2))
        dve.sem_inc(self.pause, 1)
        for j in range(self.tiles):
            ins = dve.bn_aggr(self.aggr[:, q, j, :], self.stat6[:, q, j, :])
        ins.then_inc(self.stat_ready, 1)
        dve.wait_ge(self.stat_ready, after(item * 2 + 1))
        dve.sem_inc(self.pause, 1)
        dve.tensor_copy(t.stats[:, some, :], self.aggr[:, q, :, :])


class Shared:
    pass


def load_input(nc, t, d):
    with ExitStack() as ctx:
        stat6 = ctx.enter_context(nc.sbuf_tensor("stat6", [P, TILES, 6], F32))
        sem = Semaphores(ctx, nc, "in")
        x_in, c_in, stat_ready = [sem(f"x_in{i}") for i in range(2)], sem("const_in"), sem("stat_ready")
        with nc.Block() as block:
            @block.sync
            def _(sp):
                for i in range(2):
                    sp.dma_start(t.X[:, 16 * i:16 * i + 16, :],
                                 d["x"].rearrange("(n p) c -> p n c", p=P)[:, 16 * i:16 * i + 16, :]).then_inc(x_in[i], 16)
                sp.dma_start(t.consts[:, :], d["consts"]).then_inc(c_in, 16)

            @block.vector
            def _(dve):
                for i in range(TILES):
                    if i % 16 == 0:
                        dve.wait_ge(x_in[i // 16], 16)
                    dve.bn_stats(stat6[:, i, :], t.X[:, i, :]).then_inc(stat_ready, 1)
                for i in range(TILES):
                    dve.wait_ge(stat_ready, i + 1)
                    dve.bn_aggr(t.stats[:, i, :], stat6[:, i, :])
                dve.wait_ge(c_in, 16)
                dve.tensor_copy(t.bconsts[:, :], t.consts[:, C_IDENT:CONSTS])
        sem.clear()


def load_experts(nc, t, d, tag):
    with ExitStack() as ctx:
        stage = [ctx.enter_context(nc.sbuf_tensor(f"{tag}_stage{i}", [P, EXPERTS * INNER], F32)) for i in range(3)]
        rstage = ctx.enter_context(nc.sbuf_tensor(f"{tag}_rstage", [P, 2 * EXPERTS + KC * EXPERTS], F32))
        sem = Semaphores(ctx, nc, f"{tag}_load")
        w_in, high_ready = [sem(f"w_in{i}") for i in range(4)], sem("high_ready")
        with nc.Block() as block:
            @block.sync
            def _(sp):
                sp.dma_start(rstage[:, :], d["routers"]).then_inc(w_in[3], 16)
                for i, name in enumerate(("w_gate", "w_up", "w_down")):
                    sp.dma_start(stage[i][:, :], d[name]).then_inc(w_in[i], 16)

            @block.scalar
            def _(act):
                act.wait_ge(w_in[3], 16)
                act.activation(t.rout[0][:, :], rstage[:, :], ACT.Copy).then_inc(high_ready, 1)
                for i in range(3):
                    act.wait_ge(w_in[i], 16)
                    act.activation(t.W[i][0][:, :], stage[i][:, :], ACT.Copy).then_inc(high_ready, 1)

            @block.vector
            def _(dve):
                dve.wait_ge(high_ready, 1)
                dve.tensor_tensor(t.rout[1][:, :], rstage[:, :], f32(t.rout[0][:, :]), ALU.subtract)
                for i in range(3):
                    dve.wait_ge(high_ready, i + 2)
                    dve.tensor_tensor(t.W[i][1][:, :], stage[i][:, :], f32(t.W[i][0][:, :]), ALU.subtract)
        sem.clear()


def moe_phase(nc, t, tag):
    with ExitStack() as ctx:
        def sb(name, shape, dt=F32):
            return ctx.enter_context(nc.sbuf_tensor(f"{tag}_{name}", shape, dt))

        sem = Semaphores(ctx, nc, tag)

        xn = sb("xn", [P, 2, DIM])
        xh = [sb(f"xh{i}", [P, P], F32R) for i in range(2)]
        xl = [sb(f"xl{i}", [P, P], F32R) for i in range(2)]
        logits = sb("logits", [P, 2, 16])
        top = sb("top", [P, 2, 2, 8])
        topi = sb("topi", [P, 2, 2, 8], U32)
        pick = sb("pick", [P, 2, 2, 2])
        gap = sb("gap", [P, 2, 2])
        prob = sb("prob", [P, 2, 2, 2])
        part = sb("part", [P, 2, 2, 2, EXPERTS])
        comb = sb("comb", [P, 2, 2, EXPERTS])
        dlogits = sb("dlogits", [P, 2, 8])
        dtop = sb("dtop", [P, 2, 8])
        dtopi = sb("dtopi", [P, 2, 8], U32)
        dpick = sb("dpick", [P, 2, 2])
        dgap = sb("dgap", [P, 2, 1])
        dprob = sb("dprob", [P, 2, 2])
        dhalf = sb("dhalf", [P, 2, 2])
        dpart = sb("dpart", [P, 2, 2, EXPERTS])
        dcomb = sb("dcomb", [P, 2, EXPERTS])
        acc = sb("acc", [P, 2, 2, INNER])
        sig = sb("sig", [P, 2, INNER])
        gated = sb("gated", [P, 2, INNER])
        inter = sb("inter", [P, 2, INNER])
        ih = [sb(f"ih{i}", [P, INNER], F32R) for i in range(2)]
        il = [sb(f"il{i}", [P, INNER], F32R) for i in range(2)]
        yacc = sb("yacc", [P, 2, DIM])
        stat6 = sb("stat6", [P, 2, 6])

        ps = [ctx.enter_context(nc.psum_tensor(f"{tag}_ps{i}", [P, HALF], F32)) for i in range(8)]
        expert_bank, a_bank, t_bank, y_bank = ps[0:4], ps[4], ps[5], ps[6:8]

        rstd_ready = sem("rstd_ready")
        xn_ready, xt_ready, xh_ready, xl_ready = sem("xn_ready"), sem("xt_ready"), sem("xh_ready"), sem("xl_ready")
        lg_ready, lg_copied, gap_ready, prob_ready, comb_ready = (
            sem("lg_ready"), sem("lg_copied"), sem("gap_ready"), sem("prob_ready"), sem("comb_ready"))
        prod_ready, first_used, prod_used = sem("prod_ready"), sem("first_used"), sem("prod_used")
        sig_ready, gated_ready, inter_ready = sem("sig_ready"), sem("gated_ready"), sem("inter_ready")
        it_ready, ih_ready, il_ready = sem("it_ready"), sem("ih_ready"), sem("il_ready")
        dlg_ready, dlg_copied, dgap_ready, dprob_ready, dcomb_ready = (
            sem("dlg_ready"), sem("dlg_copied"), sem("dgap_ready"), sem("dprob_ready"), sem("dcomb_ready"))
        y_ready, y_used = sem("y_ready"), sem("y_used")
        dve_a, dve_c, dve_y = sem("dve_a"), sem("dve_c"), sem("dve_y")
        pool_a, pool_c = sem("pool_a"), sem("pool_c")
        dve_pause, pool_pause = sem("dve_pause"), sem("pool_pause")
        aggr = sb("aggr", [P, 2, 2])

        ND = 2 * EXPERTS - 2
        wg, wu, wd = t.W

        def exists(m):
            return not isinstance(m, int) or 0 <= m < TILES

        def tiles(eng, body):
            body(0, 0)
            body(1, 1)
            with eng.Fori(0, (TILES - 4) // 2) as i:
                for q in range(2):
                    body(i * 2 + (2 + q), q)
            for n in range(TILES - 2, TILES + 2):
                body(n, n % 2)

        with nc.Block() as block:
            @block.tensor
            def _(pe):
                for s in (xt_ready, lg_ready, prod_ready, it_ready, dlg_ready, y_ready):
                    pe.sem_inc(s, LEAD)

                def transpose_x(n, q):
                    pe.wait_ge(xn_ready, after(n))
                    pe.wait_ge(lg_copied, after(n - 1))
                    pe.transpose(a_bank[:, 0:P], xn[:, q, :], t.ident).then_inc(xt_ready, 1)

                def route_gu(n, q):
                    pe.wait_ge(xh_ready, after(n))
                    pe.wait_ge(xl_ready, after(n))
                    for k, (a, b) in enumerate(((xh, 0), (xh, 1), (xl, 0))):
                        last = pe.matmul(a_bank[:, P:P + 16], a[q][:, :], t.rout[b][:, 0:16], start=k == 0, stop=k == 2)
                    last.then_inc(lg_ready, 1)

                def product(n, q, j):
                    if j < 4:
                        pe.wait_ge(prod_used, after(n * ND + (j - 4)))
                    elif j < 6:
                        pe.wait_ge(first_used, after(n * 2 + (j - 4)))
                    else:
                        pe.wait_ge(prod_used, after(n * ND + (j - 6)))
                    w, e = (wg, wu)[j % 2], j // 2
                    cols = slice(e * INNER, (e + 1) * INNER)
                    for k, (a, b) in enumerate(((xh, 0), (xh, 1), (xl, 0))):
                        last = pe.matmul(expert_bank[j % 4][:, :], a[q][:, :], w[b][:, cols], start=k == 0, stop=k == 2)
                    last.then_inc(prod_ready, 1)

                def transpose_inter(n, q):
                    pe.wait_ge(inter_ready, after(n))
                    pe.wait_ge(dlg_copied, after(n - 1))
                    for c in range(KC):
                        last = pe.transpose(t_bank[:, c * P:(c + 1) * P], inter[:, q, c * P:(c + 1) * P], t.ident)
                    last.then_inc(it_ready, 1)

                def route_down(n, q):
                    pe.wait_ge(ih_ready, after(n))
                    pe.wait_ge(il_ready, after(n))
                    k = 0
                    for c in range(KC):
                        rows = slice(c * P, (c + 1) * P)
                        rcol = slice(16 + c * EXPERTS, 16 + (c + 1) * EXPERTS)
                        for a, b in ((ih, 0), (ih, 1), (il, 0)):
                            last = pe.matmul(t_bank[:, 0:EXPERTS], a[q][:, rows], t.rout[b][:, rcol], start=k == 0, stop=k == 11)
                            k += 1
                    last.then_inc(dlg_ready, 1)

                def down(n, q, h, c):
                    if c == 0:
                        pe.wait_ge(ih_ready, after(n))
                        pe.wait_ge(il_ready, after(n))
                        pe.wait_ge(y_used, after((n - 1) * 2 + h))
                    rows = slice(c * P, (c + 1) * P)
                    cols = slice(c * 1024 + h * HALF, c * 1024 + (h + 1) * HALF)
                    for k, (a, b) in enumerate(((ih, 0), (ih, 1), (il, 0))):
                        last = pe.matmul(y_bank[h][:, :], a[q][:, rows], wd[b][:, cols],
                                         start=c == 0 and k == 0, stop=c == KC - 1 and k == 2)
                    if c == KC - 1:
                        last.then_inc(y_ready, 1)

                def body(n, q):
                    for j in range(16):
                        if exists(n):
                            product(n, q, j)
                        if j == 1 and exists(n + 1):
                            transpose_x(n + 1, 1 - q)
                        if j == 5 and exists(n - 1):
                            transpose_inter(n - 1, 1 - q)
                        if j == 6 and exists(n + 1):
                            route_gu(n + 1, 1 - q)
                        if j == 8 and exists(n - 1):
                            route_down(n - 1, 1 - q)
                        if j % 2 == 1 and j < 8 and exists(n - 2):
                            down(n - 2, q, 1, j // 2)
                        if j % 2 == 1 and j > 8 and exists(n - 1):
                            down(n - 1, 1 - q, 0, j // 2 - 4)

                transpose_x(0, 0)
                route_gu(0, 0)
                tiles(pe, body)

            @block.scalar
            def _(act):
                layernorm_scales(act, None, nc, t, rstd_ready)
                for s in (xh_ready, prob_ready, first_used, sig_ready, ih_ready, dprob_ready):
                    act.sem_inc(s, LEAD)

                def high_x(n, q):
                    act.wait_ge(xt_ready, after(n))
                    act.wait_ge(prod_ready, after((n - 2) * 16 + 15))
                    act.activation(xh[q][:, :], a_bank[:, 0:P], ACT.Copy).then_inc(xh_ready, 1)

                def probs(n, q):
                    act.wait_ge(gap_ready, after(n * 2 + 1))
                    act.wait_ge(comb_ready, after(n - 2))
                    act.activation(prob[:, q, :, 0], gap[:, q, :], ACT.Sigmoid)
                    act.activation(prob[:, q, :, 1], gap[:, q, :], ACT.Sigmoid, scale=-1.0).then_inc(prob_ready, 1)

                def first(n, q):
                    act.wait_ge(comb_ready, after(n))
                    act.wait_ge(inter_ready, after(n - 2))
                    for j in range(2):
                        act.wait_ge(prod_ready, after(n * 16 + j))
                        act.activation(acc[:, q, j, :], expert_bank[j][:, :], ACT.Copy,
                                       scale=comb[:, q, j, 0:1]).then_inc(first_used, 1)

                def sigmoid(n, q):
                    act.wait_ge(prod_used, after(n * ND + (ND - 2)))
                    act.wait_ge(gated_ready, after(n - 2))
                    act.activation(sig[:, q, :], acc[:, q, 0, :], ACT.Sigmoid).then_inc(sig_ready, 1)

                def high_inter(n, q):
                    act.wait_ge(it_ready, after(n))
                    act.wait_ge(y_ready, after((n - 2) * 2 + 1))
                    act.activation(ih[q][:, :], t_bank[:, :], ACT.Copy).then_inc(ih_ready, 1)

                def dprobs(n, q):
                    act.wait_ge(dgap_ready, after(n * 2 + 1))
                    act.wait_ge(dcomb_ready, after(n - 2))
                    act.activation(dprob[:, q, 0:1], dgap[:, q, :], ACT.Sigmoid)
                    act.activation(dprob[:, q, 1:2], dgap[:, q, :], ACT.Sigmoid, scale=-1.0).then_inc(dprob_ready, 1)

                def body(n, q):
                    if exists(n):
                        first(n, q)
                    if exists(n + 1):
                        high_x(n + 1, 1 - q)
                    if exists(n - 1):
                        high_inter(n - 1, 1 - q)
                    if exists(n + 1):
                        probs(n + 1, 1 - q)
                    if exists(n - 1):
                        dprobs(n - 1, 1 - q)
                    if exists(n):
                        sigmoid(n, q)

                high_x(0, 0)
                probs(0, 0)
                tiles(act, body)

            @block.gpsimd
            def _(pool):
                for s in (comb_ready, gated_ready, inter_ready, dcomb_ready, pool_a, pool_c):
                    pool.sem_inc(s, LEAD)
                own_a, own_c = Links(pool, pool_a, 1), Links(pool, pool_c, 2)

                def combine(n, q):
                    own_a.start(n)
                    pool.wait_ge(prob_ready, after(n))
                    pool.wait_ge(prod_used, after((n - 2) * ND + (ND - 1)))
                    pool.wait_ge(first_used, after((n - 2) * 2 + 1))
                    pool.sem_inc(pool_pause, 1)
                    for r in range(2):
                        for k in range(2):
                            ins = pool.tensor_scalar(part[:, q, r, k, :], t.iota8, pick[:, q, r, k:k + 1],
                                                     prob[:, q, r, k:k + 1], ALU.is_equal, ALU.mult)
                    own_a.mark(ins)
                    own_a.wait()
                    pool.tensor_tensor(comb[:, q, :, :], part[:, q, :, 0, :], part[:, q, :, 1, :], ALU.add).then_inc(comb_ready, 1)

                def dcombine(n, q):
                    own_c.start(n)
                    pool.wait_ge(dprob_ready, after(n))
                    pool.wait_ge(y_used, after((n - 2) * 2 + 1))
                    pool.sem_inc(pool_pause, 1)
                    own_c.mark(pool.tensor_scalar(dhalf[:, q, :], dprob[:, q, :], 0.5, None, ALU.mult))
                    own_c.wait()
                    pool.sem_inc(pool_pause, 1)
                    for k in range(2):
                        ins = pool.tensor_scalar(dpart[:, q, k, :], t.iota8, dpick[:, q, k:k + 1],
                                                 dhalf[:, q, k:k + 1], ALU.is_equal, ALU.mult)
                    own_c.mark(ins)
                    own_c.wait()
                    pool.tensor_tensor(dcomb[:, q, :], dpart[:, q, 0, :], dpart[:, q, 1, :], ALU.add).then_inc(dcomb_ready, 1)

                def gate(n, q):
                    pool.wait_ge(sig_ready, after(n))
                    pool.tensor_tensor(gated[:, q, :], acc[:, q, 0, :], sig[:, q, :], ALU.mult).then_inc(gated_ready, 1)
                    pool.wait_ge(gated_ready, after(n))
                    pool.wait_ge(prod_used, after(n * ND + (ND - 1)))
                    pool.wait_ge(it_ready, after(n - 2))
                    pool.tensor_tensor(inter[:, q, :], gated[:, q, :], acc[:, q, 1, :], ALU.mult).then_inc(inter_ready, 1)

                def body(n, q):
                    if exists(n + 1):
                        combine(n + 1, 1 - q)
                    if exists(n - 1):
                        dcombine(n - 1, 1 - q)
                    if exists(n):
                        gate(n, q)

                combine(0, 0)
                tiles(pool, body)

            @block.vector
            def _(dve):
                layernorm_scales(None, dve, nc, t, rstd_ready)
                for s in (xn_ready, xl_ready, lg_copied, gap_ready, prod_used, il_ready, dlg_copied, dgap_ready,
                          y_used, dve_a, dve_c, dve_y):
                    dve.sem_inc(s, LEAD)
                own_a, own_c, own_y = Links(dve, dve_a, 1), Links(dve, dve_c, 1), Links(dve, dve_y, EXPERTS)

                def normalise(n, q):
                    dve.wait_ge(xt_ready, after(n - 2))
                    dve.tensor_scalar(xn[:, q, :], t.X[:, at(n), :], t.stats[:, at(n), 0], t.rstd[:, at(n)],
                                      ALU.subtract, ALU.mult).then_inc(xn_ready, 1)

                def low_x(n, q):
                    dve.wait_ge(xh_ready, after(n))
                    dve.tensor_tensor(xl[q][:, :], a_bank[:, 0:P], f32(xh[q][:, :]), ALU.subtract).then_inc(xl_ready, 1)

                def best_gu(n, q, step):
                    if step == 0:
                        dve.wait_ge(lg_ready, after(n))
                        dve.tensor_copy(logits[:, q, :], a_bank[:, P:P + 16]).then_inc(lg_copied, 1)
                    if step == 1:
                        dve.wait_ge(lg_copied, after(n))
                        dve.sem_inc(dve_pause, 1)
                        own_a.start(n)
                        for r in range(2):
                            ins = dve.max(top[:, q, r, :], logits[:, q, 8 * r:8 * r + 8])
                        own_a.mark(ins)
                    if step == 2:
                        own_a.wait()
                        dve.wait_ge(comb_ready, after(n - 2))
                        dve.sem_inc(dve_pause, 1)
                        for r in range(2):
                            ins = dve.max_index(topi[:, q, r, :], top[:, q, r, :], logits[:, q, 8 * r:8 * r + 8])
                        ins.then_inc(gap_ready, 1)
                    if step == 3:
                        dve.wait_ge(gap_ready, after(n * 2))
                        dve.tensor_copy(pick[:, q, :, :], topi[:, q, :, 0:2])
                        dve.tensor_tensor(gap[:, q, :], top[:, q, :, 0], top[:, q, :, 1], ALU.subtract).then_inc(gap_ready, 1)

                def add(n, q, j):
                    dve.wait_ge(prod_ready, after(n * 16 + j))
                    if j < 4:
                        dve.wait_ge(first_used, after(n * 2 + (j - 2)))
                    else:
                        dve.wait_ge(prod_used, after(n * ND + (j - 4)))
                    r, e = j % 2, j // 2
                    dve.scalar_tensor_tensor(acc[:, q, r, :], expert_bank[j % 4][:, :], comb[:, q, r, e:e + 1],
                                             acc[:, q, r, :], ALU.mult, ALU.add).then_inc(prod_used, 1)

                def low_inter(n, q):
                    dve.wait_ge(ih_ready, after(n))
                    dve.tensor_tensor(il[q][:, :], t_bank[:, :], f32(ih[q][:, :]), ALU.subtract).then_inc(il_ready, 1)

                def best_down(n, q, step):
                    if step == 0:
                        dve.wait_ge(dlg_ready, after(n))
                        dve.tensor_copy(dlogits[:, q, :], t_bank[:, 0:EXPERTS]).then_inc(dlg_copied, 1)
                    if step == 1:
                        dve.wait_ge(dlg_copied, after(n))
                        dve.sem_inc(dve_pause, 1)
                        own_c.start(n)
                        own_c.mark(dve.max(dtop[:, q, :], dlogits[:, q, :]))
                    if step == 2:
                        own_c.wait()
                        dve.wait_ge(dcomb_ready, after(n - 2))
                        dve.sem_inc(dve_pause, 1)
                        dve.max_index(dtopi[:, q, :], dtop[:, q, :], dlogits[:, q, :]).then_inc(dgap_ready, 1)
                    if step == 3:
                        dve.wait_ge(dgap_ready, after(n * 2))
                        dve.tensor_copy(dpick[:, q, :], dtopi[:, q, 0:2])
                        dve.tensor_tensor(dgap[:, q, :], dtop[:, q, 0:1], dtop[:, q, 1:2], ALU.subtract).then_inc(dgap_ready, 1)

                def add_down(n, q, e):
                    if e == 0:
                        own_y.start(n)
                        dve.wait_ge(dcomb_ready, after(n))
                    if e % 4 == 0:
                        dve.wait_ge(y_ready, after(n * 2 + e // 4))
                    if e == 4:
                        dve.wait_ge(y_used, after(n * 2))
                    elif e:
                        own_y.wait()
                    src = t.X[:, at(n), :] if e == 0 else yacc[:, q, :]
                    dst = t.X[:, at(n), :] if e == EXPERTS - 1 else yacc[:, q, :]
                    ins = dve.scalar_tensor_tensor(dst, y_bank[e // 4][:, (e % 4) * P:(e % 4 + 1) * P],
                                                   dcomb[:, q, e:e + 1], src, ALU.mult, ALU.add)
                    if e % 4 == 3:
                        ins.then_inc(y_used, 1)
                    else:
                        own_y.mark(ins)

                def statistics(n, q, step):
                    if step == 0:
                        dve.wait_ge(y_used, after(n * 2 + 1))
                        dve.sem_inc(dve_pause, 1)
                        own_y.mark(dve.bn_stats(stat6[:, q, :], t.X[:, at(n), :]))
                    else:
                        own_y.wait()
                        dve.sem_inc(dve_pause, 1)
                        if step == 1:
                            own_y.mark(dve.bn_aggr(aggr[:, q, :], stat6[:, q, :]))
                        else:
                            dve.tensor_copy(t.stats[:, at(n), :], aggr[:, q, :])

                def body(n, q):
                    for j in range(16):
                        if j >= 2 and exists(n):
                            add(n, q, j)
                        if j == 3 and exists(n + 1):
                            low_x(n + 1, 1 - q)
                        if j == 7 and exists(n - 1):
                            low_inter(n - 1, 1 - q)
                        if 8 <= j <= 11 and exists(n + 1):
                            best_gu(n + 1, 1 - q, j - 8)
                        if 12 <= j and exists(n - 1):
                            best_down(n - 1, 1 - q, j - 12)
                        if exists(n - 2):
                            if j <= 3:
                                add_down(n - 2, q, j)
                            if 9 <= j <= 12:
                                add_down(n - 2, q, j - 5)
                            if 13 <= j:
                                statistics(n - 2, q, j - 13)
                    if exists(n + 2):
                        normalise(n + 2, q)

                normalise(0, 0)
                normalise(1, 1)
                low_x(0, 0)
                for step in range(4):
                    best_gu(0, 0, step)
                tiles(dve, body)
        sem.clear()


def ffn_phase(nc, t, d, tag, out):
    with ExitStack() as ctx:
        def sb(name, shape, dt=F32):
            return ctx.enter_context(nc.sbuf_tensor(f"{tag}_{name}", shape, dt))

        sem = Semaphores(ctx, nc, tag)

        w1 = sb("w1", [P, INNER])
        w2 = sb("w2", [P, INNER])
        small = sb("small", [P, FFN_SMALL])
        b1, b2, scale = small[:, 0:4], small[:, 4:5], small[0:8, 5:6]
        first_half, second_half = small[0:8, 8:12], small[0:8, 12:16]
        b2h = sb("b2h", [P, 1])
        xn = sb("xn", [P, BT, DIM])
        xT = sb("xT", [P, SEQ])
        even = sb("even", [8, DIM])
        odd = sb("odd", [8, DIM])
        evens = sb("evens", [8, DIM])
        odds = sb("odds", [8, KC, DIM])
        evenm = sb("evenm", [8, 4, 4, 32])
        w1e = sb("w1e", [P, INNER])
        w2e = sb("w2e", [P, INNER])
        hid = sb("hid", [P, 2, KC, HALF])
        oT = sb("oT", [P, 2, HALF])
        xo = sb("xo", [P, 2, KC, DIM])
        stat6 = sb("stat6", [P, 2, KC, 6])
        aggr = sb("aggr", [P, 2, KC, 2])
        ps = [ctx.enter_context(nc.psum_tensor(f"{tag}_ps{i}", [P, HALF], F32)) for i in range(8)]
        x_bank, w_bank, h_bank, o_bank = ps[0:2], ps[2], ps[3:7], ps[7]

        w_in, s_in, rstd_ready, b2h_ready = sem("w_in"), sem("s_in"), sem("rstd_ready"), sem("b2h_ready")
        xn_ready, rows_in, pairs_ready = sem("xn_ready"), sem("rows_in"), sem("pairs_ready")
        xt_ready, xt_copied, wp_ready, we_ready = sem("xt_ready"), sem("xt_copied"), sem("wp_ready"), sem("we_ready")
        h_ready, hid_ready, o_ready, o_copied = sem("h_ready"), sem("hid_ready"), sem("o_ready"), sem("o_copied")
        ot_ready, xo_ready, stat_ready = sem("ot_ready"), sem("xo_ready"), sem("stat_ready")
        dve_pause = sem("dve_pause")

        with nc.Block() as block:
            @block.sync
            def _(sp):
                sp.dma_start(w1[:, :], d["w1"]).then_inc(w_in, 16)
                sp.dma_start(w2[:, :], d["w2"]).then_inc(w_in, 16)
                sp.dma_start(small[:, :], d["ffn_small"]).then_inc(s_in, 16)
                with sp.Fori(0, BATCH) as b:
                    sp.wait_ge(xn_ready, after(b * BT))
                    sp.wait_ge(we_ready, after((b - 1) * 2 + 1))
                    sp.dma_start(even[:, :], xn[1:16:2, 0, :]).then_inc(rows_in, 16)
                    sp.dma_start(odd[:, :], xn[2:17:2, 0, :]).then_inc(rows_in, 16)

            @block.tensor
            def _(pe):
                for s in (xt_ready, wp_ready, h_ready, o_ready, ot_ready):
                    pe.sem_inc(s, LEAD)
                with pe.Fori(0, BATCH) as b:
                    for s in range(2):
                        pe.wait_ge(xn_ready, after(b * BT + 4 * s + 3))
                        pe.wait_ge(xo_ready, after((b - 1) * 2 + s))
                        for j in range(4):
                            last = pe.transpose(x_bank[s][:, j * P:(j + 1) * P], xn[:, 4 * s + j, :], t.ident)
                        last.then_inc(xt_ready, 1)
                    pe.wait_ge(pairs_ready, after(b * 3 + 2))
                    for p in range(KC):
                        last = pe.matmul(w_bank[:, p * P:(p + 1) * P], odds[:, p, :], even[:, :], start=True, stop=True)
                    last.then_inc(wp_ready, 1)
                    pe.wait_ge(we_ready, after(b * 2))
                    for c in range(KC):
                        last = pe.matmul(w_bank[:, c * P:(c + 1) * P], odd[:, :], evenm[:, c, :, :], start=True, stop=True)
                    last.then_inc(wp_ready, 1)
                    for s in range(2):
                        pe.wait_ge(xt_copied, after(b * 2 + s))
                        for c in range(KC):
                            pe.wait_ge(hid_ready, after((b * 2 + s - 1) * KC + c))
                            pe.matmul(h_bank[c][:, :], w1e[:, c * P:(c + 1) * P], xT[:, s * HALF:(s + 1) * HALF],
                                      start=True, stop=True).then_inc(h_ready, 1)
                    pe.wait_ge(we_ready, after(b * 2 + 1))
                    for s in range(2):
                        pe.wait_ge(o_copied, after(b * 2 + s - 1))
                        for c in range(KC):
                            pe.wait_ge(hid_ready, after((b * 2 + s) * KC + c))
                            last = pe.matmul(o_bank[:, :], w2e[:, c * P:(c + 1) * P], hid[:, s, c, :], start=c == 0, stop=c == KC - 1)
                        last.then_inc(o_ready, 1)
                    for s in range(2):
                        pe.wait_ge(o_copied, after(b * 2 + s))
                        for j in range(4):
                            last = pe.transpose(x_bank[s][:, j * P:(j + 1) * P], oT[:, s, j * P:(j + 1) * P], t.ident)
                        last.then_inc(ot_ready, 1)

            @block.scalar
            def _(act):
                layernorm_scales(act, None, nc, t, rstd_ready)
                for s in (xt_copied, hid_ready, o_copied):
                    act.sem_inc(s, LEAD)
                act.wait_ge(b2h_ready, 1)
                with act.Fori(0, BATCH) as b:
                    for s in range(2):
                        act.wait_ge(xt_ready, after(b * 2 + s))
                        act.wait_ge(h_ready, after((b - 1) * 2 * KC + (s + 1) * KC - 1))
                        act.activation(xT[:, s * HALF:(s + 1) * HALF], x_bank[s][:, :], ACT.Copy).then_inc(xt_copied, 1)
                    for s in range(2):
                        for c in range(KC):
                            act.wait_ge(h_ready, after((b * 2 + s) * KC + c))
                            act.wait_ge(o_ready, after((b - 1) * 2 + s))
                            act.activation(hid[:, s, c, :], h_bank[c][:, :], ACT.Gelu, bias=b1[:, c:c + 1]).then_inc(hid_ready, 1)
                    for s in range(2):
                        act.wait_ge(o_ready, after(b * 2 + s))
                        act.wait_ge(ot_ready, after((b - 1) * 2 + s))
                        act.activation(oT[:, s, :], o_bank[:, :], ACT.Identity, bias=b2h[:, :], scale=0.5).then_inc(o_copied, 1)

            @block.vector
            def _(dve):
                layernorm_scales(None, dve, nc, t, rstd_ready)
                for s in (xn_ready, pairs_ready, we_ready, xo_ready, stat_ready):
                    dve.sem_inc(s, LEAD)
                dve.wait_ge(s_in, 16)
                dve.tensor_scalar(b2h[:, :], b2, 0.5, None, ALU.mult).then_inc(b2h_ready, 1)
                dve.wait_ge(w_in, 32)
                with dve.Fori(0, BATCH) as b:
                    for j in range(BT):
                        if j % 4 == 0:
                            dve.wait_ge(xt_ready, after((b - 1) * 2 + j // 4))
                            if j == 0:
                                dve.wait_ge(pairs_ready, after((b - 1) * 3 + 2))
                        n = b * BT + j
                        dve.tensor_scalar(xn[:, j, :], t.X[:, at(n), :], t.stats[:, at(n), 0], t.rstd[:, at(n)],
                                          ALU.subtract, ALU.mult).then_inc(xn_ready, 1)
                    dve.wait_ge(rows_in, (b + 1) * 32)
                    dve.scalar_tensor_tensor(odds[:, :, :], odd[:, :].unsqueeze(1).to_broadcast([8, KC, DIM]), scale,
                                             first_half.unsqueeze(2).to_broadcast([8, KC, DIM]), ALU.mult, ALU.mult).then_inc(pairs_ready, 1)
                    dve.tensor_scalar(evens[:, :], even[:, :], scale, None, ALU.mult).then_inc(pairs_ready, 1)
                    dve.wait_ge(pairs_ready, after(b * 3 + 1))
                    ev = evens[:, :].rearrange("k (i r) -> k r i", r=4).unsqueeze(2).to_broadcast([8, 4, 4, 32])
                    sh = second_half.unsqueeze(1).unsqueeze(3).to_broadcast([8, 4, 4, 32])
                    dve.tensor_tensor(evenm[:, :, :, :], ev, sh, ALU.mult).then_inc(pairs_ready, 1)
                    for k, (we, w) in enumerate(((w1e, w1), (w2e, w2))):
                        dve.wait_ge(wp_ready, after(b * 2 + k))
                        dve.tensor_tensor(we[:, :], w_bank[:, :], w[:, :], ALU.add).then_inc(we_ready, 1)
                    for s in range(2):
                        dve.wait_ge(ot_ready, after(b * 2 + s))
                        half = bass.ds(b * BT + 4 * s, 4)
                        dve.tensor_tensor(xo[:, s, :, :], x_bank[s][:, :].rearrange("p (j c) -> p j c", c=DIM), t.X[:, half, :],
                                          ALU.add).then_inc(xo_ready, 1)
                        dve.wait_ge(xo_ready, after(b * 2 + s))
                        dve.sem_inc(dve_pause, 1)
                        dve.tensor_copy(t.X[:, half, :], xo[:, s, :, :])
                        for j in range(4):
                            ins = dve.bn_stats(stat6[:, s, j, :], xo[:, s, j, :])
                        ins.then_inc(stat_ready, 1)
                        dve.wait_ge(stat_ready, after(b * 4 + 2 * s))
                        dve.sem_inc(dve_pause, 1)
                        for j in range(4):
                            ins = dve.bn_aggr(aggr[:, s, j, :], stat6[:, s, j, :])
                        ins.then_inc(stat_ready, 1)
                        dve.wait_ge(stat_ready, after(b * 4 + 2 * s + 1))
                        dve.sem_inc(dve_pause, 1)
                        dve.tensor_copy(t.stats[:, half, :], aggr[:, s, :, :])
        sem.clear()


FFN_SMALL = 16


def ffn_laid_out(np, a, r):
    r["w1"] = a["L1_ffn_W1"].T
    r["w2"] = a["L1_ffn_W2"].reshape(DIM, KC, P).transpose(2, 1, 0).reshape(P, INNER)
    small = np.zeros((P, FFN_SMALL), np.float32)
    small[:, 0:4] = a["L1_ffn_b1"].reshape(KC, P).T
    small[:, 4] = a["L1_ffn_b2"]
    small[:, 5] = a["L1_ffn_scale"]
    small[0:4, 8:12] = np.eye(4)
    small[4:8, 12:16] = np.eye(4)
    r["ffn_small"] = small


GW = 3 * P
ROW = 32
SLOPE, SHIFT, DIVISOR = -0.01, 100.0, 1000.0
BOUND = 99.0


def attn0_phase(nc, t, d, tag):
    with ExitStack() as ctx:
        def sb(name, shape, dt=F32):
            return ctx.enter_context(nc.sbuf_tensor(f"{tag}_{name}", shape, dt))

        sem = Semaphores(ctx, nc, tag)

        w32 = sb("w32", [P, GROUPS, GW])
        w = [sb(f"w{i}", [P, GROUPS, GW], F32R) for i in range(2)]
        wp = sb("wp", [P, GROUPS * DIM])
        small = sb("small", [P, A0_SMALL])
        k_low, q_low, q_ones, head_mask = small[:, 0:1], small[:, 1:2], small[:, 2:3], small[:, 4:8]
        first_rows = small[:, 3:4]
        state_mask, kv_ones, seen = small[:, 8:136], small[:, 136:392], small[:, 392:904]
        xn = sb("xn", [P, BT, DIM])
        xT = [sb(f"xT{i}", [P, SEQ], F32R) for i in range(2)]
        low = sb("low", [P, 2, HALF], F32R)
        kS = sb("kS", [P, SEQ], F32R)
        kM = [sb(f"kM{q}", [P, GH, SEQ], F32R) for q in range(2)]
        qS = [sb(f"qS{q}", [P, SEQ], F32R) for q in range(2)]
        KV = [sb(f"KV{q}", [P, BT, 2 * P]) for q in range(2)]
        run = sb("run", [P, BT, P])
        runm = sb("runm", [P, BT, P])
        runl = sb("runl", [P, BT, P], F32R)
        S = [sb(f"S{q}", [P, BT, P], F32R) for q in range(2)]
        R = sb("R", [P, 2, GH, HALF])
        L = sb("L", [P, 2, GH, HALF])
        yS = sb("yS", [P, GROUPS, SEQ])
        bound = sb("bound", [P, 2, 3])
        peak = sb("peak", [1, 2])
        flag = sb("flag", [1, 2], mybir.dt.int32)
        res = ResidualAdd(ctx, nc, sem, t, tag, 4)
        ps = [ctx.enter_context(nc.psum_tensor(f"{tag}_ps{i}", [P, HALF], F32)) for i in range(8)]
        e_bank, a_bank, y_bank, x_bank = ps[0:4], ps[4:6], ps[6], ps[7]

        w_in, w_high, w_low, rstd_ready, zero_ready = sem("w_in"), sem("w_high"), sem("w_low"), sem("rstd_ready"), sem("zero_ready")
        xn_ready, xt_ready, xh_ready, xl_ready = sem("xn_ready"), sem("xt_ready"), sem("xh_ready"), sem("xl_ready")
        ap_ready, t_ready, av_ready, run_ready = sem("ap_ready"), sem("t_ready"), sem("av_ready"), sem("run_ready")
        km_ready, runm_ready, runl_ready, S_ready = sem("km_ready"), sem("runm_ready"), sem("runl_ready"), sem("S_ready")
        s_ready, r_ready, u_ready, l_ready, g_ready = (
            sem("s_ready"), sem("r_ready"), sem("u_ready"), sem("l_ready"), sem("g_ready"))
        pv_ready, y_ready, yc_ready, o_ready = sem("pv_ready"), sem("y_ready"), sem("yc_ready"), sem("o_ready")
        pe_pause, act_pause, dve_pause, pool_pause = sem("pe_pause"), sem("act_pause"), sem("vector_pause"), sem("pool_pause")
        bound_ready, peak_ready, top_ready, flag_ready = sem("bound_ready"), sem("peak_ready"), sem("top_ready"), sem("flag_ready")
        cs_ready, cl_ready, cm_ready, cc_ready, cv_ready, cy_ready = (
            sem("cs_ready"), sem("cl_ready"), sem("cm_ready"), sem("cc_ready"), sem("cv_ready"), sem("cy_ready"))

        units = [(s, u) for s in range(2) for u in key_units(s)]
        NU, NQ0 = len(units), len(key_units(0))
        US = NU * GH
        PRODUCTS = ((0, 0), (1, 0), (0, 1))
        PREP = [("k", 0), ("k", 1), ("kv", 0), ("kv", 1), ("kv", 2), ("kv", 3), ("q", 0), ("q", 1), ("run", 0), ("run", 1)]
        KMASKS = (4, 5, 8, 9)
        LOWS = {0: 0, 1: 1, 6: 2, 7: 3}

        def width(u):
            pieces = units[u][1]
            return pieces[0][3] if len(pieces) == 1 else HALF

        def correct(eng, pause, m, q, body, totals):
            eng.wait_ge(flag_ready, after(m))
            eng.sem_inc(pause, 1)
            may_be_low = eng.value_load(flag[0:1, q:q + 1], min_val=0, max_val=1)
            with eng.If(may_be_low):
                nc.disable_value_cache = True
                body()
                nc.disable_value_cache = False
            with eng.Else():
                for s, n in totals:
                    eng.sem_inc(s, n)

        def pipeline(eng, open_element, prepare, attend, finish):
            def element(b, more):
                for g in range(GROUPS):
                    m, has_next = b * GROUPS + g, more or g + 1 < GROUPS
                    nxt = (lambda k: prepare(m + 1, (g + 1) % GROUPS, k)) if has_next else (lambda k: None)
                    attend(m, g, nxt, b, more)
                finish(b, more)

            open_element(0)
            for k in range(NU):
                prepare(0, 0, k)
            with eng.Fori(0, BATCH - 1) as b:
                element(b, True)
            element(BATCH - 1, False)

        with nc.Block() as block:
            @block.sync
            def _(sp):
                sp.dma_start(w32[:, :, :], d["wqkv"].rearrange("p (g n) -> p g n", g=GROUPS)).then_inc(w_in, 16)
                sp.dma_start(wp[:, :], d["wproj"]).then_inc(w_in, 16)
                sp.dma_start(small[:, :], d["attn0_small"]).then_inc(w_in, 16)

            @block.gpsimd
            def _(pool):
                for s in (runm_ready, runl_ready, S_ready, g_ready):
                    pool.sem_inc(s, LEAD)
                pool.memset(run[:, 0, :], 0.0).then_inc(zero_ready, 1)
                pool.wait_ge(w_in, 48)

                def prepare(m, g, k):
                    q = g % 2
                    if k == NU - 1:
                        pool.wait_ge(av_ready, after(m * NU + NU - 1))
                        pool.wait_ge(y_ready, after((m - 1) * 2 - 1))
                        pool.tensor_tensor(runm[:, :, :], run[:, :, :], state_mask.unsqueeze(1).to_broadcast([P, BT, P]),
                                           ALU.mult).then_inc(runm_ready, 1)
                        pool.wait_ge(runm_ready, after(m))
                        pool.sem_inc(pool_pause, 1)
                        pool.tensor_tensor(runl[:, :, :], runm[:, :, :], k_low.unsqueeze(2).to_broadcast([P, BT, P]),
                                           ALU.mult).then_inc(runl_ready, 1)
                        pool.wait_ge(runl_ready, after(m))
                        pool.tensor_tensor(S[q][:, :, :], runm[:, :, :], f32(runl[:, :, :]), ALU.subtract).then_inc(S_ready, 1)

                def attend(m, g, nxt, b, more):
                    for u in range(NU):
                        if units[u][1][0][4]:
                            s = units[u][0]
                            for j in range(GH):
                                n = m * 2 * GH + (GH if u else 0) + j
                                pool.wait_ge(l_ready, after(n))
                                pool.tensor_tensor(L[:, s, j, :], L[:, s, j, :], seen, ALU.mult).then_inc(g_ready, 1)
                        nxt(u)

                pipeline(pool, lambda b: None, prepare, attend, lambda b, more: None)

            @block.tensor
            def _(pe):
                for s in (xt_ready, ap_ready, s_ready, pv_ready, y_ready, o_ready, peak_ready, cs_ready, cv_ready):
                    pe.sem_inc(s, LEAD)
                pe.wait_ge(w_in, 48)
                pe.wait_ge(w_low, 1)

                def open_element(b):
                    pe.wait_ge(av_ready, after(b * GROUPS * NU - 1))
                    for s in range(2):
                        pe.wait_ge(xn_ready, after(b * BT + 4 * s + 3))
                        for j in range(4):
                            last = pe.transpose(a_bank[s][:, j * P:(j + 1) * P], xn[:, 4 * s + j, :], t.ident)
                        last.then_inc(xt_ready, 1)
                    if isinstance(b, int):
                        pe.wait_ge(xl_ready, after(1))

                def prepare(m, g, k):
                    q = g % 2
                    kind, i = PREP[k]
                    bank = a_bank[k % 2]
                    pe.wait_ge(av_ready, after(m * NU + k - 2))
                    if kind in "kq":
                        off = P if kind == "k" else 0
                        for n, (a, b_) in enumerate(PRODUCTS):
                            last = pe.matmul(bank[:, :], w[b_][:, g, off:off + P], xT[a][:, i * HALF:(i + 1) * HALF],
                                             start=n == 0, stop=n == 2)
                    elif kind == "kv":
                        for h in range(2):
                            j = 2 * i + h
                            for n, (a, b_) in enumerate(PRODUCTS):
                                last = pe.matmul(bank[:, h * 2 * P:(h + 1) * 2 * P], xT[a][:, j * P:(j + 1) * P], w[b_][:, g, P:GW],
                                                 start=n == 0, stop=n == 2)
                    else:
                        pe.wait_ge(av_ready, after(m * NU + 5))
                        if i == 0:
                            pe.wait_ge(bound_ready, after(m * 3 + 2))
                            pe.wait_ge(flag_ready, after(m - 1))
                            pe.matmul(x_bank[0:1, 0:GH], bound[:, q, 2:3], head_mask, start=True, stop=True).then_inc(peak_ready, 1)
                        for h in range(4 if i == 0 else 3):
                            j = 4 * i + h
                            last = pe.matmul(bank[:, h * P:(h + 1) * P], KV[q][:, j, 0:P], KV[q][:, j, P:2 * P], start=True, stop=True)
                    last.then_inc(ap_ready, 1)

                def scores(m, g, u):
                    q = g % 2
                    s, pieces = units[u]
                    for j in range(GH):
                        pe.wait_ge(r_ready, after(m * US + (u - 1) * GH + j))
                        diagonal = pieces[0][4]
                        for k, (kt, at_, qc, n, _) in enumerate(pieces):
                            last = pe.matmul(e_bank[j][:, at_:at_ + n], kM[q][:, j, kt * P:(kt + 1) * P],
                                             qS[q][:, s * HALF + qc:s * HALF + qc + n], start=not diagonal or k == 0,
                                             stop=not diagonal, skip_group_check=diagonal)
                        if diagonal:
                            last = pe.matmul(e_bank[j][:, :], t.identb, t.neg_kq, start=False, stop=True, skip_group_check=True)
                        last.then_inc(s_ready, 1)

                def values(m, g, u):
                    q = g % 2
                    s, pieces = units[u]
                    first, end = u in (0, NQ0), u in (NQ0 - 1, NU - 1)
                    if first:
                        pe.wait_ge(yc_ready, after(m * 2 + s - 1))
                    pe.wait_ge(u_ready, after(m * US + u * GH + GH - 1))
                    for k, (kt, at_, qc, n, diagonal) in enumerate(pieces):
                        for j in range(GH):
                            rows = slice(j * ROW, (j + 1) * ROW)
                            last = pe.matmul(y_bank[rows, qc:qc + n], KV[q][:, kt, P + j * ROW:P + (j + 1) * ROW],
                                             R[:, u % 2, j, at_:at_ + n], start=first and k == 0, stop=False, skip_group_check=True)
                    last.then_inc(pv_ready, 1)
                    if end:
                        pe.wait_ge(g_ready, after((m * 2 + s) * GH + GH - 1))
                        for kt, at_, qc, n, _ in key_units(s)[0]:
                            for j in range(GH):
                                rows = slice(j * ROW, (j + 1) * ROW)
                                pe.matmul(y_bank[rows, qc:qc + n], KV[q][:, kt, P + j * ROW:P + (j + 1) * ROW],
                                          L[:, s, j, at_:at_ + n], start=False, stop=False, skip_group_check=True)
                        pe.wait_ge(S_ready, after(m))
                        chunks = [c for c in range(4 * s, 4 * s + 4) if c]
                        for c in chunks:
                            last = pe.matmul(y_bank[:, (c % 4) * P:(c % 4 + 1) * P], S[q][:, c, :], qS[q][:, c * P:(c + 1) * P],
                                             start=False, stop=c == chunks[-1], skip_group_check=True)
                        last.then_inc(y_ready, 1)

                def attend(m, g, nxt, b, more):
                    pe.wait_ge(km_ready, after(m * GH + GH - 1))
                    pe.wait_ge(av_ready, after(m * NU + NU - 1))
                    for u in range(NU):
                        scores(m, g, u)
                        if u == 0 and g == GROUPS - 1 and more:
                            pe.wait_ge(xl_ready, after(b * 2 + 3))
                        if u == 0 and g == 0:
                            pe.wait_ge(res.xo_ready, after(b * 2 - 1))
                        nxt(u)
                        if u >= 1:
                            values(m, g, u - 1)
                    if more and g == GROUPS - 2:
                        open_element(b + 1)
                    values(m, g, NU - 1)
                    correct(pe, pe_pause, m, g % 2, lambda: low_scores(m, g), ((cs_ready, US), (cv_ready, NU)))

                def low_scores(m, g):
                    q = g % 2
                    for u in range(NU):
                        s, pieces = units[u]
                        for j in range(GH):
                            pe.wait_ge(cc_ready, after(m * US + (u - 1) * GH + j))
                            for kt, at_, qc, n, _ in pieces:
                                last = pe.matmul(e_bank[j][:, at_:at_ + n], kM[q][:, j, kt * P:(kt + 1) * P],
                                                 qS[q][:, s * HALF + qc:s * HALF + qc + n], start=True, stop=True)
                            last.then_inc(cs_ready, 1)
                        if u == 0:
                            pe.wait_ge(yc_ready, after(m * 2 + 1))
                        if u == NQ0:
                            pe.wait_ge(cy_ready, after(m * 2))
                        pe.wait_ge(cc_ready, after(m * US + u * GH + GH - 1))
                        for k, (kt, at_, qc, n, _) in enumerate(pieces):
                            for j in range(GH):
                                rows = slice(j * ROW, (j + 1) * ROW)
                                last = pe.matmul(y_bank[rows, qc:qc + n], KV[q][:, kt, P + j * ROW:P + (j + 1) * ROW],
                                                 R[:, 0, j, at_:at_ + n], start=u in (0, NQ0) and k == 0,
                                                 stop=u in (NQ0 - 1, NU - 1), skip_group_check=True)
                        last.then_inc(cv_ready, 1)
                    pe.wait_ge(cy_ready, after(m * 2 + 1))

                def finish(b, more):
                    pe.wait_ge(yc_ready, after((b + 1) * GROUPS * 2 - 1))
                    pe.wait_ge(cy_ready, after((b + 1) * GROUPS * 2 - 1))
                    pe.wait_ge(av_ready, after((b + 1) * GROUPS * NU + (NU - 1 if more else -1)))
                    for s in range(2):
                        for j in range(4):
                            for g in range(GROUPS):
                                c = s * HALF + j * P
                                last = pe.matmul(a_bank[s][:, j * P:(j + 1) * P], yS[:, g, c:c + P], wp[:, g * DIM:(g + 1) * DIM],
                                                 start=g == 0, stop=g == GROUPS - 1)
                        last.then_inc(o_ready, 1)

                pipeline(pe, open_element, prepare, attend, finish)

            @block.scalar
            def _(act):
                layernorm_scales(act, None, nc, t, rstd_ready)
                for s in (xh_ready, t_ready, r_ready, l_ready, km_ready, yc_ready, cl_ready):
                    act.sem_inc(s, LEAD)
                act.wait_ge(w_in, 48)
                act.activation(w[0][:, :, 0:P], w32[:, :, 0:P], ACT.Copy, scale=SCORE_SCALE)
                act.activation(w[0][:, :, P:GW], w32[:, :, P:GW], ACT.Copy).then_inc(w_high, 1)

                def open_element(b):
                    for s in range(2):
                        act.wait_ge(xt_ready, after(b * 2 + s))
                        act.wait_ge(ap_ready, after(b * GROUPS * NU - 1))
                        act.activation(xT[0][:, s * HALF:(s + 1) * HALF], a_bank[s][:, :], ACT.Copy).then_inc(xh_ready, 1)

                def prepare(m, g, k):
                    if k in LOWS:
                        act.wait_ge(ap_ready, after(m * NU + k))
                        act.wait_ge(av_ready, after(m * NU + k - 2))
                        act.activation(low[:, k % 2, :], a_bank[k % 2][:, :], ACT.Copy,
                                       scale=k_low if PREP[k][0] == "k" else q_low).then_inc(t_ready, 1)
                    if k in KMASKS:
                        j = KMASKS.index(k)
                        if j == 0:
                            act.wait_ge(av_ready, after(m * NU + 1))
                            act.wait_ge(s_ready, after((m - 1) * US - 1))
                        act.activation(kM[g % 2][:, j, :], f32(kS[:, :]), ACT.Copy, scale=head_mask[:, j:j + 1]).then_inc(km_ready, 1)

                def copy_out(m, g, s):
                    act.wait_ge(y_ready, after(m * 2 + s))
                    act.activation(yS[:, g, s * HALF:(s + 1) * HALF], y_bank[:, :], ACT.Copy, scale=1.0 / DIVISOR).then_inc(yc_ready, 1)

                def attend(m, g, nxt, b, more):
                    for u in range(NU):
                        pieces, n = units[u][1], width(u)
                        for j in range(GH):
                            act.wait_ge(s_ready, after(m * US + u * GH + j))
                            if j == 0:
                                act.wait_ge(pv_ready, after(m * NU + u - 2))
                            if pieces[0][4]:
                                if j == 0:
                                    act.wait_ge(y_ready, after((m - 1) * 2 + units[u][0]))
                                act.activation(L[:, units[u][0], j, :], e_bank[j][:, :], ACT.Copy, bias=1.0, scale=SLOPE).then_inc(l_ready, 1)
                            act.activation(R[:, u % 2, j, HALF - n:HALF], e_bank[j][:, HALF - n:HALF], ACT.Relu).then_inc(r_ready, 1)
                        nxt(u)
                        if u == NQ0:
                            copy_out(m, g, 0)
                    if more and g == GROUPS - 2:
                        open_element(b + 1)
                    copy_out(m, g, 1)
                    correct(act, act_pause, m, g % 2, lambda: low_terms(m), ((cl_ready, US),))

                def low_terms(m):
                    for u in range(NU):
                        n = width(u)
                        for j in range(GH):
                            act.wait_ge(cs_ready, after(m * US + u * GH + j))
                            act.wait_ge(cc_ready, after(m * US + (u - 1) * GH + j))
                            act.activation(L[:, 0, j, HALF - n:HALF], e_bank[j][:, HALF - n:HALF], ACT.Copy, bias=-1.0,
                                           scale=-SLOPE).then_inc(cl_ready, 1)

                pipeline(act, open_element, prepare, attend, lambda b, more: None)

            @block.vector
            def _(dve):
                layernorm_scales(None, dve, nc, t, rstd_ready)
                for s in (xn_ready, xl_ready, av_ready, run_ready, u_ready, bound_ready, top_ready,
                          flag_ready, cm_ready, cc_ready, cy_ready):
                    dve.sem_inc(s, LEAD)
                res.prime(dve)
                dve.wait_ge(w_high, 1)
                dve.wait_ge(zero_ready, 1)
                dve.scalar_tensor_tensor(w[1][:, :, 0:P], w32[:, :, 0:P], SCORE_SCALE, f32(w[0][:, :, 0:P]), ALU.mult, ALU.subtract)
                dve.tensor_tensor(w[1][:, :, P:GW], w32[:, :, P:GW], f32(w[0][:, :, P:GW]), ALU.subtract).then_inc(w_low, 1)

                def normalise(b):
                    for j in range(BT):
                        if j % 4 == 0:
                            dve.wait_ge(xt_ready, after((b - 1) * 2 + j // 4))
                        n = b * BT + j
                        dve.tensor_scalar(xn[:, j, :], t.X[:, at(n), :], t.stats[:, at(n), 0], t.rstd[:, at(n)],
                                          ALU.subtract, ALU.mult).then_inc(xn_ready, 1)

                def open_element(b):
                    for s in range(2):
                        half = slice(s * HALF, (s + 1) * HALF)
                        dve.wait_ge(xh_ready, after(b * 2 + s))
                        dve.tensor_tensor(xT[1][:, half], a_bank[s][:, :], f32(xT[0][:, half]), ALU.subtract).then_inc(xl_ready, 1)

                def prepare(m, g, k):
                    q = g % 2
                    kind, i = PREP[k]
                    bank = a_bank[k % 2]
                    half = slice(i * HALF, (i + 1) * HALF)
                    if k in LOWS:
                        dve.wait_ge(t_ready, after(m * 4 + LOWS[k]))
                    else:
                        dve.wait_ge(ap_ready, after(m * NU + k))
                    if kind == "k":
                        dve.wait_ge(km_ready, after(m * GH - 1))
                        ins = dve.tensor_tensor(kS[:, half], bank[:, :], f32(low[:, k % 2, :]), ALU.subtract)
                    elif kind == "q":
                        dve.wait_ge(y_ready, after((m - 1) * 2 - 1))
                        ins = dve.scalar_tensor_tensor(qS[q][:, half], bank[:, :], q_ones, f32(low[:, k % 2, :]), ALU.add, ALU.subtract)
                    elif kind == "kv":
                        dve.wait_ge(y_ready, after((m - 1) * 2 - 1))
                        ins = dve.tensor_tensor(KV[q][:, 2 * i:2 * i + 2, :], bank[:, :].rearrange("p (j n) -> p j n", n=2 * P),
                                                kv_ones.unsqueeze(1).to_broadcast([P, 2, 2 * P]), ALU.add)
                    else:
                        dve.wait_ge(runm_ready, after(m - 1))
                        for h in range(4 if i == 0 else 3):
                            c = 4 * i + h
                            if c == 4:
                                dve.wait_ge(av_ready, after(m * NU + k - 1))
                            elif c:
                                dve.wait_ge(run_ready, after(m * 5 + c - 1 - (c > 4)))
                            ins = dve.tensor_tensor(run[:, c + 1, :], bank[:, h * P:(h + 1) * P], run[:, c, :], ALU.add)
                            if h != (3 if i == 0 else 2):
                                ins.then_inc(run_ready, 1)
                    ins.then_inc(av_ready, 1)
                    if k in (1, 7):
                        dve.wait_ge(av_ready, after(m * NU + k))
                        c = (k == 7) * 1
                        dve.reduce_max(bound[:, q, c:c + 1], f32((qS[q] if c else kS)[:, :]), AX.X,
                                       apply_absolute_value=True).then_inc(bound_ready, 1)
                    if k == 7:
                        dve.wait_ge(bound_ready, after(m * 3 + 1))
                        dve.scalar_tensor_tensor(bound[:, q, 2:3], bound[:, q, 0:1], bound[:, q, 1:2], first_rows,
                                                 ALU.mult, ALU.mult).then_inc(bound_ready, 1)
                    if k == NU - 1:
                        dve.wait_ge(peak_ready, after(m))
                        dve.reduce_max(peak[:, q:q + 1], x_bank[0:1, 0:GH], AX.X).then_inc(top_ready, 1)
                        dve.wait_ge(top_ready, after(m))
                        dve.tensor_scalar(flag[:, q:q + 1], peak[:, q:q + 1], BOUND, None, ALU.is_ge).then_inc(flag_ready, 1)

                def attend(m, g, nxt, b, more):
                    for u in range(NU):
                        pieces, n = units[u][1], width(u)
                        for j in range(GH):
                            dve.wait_ge(r_ready, after(m * US + u * GH + j))
                            r = R[:, u % 2, j, HALF - n:HALF]
                            dve.scalar_tensor_tensor(r, r, -SLOPE, r, ALU.add, ALU.mult).then_inc(u_ready, 1)
                        nxt(u)
                        if more and g == GROUPS - 2 and u == NQ0:
                            normalise(b + 1)
                    if more and g == GROUPS - 2:
                        open_element(b + 1)
                    correct(dve, dve_pause, m, g % 2, lambda: low_weights(m, g), ((cc_ready, US), (cm_ready, 2 * GH), (cy_ready, 2)))

                def low_weights(m, g):
                    for u in range(NU):
                        n = width(u)
                        for j in range(GH):
                            dve.wait_ge(cl_ready, after(m * US + u * GH + j))
                            if j == 0:
                                dve.wait_ge(cv_ready, after(m * NU + u - 1))
                            c = R[:, 0, j, HALF - n:HALF]
                            ins = dve.scalar_tensor_tensor(c, e_bank[j][:, HALF - n:HALF], -SHIFT, L[:, 0, j, HALF - n:HALF],
                                                           ALU.is_lt, ALU.mult)
                            if units[u][1][0][4]:
                                ins.then_inc(cm_ready, 1)
                                dve.wait_ge(cm_ready, after(m * 2 * GH + (GH if u else 0) + j))
                                ins = dve.tensor_tensor(c, c, seen, ALU.mult)
                            ins.then_inc(cc_ready, 1)
                        if u in (NQ0 - 1, NU - 1):
                            s = units[u][0]
                            dve.wait_ge(cv_ready, after(m * NU + u))
                            y = yS[:, g, s * HALF:(s + 1) * HALF]
                            dve.scalar_tensor_tensor(y, y_bank[:, :], 1.0 / DIVISOR, y, ALU.mult, ALU.add).then_inc(cy_ready, 1)

                def finish(b, more):
                    for s in range(2):
                        dve.wait_ge(o_ready, after(b * 2 + s))
                        res.add(dve, b * 2 + s, s, b * BT + 4 * s, a_bank[s][:, :])

                normalise(0)
                pipeline(dve, open_element, prepare, attend, finish)
        sem.clear()


A0_SMALL = 904


def attn0_laid_out(np, a, r):
    wqkv = a["L0_attn_W_attn"].reshape(DIM, 3, GROUPS, GH, HD)
    w = np.zeros((DIM, GROUPS, 3, GH, ROW), np.float32)
    for part in range(3):
        w[:, :, 0:2, :, part * HD:(part + 1) * HD] = wqkv[:, 0:2].transpose(0, 2, 1, 3, 4)
    w[:, :, 2, :, 0:HD] = wqkv[:, 2]
    r["wqkv"] = w.reshape(P, GROUPS * GW)
    wp = np.zeros((GROUPS, GH, ROW, DIM), np.float32)
    wp[:, :, 0:HD] = a["L0_attn_W_proj"].reshape(GROUPS, GH, HD, DIM)
    r["wproj"] = wp.transpose(1, 2, 0, 3).reshape(P, GROUPS * DIM)
    row, col = np.arange(P) % ROW, np.arange(P)
    small = np.zeros((P, A0_SMALL), np.float32)
    small[:, 0] = ((row >= HD) & (row < 2 * HD)) | (row == 25)
    small[:, 1] = (row >= 2 * HD) & (row < 3 * HD)
    small[:, 2] = (row == 24) | (row == 25)
    small[:, 3] = row < HD
    small[:, 4:8] = np.arange(P)[:, None] // ROW == np.arange(GH)
    same = (np.arange(P)[:, None] // ROW) == (col[None, :] // ROW)
    small[:, 8:136] = same * np.where(row < 24, SLOPE, 1.0)[:, None]
    small[:, 136:264] = ((row == 24) | (row == 25))[None, :]
    small[:, 392:904] = np.tile(np.triu(np.ones((P, P))), (1, 4))
    r["attn0_small"] = small


PAIRS = HEADS // 2
STACK = 3 * LAT
KROWS = STACK + 2
ZW = 5 * P
VW = 64
L1_COLS = 2 * LAT + 8 + 4 * HEADS


def key_units(s):
    k = 4 * s
    diagonal = [(k + i, i * P, i * P, P, True) for i in range(4)]
    split = [(k, P, P, 3 * P, False), (k + 2, 0, 3 * P, P, False)]
    half = [(k + 1, 2 * P, 2 * P, 2 * P, False)]
    return [diagonal, split, half] + [[(i, 0, 0, HALF, False)] for i in range(k)]


def attn1_phase(nc, t, d, tag):
    with ExitStack() as ctx:
        def sb(name, shape, dt=F32):
            return ctx.enter_context(nc.sbuf_tensor(f"{tag}_{name}", shape, dt))

        sem = Semaphores(ctx, nc, tag)

        wd32 = sb("wd32", [P, HEADS * STACK])
        wd = [sb(f"wd{i}", [P, HEADS * STACK], F32R) for i in range(2)]
        lat32 = sb("lat32", [P, STACK])
        lat = [sb(f"lat{i}", [P, STACK], F32R) for i in range(2)]
        wo = sb("wo", [P, ZW])
        cols = sb("cols", [P, L1_COLS])
        v_bias, k_bias, k_low, q_low = cols[:, 0:LAT], cols[0:STACK, 36:37], cols[0:STACK, 37:38], cols[0:STACK, 38:39]
        q_bias = cols[0:STACK, 40:40 + HEADS]
        k_lbias = sb("k_lbias", [STACK, 1])
        qb_low = sb("qb_low", [STACK, HEADS])
        xn = sb("xn", [P, BT, DIM])
        xT = [sb(f"xT{i}", [P, SEQ], F32R) for i in range(2)]
        kT = sb("kT", [STACK, 2, HALF], F32R)
        kS = sb("kS", [KROWS, SEQ], F32R)
        V = sb("V", [P, BT, VW])
        kN = sb("kN", [STACK, SEQ], F32R)
        VN = sb("VN", [P, BT, LAT])
        wcur = sb("wcur", [P, 2, 2 * STACK], F32R)
        bcur = sb("bcur", [STACK, 2, 2])
        qT = sb("qT", [STACK, 2, HALF], F32R)
        qS = [[sb(f"qS{q}{c}", [KROWS, SEQ], F32R) for c in range(2)] for q in range(2)]
        mx = sb("mx", [P, 2, 16])
        mh = sb("mh", [16, 2, P], F32R)
        ml = sb("ml", [16, 2, P], F32R)
        probs = sb("probs", [P, 2, 2, HALF])
        yT = sb("yT", [P, PAIRS, SEQ])
        rcp = sb("rcp", [P, 2, HEADS])
        z = sb("z", [P, 2, ZW])
        zT = sb("zT", [P, 2, ZW])
        res = ResidualAdd(ctx, nc, sem, t, tag, 1)
        m_all = ctx.enter_context(nc.psum_tensor(f"{tag}_psm", [P, 4 * HALF], F32))
        m_bank = [m_all[:, i * HALF:(i + 1) * HALF] for i in range(4)]
        e_bank = [ctx.enter_context(nc.psum_tensor(f"{tag}_pse{i}", [P, HALF], F32)) for i in range(2)]
        y_bank = ctx.enter_context(nc.psum_tensor(f"{tag}_psy", [P, HALF], F32))
        o_bank = ctx.enter_context(nc.psum_tensor(f"{tag}_pso", [P, HALF], F32))

        w_in, k_in, w_high, w_low, rstd_ready = sem("w_in"), sem("k_in"), sem("w_high"), sem("w_low"), sem("rstd_ready")
        minus = sb("minus", [2, SEQ], F32R)
        const_ready, minus_ready = sem("const_ready"), sem("minus_ready")
        xn_ready, xt_ready, xh_ready, xl_ready = sem("xn_ready"), sem("xt_ready"), sem("xh_ready"), sem("xl_ready")
        kp_ready, kt_ready, ks_ready, vp_ready, v_ready = (
            sem("kp_ready"), sem("kt_ready"), sem("ks_ready"), sem("vp_ready"), sem("v_ready"))
        wq_ready, qp_ready, qt_ready, qs_ready = sem("wq_ready"), sem("qp_ready"), sem("qt_ready"), sem("qs_ready")
        sm_ready, mx_ready, mt_ready, mh_ready, ml_ready, m_in = (
            sem("sm_ready"), sem("mx_ready"), sem("mt_ready"), sem("mh_ready"), sem("ml_ready"), sem("m_in"))
        s_ready, p_ready, pv_ready, y_ready, yc_ready = (
            sem("s_ready"), sem("p_ready"), sem("pv_ready"), sem("y_ready"), sem("yc_ready"))
        zt_ready, r_ready, z_ready, zz_ready, zc_ready, o_ready = (
            sem("zt_ready"), sem("r_ready"), sem("z_ready"), sem("zz_ready"), sem("zc_ready"), sem("o_ready"))
        kc_ready, pool_pause = sem("kc_ready"), sem("pool_pause")

        units = [(s, u) for s in range(2) for u in key_units(s)]
        NU = len(units)
        NQ0 = len(key_units(0))
        PRODUCTS = ((0, 0), (1, 0), (0, 1))

        def pipeline(eng, start, pair, finish):
            def element(b, more):
                with eng.Fori(0, PAIRS // 2 - 1) as i:
                    for q in range(2):
                        pair(b * PAIRS + i * 2 + q, q, i * 2 + q, b, (True, True))
                pair(b * PAIRS + PAIRS - 2, 0, PAIRS - 2, b, (True, more))
                pair(b * PAIRS + PAIRS - 1, 1, PAIRS - 1, b, (more, more))
                finish(b, more)

            start()
            with eng.Fori(0, BATCH - 1) as b:
                element(b, True)
            element(BATCH - 1, False)

        def opens(i, ahead):
            return isinstance(i, int) and i == PAIRS - 2 and ahead[1]

        MAXIMA = (range(0, 4), range(4, 6), range(6, 7), range(7, 9), range(9, 12), range(12, 14), range(14, 16))

        with nc.Block() as block:
            @block.sync
            def _(sp):
                sp.dma_start(wd32[:, :], d["wd"]).then_inc(w_in, 16)
                sp.dma_start(lat32[:, :], d["latent"]).then_inc(w_in, 16)
                sp.dma_start(wo[:, :], d["wo"]).then_inc(w_in, 16)
                sp.dma_start(cols[:, :], d["attn1_small"]).then_inc(w_in, 16)
                sp.wait_ge(minus_ready, 1)
                sp.dma_start(f32(kS[STACK:KROWS, :]), f32(minus[:, :])).then_inc(k_in, 16)

                def maxima(m, q):
                    sp.wait_ge(ml_ready, after(m))
                    for c in range(2):
                        sp.dma_start(f32(qS[q][c][STACK:STACK + 1, :]), f32(mh[8 * c:8 * c + 8, q, :])).then_inc(m_in, 16)
                        sp.dma_start(f32(qS[q][c][STACK + 1:STACK + 2, :]), f32(ml[8 * c:8 * c + 8, q, :])).then_inc(m_in, 16)

                def pair(m, q, i, b, ahead):
                    if ahead[0]:
                        maxima(m + 1, 1 - q)

                pipeline(sp, lambda: maxima(0, 0), pair, lambda b, more: None)

            @block.gpsimd
            def _(pool):
                for s in (wq_ready, kc_ready):
                    pool.sem_inc(s, LEAD)
                pool.memset(V[:, :, LAT:VW], 0.0)
                pool.memset(z[:, :, HEADS * LAT:ZW], 0.0).then_inc(const_ready, 1)
                pool.wait_ge(const_ready, 1)
                pool.memset(V[:, :, LAT:LAT + 1], 1.0)
                pool.memset(z[:, :, HEADS * LAT:HEADS * LAT + 1], 1.0).then_inc(const_ready, 1)
                pool.wait_ge(w_low, 2)

                def weights(m, i):
                    pool.wait_ge(qs_ready, after(m * 4 - 1))
                    pool.sem_inc(pool_pause, 1)
                    for k in range(2):
                        pool.tensor_copy(wcur[:, k, :], wd[k][:, bass.ds(i * 2 * STACK, 2 * STACK)])
                    pool.tensor_copy(bcur[:, 0, :], q_bias[:, bass.ds(i * 2, 2)])
                    pool.tensor_copy(bcur[:, 1, :], qb_low[:, bass.ds(i * 2, 2)]).then_inc(wq_ready, 1)

                def take_over(b):
                    pool.wait_ge(ks_ready, after(b * 2 + 1))
                    pool.wait_ge(v_ready, after(b))
                    pool.wait_ge(s_ready, after(b * PAIRS * 2 * NU - 1))
                    pool.wait_ge(y_ready, after(b * PAIRS * 2 - 1))
                    pool.sem_inc(pool_pause, 1)
                    pool.tensor_copy(kS[0:STACK, :], kN[:, :])
                    pool.tensor_copy(V[:, :, 0:LAT], VN[:, :, :]).then_inc(kc_ready, 1)

                def start():
                    weights(0, 0)
                    weights(1, 1)
                    take_over(0)

                def pair(m, q, i, b, ahead):
                    if ahead[1]:
                        weights(m + 2, (i + 2) % PAIRS if isinstance(i, int) else i + 2)

                pipeline(pool, start, pair, lambda b, more: take_over(b + 1) if more else None)

            @block.tensor
            def _(pe):
                for s in (xt_ready, kp_ready, vp_ready, qp_ready, sm_ready, mt_ready, s_ready, pv_ready, y_ready,
                          zt_ready, zz_ready, o_ready):
                    pe.sem_inc(s, LEAD)
                pe.wait_ge(w_in, 64)
                pe.wait_ge(w_low, 2)
                pe.wait_ge(k_in, 16)
                pe.wait_ge(const_ready, 2)

                def transpose_x(b):
                    for s in range(2):
                        pe.wait_ge(xn_ready, after(b * BT + 4 * s + 3))
                        pe.wait_ge(mx_ready, after(b * PAIRS * 16 - 1))
                        for j in range(4):
                            last = pe.transpose(m_bank[s][:, j * P:(j + 1) * P], xn[:, 4 * s + j, :], t.ident)
                        last.then_inc(xt_ready, 1)

                def latents(b):
                    for s in range(2):
                        pe.wait_ge(xl_ready, after(b * 2 + s))
                        for k, (a, w) in enumerate(PRODUCTS):
                            last = pe.matmul(m_bank[2 + s][0:STACK, :], lat[w][:, :], xT[a][:, s * HALF:(s + 1) * HALF],
                                             start=k == 0, stop=k == 2)
                        last.then_inc(kp_ready, 1)

                def latent_rows(b):
                    pe.wait_ge(ml_ready, after(b * PAIRS - 1))
                    for j in range(BT):
                        for k, (a, w) in enumerate(PRODUCTS):
                            last = pe.matmul(o_bank[:, j * VW:j * VW + LAT], xT[a][:, j * P:(j + 1) * P], lat[w][:, 0:LAT],
                                             start=k == 0, stop=k == 2)
                    last.then_inc(vp_ready, 1)
                    pe.wait_ge(ks_ready, after(b * 2 + 1))

                def project(m, c):
                    pe.wait_ge(wq_ready, after(m))
                    pe.wait_ge(mx_ready, after((m - 1) * 16 + 15))
                    for s in range(2):
                        for k, (a, w) in enumerate(PRODUCTS):
                            last = pe.matmul(m_bank[2 * c + s][0:STACK, :], wcur[:, w, c * STACK:(c + 1) * STACK],
                                             xT[a][:, s * HALF:(s + 1) * HALF], start=k == 0, stop=k == 2)
                        last.then_inc(qp_ready, 1)

                def scores_max(m, q, v, keys):
                    c, j = v // 8, v % 8
                    if v < 2:
                        pe.wait_ge(qs_ready, after(m * 4 + 1 + 2 * v))
                    else:
                        pe.wait_ge(mx_ready, after(m * 16 + v - 2))
                    base = (v % 2) * 2 * HALF
                    for lo in range(0, (j + 1) * P, HALF):
                        hi = min(lo + HALF, (j + 1) * P)
                        pe.matmul(m_all[:, base + lo:base + hi], qS[q][c][0:STACK, j * P:(j + 1) * P], keys[0:STACK, lo:hi],
                                  start=True, stop=hi < (j + 1) * P)
                    pe.matmul(m_all[:, base + j * P:base + (j + 1) * P], t.identb, t.neg_qk, start=False, stop=True).then_inc(sm_ready, 1)

                def transpose_max(m, q):
                    pe.wait_ge(mx_ready, after(m * 16 + 15))
                    pe.wait_ge(ml_ready, after(m - 1))
                    pe.transpose(o_bank[0:16, 0:P], mx[:, q, :], t.ident).then_inc(mt_ready, 1)

                def scores(m, q, u):
                    s, pieces = units[u]
                    for c in range(2):
                        pe.wait_ge(p_ready, after(m * 2 * NU + 2 * (u - 1) + c))
                        diagonal = pieces[0][4]
                        for k, (kt, at_, qc, n, _) in enumerate(pieces):
                            last = pe.matmul(e_bank[c][:, at_:at_ + n], kS[:, kt * P:(kt + 1) * P],
                                             qS[q][c][:, s * HALF + qc:s * HALF + qc + n], start=True if not diagonal else k == 0,
                                             stop=not diagonal, skip_group_check=diagonal)
                        if diagonal:
                            last = pe.matmul(e_bank[c][:, :], t.identb, t.neg_kq, start=False, stop=True, skip_group_check=True)
                        last.then_inc(s_ready, 1)

                def values(m, q, u):
                    s, pieces = units[u]
                    first = u in (0, NQ0)
                    if first:
                        pe.wait_ge(yc_ready, after(m * 2 + s - 1))
                    pe.wait_ge(p_ready, after(m * 2 * NU + 2 * u + 1))
                    end = u in (NQ0 - 1, NU - 1)
                    for k, (kt, at_, qc, n, _) in enumerate(pieces):
                        for c in range(2):
                            last = pe.matmul(y_bank[VW * c:VW * (c + 1), qc:qc + n], V[:, kt, :], probs[:, u % 2, c, at_:at_ + n],
                                             start=first and k == 0, stop=end, skip_group_check=True)
                    last.then_inc(y_ready if end else pv_ready, 1)

                def start():
                    transpose_x(0)
                    latents(0)
                    latent_rows(0)
                    for c in range(2):
                        project(0, c)
                    for v in range(16):
                        scores_max(0, 0, v, kN)
                    pe.wait_ge(v_ready, after(0))
                    transpose_max(0, 0)
                    for c in range(2):
                        project(1, c)
                    pe.wait_ge(kc_ready, after(0))

                def pair(m, q, i, b, ahead):
                    last_pair = isinstance(i, int) and i == PAIRS - 1
                    pe.wait_ge(m_in, (m + 1) * 64)
                    for u in range(NU):
                        scores(m, q, u)
                        if ahead[0]:
                            for v in MAXIMA[u] if u < len(MAXIMA) else ():
                                scores_max(m + 1, 1 - q, v, kN if last_pair else kS)
                            if u == NU - 3:
                                if last_pair:
                                    pe.wait_ge(v_ready, after(b + 1))
                                transpose_max(m + 1, 1 - q)
                        if opens(i, ahead):
                            if u == NU - 3:
                                transpose_x(b + 1)
                            if u == NU - 2:
                                latents(b + 1)
                        if u >= 1:
                            values(m, q, u - 1)
                        if opens(i, ahead) and u == NU - 2:
                            latent_rows(b + 1)
                    if ahead[1]:
                        for c in range(2):
                            project(m + 2, c)
                    values(m, q, NU - 1)

                def finish(b, more):
                    def heads_out(j):
                        if j == 0:
                            pe.wait_ge(yc_ready, after((b + 1) * PAIRS * 2 - 1))
                            if more:
                                pe.wait_ge(qs_ready, after((b + 1) * PAIRS * 4 + 7))
                        pe.wait_ge(z_ready, after(b * BT + j - 2))
                        for i in range(PAIRS):
                            last = pe.transpose(m_all[:, (j % 2) * 2 * HALF + i * P:(j % 2) * 2 * HALF + (i + 1) * P],
                                                yT[:, i, j * P:(j + 1) * P], t.ident)
                        last.then_inc(zt_ready, 1)

                    def output(j):
                        pe.wait_ge(zc_ready, after((b * BT + j) * 2 + 1))
                        if j == 0:
                            pe.wait_ge(ml_ready, after((b + 1) * PAIRS - (0 if more else 1)))
                        pe.wait_ge(res.xo_ready, after(b * BT + j - 1))
                        for k in range(5):
                            last = pe.matmul(o_bank[:, 0:P], zT[:, j % 2, k * P:(k + 1) * P], wo[:, k * P:(k + 1) * P], start=k == 0, stop=k == 4)
                        last.then_inc(o_ready, 1)

                    heads_out(0)
                    for j in range(BT):
                        if j + 1 < BT:
                            heads_out(j + 1)
                        pe.wait_ge(z_ready, after(b * BT + j))
                        pe.wait_ge(zc_ready, after((b * BT + j - 1) * 2 + 1))
                        pe.wait_ge(p_ready, after((b + 1) * PAIRS * 2 * NU - 1))
                        for k in range(5):
                            last = pe.transpose(e_bank[k // 4][:, (k % 4) * P:(k % 4 + 1) * P], z[:, j % 2, k * P:(k + 1) * P], t.ident)
                        last.then_inc(zz_ready, 1)
                        if j >= 1:
                            output(j - 1)
                    output(BT - 1)
                    if more:
                        pe.wait_ge(kc_ready, after(b + 1))
                        pe.wait_ge(res.xo_ready, after(b * BT + BT - 1))

                pipeline(pe, start, pair, finish)

            @block.scalar
            def _(act):
                layernorm_scales(act, None, nc, t, rstd_ready)
                for s in (xh_ready, kt_ready, qt_ready, mh_ready, p_ready, zc_ready):
                    act.sem_inc(s, LEAD)
                act.wait_ge(w_in, 64)
                act.activation(wd[0][:, :], wd32[:, :], ACT.Copy)
                act.activation(lat[0][:, :], lat32[:, :], ACT.Copy).then_inc(w_high, 1)
                act.wait_ge(w_low, 2)

                def high_x(b):
                    for s in range(2):
                        act.wait_ge(xt_ready, after(b * 2 + s))
                        act.wait_ge(qp_ready, after(b * PAIRS * 4 - 1))
                        act.activation(xT[0][:, s * HALF:(s + 1) * HALF], m_bank[s], ACT.Copy).then_inc(xh_ready, 1)

                def low_keys(b):
                    for s in range(2):
                        act.wait_ge(kp_ready, after(b * 2 + s))
                        act.wait_ge(ks_ready, after((b - 1) * 2 + s))
                        act.activation(kT[:, s, :], m_bank[2 + s][0:STACK, :], ACT.Identity, bias=k_lbias[:, :],
                                       scale=k_low).then_inc(kt_ready, 1)

                def start():
                    high_x(0)
                    low_keys(0)
                    for g in range(4):
                        low_query(0, g)
                    high_max(0, 0)
                    for g in range(4):
                        low_query(1, g)

                def low_query(m, g):
                    act.wait_ge(qp_ready, after(m * 4 + g))
                    act.wait_ge(qs_ready, after(m * 4 + g - 2))
                    act.activation(qT[:, g % 2, :], m_bank[g][0:STACK, :], ACT.Identity, bias=bcur[:, 1, g // 2:g // 2 + 1],
                                   scale=q_low).then_inc(qt_ready, 1)

                def high_max(m, q):
                    act.wait_ge(mt_ready, after(m))
                    act.activation(mh[:, q, :], o_bank[0:16, 0:P], ACT.Copy).then_inc(mh_ready, 1)

                def pair(m, q, i, b, ahead):
                    for u in range(NU):
                        for c in range(2):
                            act.wait_ge(s_ready, after(m * 2 * NU + 2 * u + c))
                            if c == 0:
                                if u in (0, 1):
                                    act.wait_ge(pv_ready if u == 0 else y_ready, after((m - 1) * (NU - 2) + NU - 3) if u == 0 else after(m * 2 - 1))
                                elif u - 2 == NQ0 - 1:
                                    act.wait_ge(y_ready, after(m * 2))
                                else:
                                    act.wait_ge(pv_ready, after(m * (NU - 2) + (u - 2) - (1 if u - 2 >= NQ0 else 0)))
                            n = 256 if len(units[u][1]) == 1 and units[u][1][0][3] == 256 else HALF
                            act.activation(probs[:, u % 2, c, HALF - n:HALF], e_bank[c][:, HALF - n:HALF], ACT.Exp,
                                           scale=SCORE_SCALE).then_inc(p_ready, 1)
                        if ahead[0] and u == NU - 3:
                            high_max(m + 1, 1 - q)
                        if opens(i, ahead):
                            if u == NU - 3:
                                high_x(b + 1)
                            if u == NU - 2:
                                low_keys(b + 1)
                    if ahead[1]:
                        for g in range(4):
                            low_query(m + 2, g)

                def finish(b, more):
                    for j in range(BT):
                        act.wait_ge(zz_ready, after(b * BT + j))
                        act.wait_ge(o_ready, after(b * BT + j - 2))
                        act.activation(zT[:, j % 2, 0:HALF], e_bank[0][:, :], ACT.Copy).then_inc(zc_ready, 1)
                        act.activation(zT[:, j % 2, HALF:ZW], e_bank[1][:, 0:P], ACT.Copy).then_inc(zc_ready, 1)

                pipeline(act, start, pair, finish)

            @block.vector
            def _(dve):
                layernorm_scales(None, dve, nc, t, rstd_ready)
                for s in (xn_ready, xl_ready, ks_ready, v_ready, qs_ready, mx_ready, ml_ready, yc_ready, r_ready, z_ready):
                    dve.sem_inc(s, LEAD)
                res.prime(dve)
                dve.memset(f32(minus[:, :]), -1.0).then_inc(minus_ready, 1)
                dve.wait_ge(w_in, 64)
                dve.tensor_scalar(k_lbias[:, :], k_bias, k_low, None, ALU.mult)
                dve.tensor_scalar(qb_low[:, :], q_bias, q_low, None, ALU.mult).then_inc(w_low, 1)
                dve.wait_ge(w_high, 1)
                dve.tensor_tensor(wd[1][:, :], wd32[:, :], f32(wd[0][:, :]), ALU.subtract)
                dve.tensor_tensor(lat[1][:, :], lat32[:, :], f32(lat[0][:, :]), ALU.subtract).then_inc(w_low, 1)
                dve.wait_ge(k_in, 16)
                dve.wait_ge(const_ready, 2)

                def normalise(b):
                    for j in range(BT):
                        if j % 4 == 0:
                            dve.wait_ge(xt_ready, after((b - 1) * 2 + j // 4))
                        n = b * BT + j
                        dve.tensor_scalar(xn[:, j, :], t.X[:, at(n), :], t.stats[:, at(n), 0], t.rstd[:, at(n)],
                                          ALU.subtract, ALU.mult).then_inc(xn_ready, 1)

                def low_x(b):
                    for s in range(2):
                        half = slice(s * HALF, (s + 1) * HALF)
                        dve.wait_ge(xh_ready, after(b * 2 + s))
                        dve.tensor_tensor(xT[1][:, half], m_bank[s], f32(xT[0][:, half]), ALU.subtract).then_inc(xl_ready, 1)

                def next_keys(b):
                    for s in range(2):
                        dve.wait_ge(kt_ready, after(b * 2 + s))
                        dve.wait_ge(kc_ready, after(b - 1))
                        dve.scalar_tensor_tensor(kN[:, s * HALF:(s + 1) * HALF], m_bank[2 + s][0:STACK, :], k_bias,
                                                 f32(kT[:, s, :]), ALU.add, ALU.subtract).then_inc(ks_ready, 1)
                    dve.wait_ge(vp_ready, after(b))
                    dve.tensor_tensor(VN[:, :, :], o_bank[:, :].rearrange("p (j v) -> p j v", v=VW)[:, :, 0:LAT],
                                      v_bias.unsqueeze(1).to_broadcast([P, BT, LAT]), ALU.add).then_inc(v_ready, 1)

                def start():
                    normalise(0)
                    low_x(0)
                    next_keys(0)
                    for g in range(4):
                        query(0, 0, g)
                    for v in range(16):
                        maximum(0, 0, v)
                    low_max(0, 0)
                    for g in range(4):
                        query(1, 1, g)

                def query(m, q, g):
                    c, s = g // 2, g % 2
                    dve.wait_ge(qt_ready, after(m * 4 + g))
                    dve.wait_ge(s_ready, after((m - 1) * 2 * NU - 1))
                    dve.scalar_tensor_tensor(qS[q][c][0:STACK, s * HALF:(s + 1) * HALF], m_bank[g][0:STACK, :],
                                             bcur[:, 0, c:c + 1], f32(qT[:, g % 2, :]), ALU.add, ALU.subtract).then_inc(qs_ready, 1)

                def maximum(m, q, v):
                    dve.wait_ge(sm_ready, after(m * 16 + v))
                    base = (v % 2) * 2 * HALF
                    dve.reduce_max(mx[:, q, v:v + 1], m_all[:, base:base + (v % 8 + 1) * P], AX.X).then_inc(mx_ready, 1)

                def low_max(m, q):
                    dve.wait_ge(mh_ready, after(m))
                    dve.tensor_tensor(ml[:, q, :], o_bank[0:16, 0:P], f32(mh[:, q, :]), ALU.subtract).then_inc(ml_ready, 1)

                def copy_out(m, i, s):
                    dve.wait_ge(y_ready, after(m * 2 + s))
                    dve.tensor_scalar(yT[:, at(i), s * HALF:(s + 1) * HALF], y_bank[:, :], 1.0, None, ALU.mult).then_inc(yc_ready, 1)

                def pair(m, q, i, b, ahead):
                    if ahead[0]:
                        for v in range(9):
                            maximum(m + 1, 1 - q, v)
                    copy_out(m, i, 0)
                    if opens(i, ahead):
                        normalise(b + 1)
                    if ahead[0]:
                        for v in range(9, 16):
                            maximum(m + 1, 1 - q, v)
                        low_max(m + 1, 1 - q)
                    if opens(i, ahead):
                        low_x(b + 1)
                        next_keys(b + 1)
                    if ahead[1]:
                        for g in range(4):
                            query(m + 2, q, g)
                    copy_out(m, i, 1)

                def finish(b, more):
                    for j in range(BT):
                        n = b * BT + j
                        heads = m_all[:, (j % 2) * 2 * HALF:(j % 2 + 1) * 2 * HALF].rearrange("p (h v) -> p h v", v=VW)
                        dve.wait_ge(zt_ready, after(n))
                        dve.reciprocal(rcp[:, j % 2, :], heads[:, :, LAT]).then_inc(r_ready, 1)
                        dve.wait_ge(r_ready, after(n))
                        dve.wait_ge(zz_ready, after(n - 2))
                        dve.tensor_tensor(z[:, j % 2, 0:HEADS * LAT].rearrange("p (h v) -> p h v", v=LAT), heads[:, :, 0:LAT],
                                          rcp[:, j % 2, :].unsqueeze(2).to_broadcast([P, HEADS, LAT]), ALU.mult).then_inc(z_ready, 1)
                        if j >= 2:
                            add_output(b * BT + j - 2, j % 2)
                    for j in range(BT - 2, BT):
                        add_output(b * BT + j, j % 2)

                def add_output(n, q):
                    dve.wait_ge(o_ready, after(n))
                    res.add(dve, n, q, n, o_bank[:, 0:P])

                pipeline(dve, start, pair, finish)
        sem.clear()





def attn1_laid_out(np, a, r):
    wd = np.repeat(a["L1_attn_Wd_w"].transpose(1, 0, 2)[:, :, None, :], 3, axis=2)
    r["wd"] = wd.reshape(P, HEADS * STACK)
    r["latent"] = np.tile(a["L1_attn_latent_w"], (1, 3))
    wo = np.zeros((ZW, DIM), np.float32)
    wo[0:HEADS * LAT] = a["L1_attn_out_w"]
    wo[HEADS * LAT] = a["L1_attn_out_b"]
    r["wo"] = wo.reshape(5, P, DIM).transpose(1, 0, 2).reshape(P, ZW)
    small = np.zeros((P, L1_COLS), np.float32)
    small[:, 0:LAT] = a["L1_attn_latent_b"]
    small[0:STACK, 36] = np.tile(a["L1_attn_latent_b"], 3)
    small[LAT:2 * LAT, 37] = 1.0
    small[2 * LAT:STACK, 38] = 1.0
    small[0:STACK, 40:40 + HEADS] = np.tile(a["L1_attn_Wd_b"].T, (3, 1))
    r["attn1_small"] = small


def macaron(nc, d, out, phases=("moe", "attn0", "moe", "ffn", "attn1", "ffn")):
    t = Shared()
    with ExitStack() as ctx:
        def sb(name, shape, dt=F32):
            return ctx.enter_context(nc.sbuf_tensor(name, shape, dt))

        t.X = sb("X", [P, TILES, DIM])
        t.stats = sb("stats", [P, TILES, 2])
        t.rstd = sb("rstd", [P, TILES])
        t.consts = sb("consts", [P, CONSTS])
        t.ident = t.consts[:, C_IDENT:C_IDENT + P]
        t.bconsts = sb("bconsts", [P, CONSTS - C_IDENT], BF16)
        t.identb = t.bconsts[:, 0:P]
        t.neg_qk = t.bconsts[:, C_NEG_QK - C_IDENT:C_NEG_KQ - C_IDENT]
        t.neg_kq = t.bconsts[:, C_NEG_KQ - C_IDENT:C_NEG_KQ - C_IDENT + HALF]
        t.iota8 = t.consts[:, C_IOTA:C_IOTA + EXPERTS]
        load_input(nc, t, d)
        for n, name in enumerate(phases):
            if name == "moe":
                with ExitStack() as moe:
                    t.rout = [moe.enter_context(nc.sbuf_tensor(f"m{n}_routers{i}", [P, 2 * EXPERTS + KC * EXPERTS], F32R)) for i in range(2)]
                    t.W = [[moe.enter_context(nc.sbuf_tensor(f"m{n}_W{w}{i}", [P, EXPERTS * INNER], F32R)) for i in range(2)] for w in "gud"]
                    load_experts(nc, t, d, f"m{n}")
                    moe_phase(nc, t, f"m{n}")
            if name == "attn0":
                attn0_phase(nc, t, d, f"a{n}")
            if name == "ffn":
                ffn_phase(nc, t, d, f"f{n}", None)
            if name == "attn1":
                attn1_phase(nc, t, d, f"b{n}")
        store_phase(nc, t, out)


def store_phase(nc, t, out):
    with nc.semaphore("out_done") as out_done, nc.Block() as block:
        @block.sync
        def _(sp):
            sp.dma_start(out.rearrange("(n p) c -> p n c", p=P), t.X[:, :, :]).then_inc(out_done, 16)
            sp.wait_ge(out_done, 16)


C_EPS, C_IOTA, C_IDENT = 0, 8, 16
C_NEG_QK = C_IDENT + P
C_NEG_KQ = C_NEG_QK + P
CONSTS = C_NEG_KQ + HALF
NEG = -1e30


def constants(np):
    c = np.zeros((P, CONSTS), np.float32)
    c[:, C_EPS] = EPS
    c[:, C_IOTA:C_IOTA + EXPERTS] = np.arange(EXPERTS)
    c[:, C_IDENT:C_IDENT + P] = np.eye(P)
    c[:, C_NEG_QK:C_NEG_KQ] = NEG * np.triu(np.ones((P, P)), 1)
    c[:, C_NEG_KQ:] = np.tile(NEG * np.tril(np.ones((P, P)), -1), (1, 4))
    return c


def laid_out(inputs):
    import numpy as np

    a = {k: np.asarray(v) for k, v in inputs.items()}
    r = {}
    r["x"] = a["L0_attn_x"].reshape(BATCH * SEQ, DIM)
    r["w_gate"] = a["L0_ffn_w_gate"].transpose(2, 0, 1).reshape(P, EXPERTS * INNER)
    r["w_up"] = a["L0_ffn_w_up"].transpose(2, 0, 1).reshape(P, EXPERTS * INNER)
    r["w_down"] = a["L0_ffn_w_down"].reshape(EXPERTS, DIM, KC, P).transpose(3, 2, 0, 1).reshape(P, KC * EXPERTS * DIM)
    r["routers"] = np.concatenate([
        a["L0_ffn_router_gate"].T, a["L0_ffn_router_up"].T,
        a["L0_ffn_router_down"].reshape(EXPERTS, KC, P).transpose(2, 1, 0).reshape(P, KC * EXPERTS)], axis=1)
    r["consts"] = constants(np)
    attn0_laid_out(np, a, r)
    ffn_laid_out(np, a, r)
    attn1_laid_out(np, a, r)
    return {k: np.ascontiguousarray(v) for k, v in r.items()}


def kernel(**inputs):
    import concourse.bacc as bacc
    from concourse.bass_utils import run_bass_kernel_spmd

    nc = bacc.Bacc("TRN2", target_bir_lowering=False, num_devices=1)
    arrays = {f"in_{k}": v for k, v in laid_out(inputs).items()}
    d = {k[3:]: nc.dram_tensor(k, v.shape, mybir.dt.from_np(v.dtype), kind="ExternalInput").ap() for k, v in arrays.items()}
    out = nc.dram_tensor("out", (BATCH * SEQ, DIM), F32, kind="ExternalOutput").ap()
    macaron(nc, d, out)
    r = run_bass_kernel_spmd(nc, [arrays], core_ids=[0])
    return r.results[0]["out"].reshape(BATCH, SEQ, DIM)
```

```python
import concourse.bass as bass
from concourse import mybir
from contextlib import ExitStack

F32 = mybir.dt.float32
F32R = mybir.dt.float32r
BF16 = mybir.dt.bfloat16
U32 = mybir.dt.uint32
ALU = mybir.AluOpType
ACT = mybir.ActivationFunctionType
AX = mybir.AxisListType

P = 128
BATCH, SEQ, DIM = 4, 1024, 128
TILES = BATCH * SEQ // P
BT = SEQ // P
EXPERTS, INNER = 8, 512
KC = INNER // P
HALF = 512
HEADS, HD = 16, 8
GROUPS, GH = 4, 4
LAT = 36
EPS = 1e-5
SCORE_SCALE = HD ** -0.5

LEAD = 64


def after(n):
    return n + 1 + LEAD


def at(t):
    return bass.ds(t, 1)


def f32(ap):
    return ap.bitcast(F32)


class Links:

    def __init__(self, eng, sem, per):
        self.eng, self.sem, self.per = eng, sem, per
        self.item, self.k = 0, per

    def start(self, item):
        assert self.k == self.per, (self.k, self.per)
        self.item, self.k = item, 0

    def mark(self, ins):
        ins.then_inc(self.sem, 1)
        self.k += 1

    def wait(self):
        self.eng.wait_ge(self.sem, self.item * self.per + (self.k + LEAD))


def layernorm_scales(act, t, sqrt_ready):
    act.activation(t.rstd[:, :], t.stats[:, :, 1], ACT.Sqrt, bias=t.consts[:, 0:1]).then_inc(sqrt_ready, 1)


def layernorm_reciprocals(dve, t, sqrt_ready):
    dve.wait_ge(sqrt_ready, 1)
    dve.reciprocal(t.rstd[:, :], t.rstd[:, :]).then_inc(sqrt_ready, 1)
    dve.wait_ge(sqrt_ready, 2)


class Semaphores:

    def __init__(self, ctx, nc, tag):
        self.ctx, self.nc, self.tag, self.all = ctx, nc, tag, []

    def __call__(self, name):
        s = self.ctx.enter_context(self.nc.semaphore(f"{self.tag}_{name}"))
        self.all.append(s)
        return s

    def clear(self):
        with self.nc.Block() as block:
            @block.sync
            def _(sp):
                for s in self.all:
                    sp.sem_clear(s)


class ResidualAdd:

    def __init__(self, ctx, nc, sem, t, tag, tiles):
        self.t, self.tiles = t, tiles
        self.xo = ctx.enter_context(nc.sbuf_tensor(f"{tag}_xo", [P, 2, tiles, DIM], F32))
        self.stat6 = ctx.enter_context(nc.sbuf_tensor(f"{tag}_stat6", [P, 2, tiles, 6], F32))
        self.aggr = ctx.enter_context(nc.sbuf_tensor(f"{tag}_aggr", [P, 2, tiles, 2], F32))
        self.xo_ready, self.stat_ready, self.pause = sem("xo_ready"), sem("stat_ready"), sem("dve_pause")

    def prime(self, dve):
        dve.sem_inc(self.xo_ready, LEAD)
        dve.sem_inc(self.stat_ready, LEAD)

    def add(self, dve, item, q, tile, bank):
        t, some = self.t, bass.ds(tile, self.tiles)
        dve.tensor_tensor(self.xo[:, q, :, :], bank.rearrange("p (j c) -> p j c", c=DIM), t.X[:, some, :],
                          ALU.add).then_inc(self.xo_ready, 1)
        dve.wait_ge(self.xo_ready, after(item))
        dve.sem_inc(self.pause, 1)
        dve.tensor_copy(t.X[:, some, :], self.xo[:, q, :, :])
        for j in range(self.tiles):
            ins = dve.bn_stats(self.stat6[:, q, j, :], self.xo[:, q, j, :])
        ins.then_inc(self.stat_ready, 1)
        dve.wait_ge(self.stat_ready, after(item * 2))
        dve.sem_inc(self.pause, 1)
        for j in range(self.tiles):
            ins = dve.bn_aggr(self.aggr[:, q, j, :], self.stat6[:, q, j, :])
        ins.then_inc(self.stat_ready, 1)
        dve.wait_ge(self.stat_ready, after(item * 2 + 1))
        dve.sem_inc(self.pause, 1)
        dve.tensor_copy(t.stats[:, some, :], self.aggr[:, q, :, :])


class Shared:
    pass


def input_statistics(dve, t, stat6, x_in, c_in, stat_ready):
    for i in range(TILES):
        if i % 16 == 0:
            dve.wait_ge(x_in[i // 16], 16)
        dve.bn_stats(stat6[:, i, :], t.X[:, i, :]).then_inc(stat_ready, 1)
    for i in range(TILES):
        dve.wait_ge(stat_ready, i + 1)
        dve.bn_aggr(t.stats[:, i, :], stat6[:, i, :]).then_inc(stat_ready, 1)
    dve.wait_ge(c_in, 16)
    dve.tensor_copy(t.bconsts[:, :], t.consts[:, C_IDENT:CONSTS]).then_inc(stat_ready, 1)


def read_input(sp, t, d, x_in, c_in):
    sp.dma_start(t.consts[:, :], d["consts"]).then_inc(c_in, 16)
    for i in range(2):
        sp.dma_start(t.X[:, 16 * i:16 * i + 16, :],
                     d["x"].rearrange("(n p) c -> p n c", p=P)[:, 16 * i:16 * i + 16, :]).then_inc(x_in[i], 16)


def moe_phase(nc, t, d, tag, reads_input, load_ahead):
    with ExitStack() as ctx:
        def sb(name, shape, dt=F32):
            return ctx.enter_context(nc.sbuf_tensor(f"{tag}_{name}", shape, dt))

        sem = Semaphores(ctx, nc, tag)

        W = [[sb(f"W{w}{i}", [P, EXPERTS * INNER], F32R) for i in range(2)] for w in "gud"]
        stage = [sb(f"stage{w}", [P, EXPERTS * INNER]) for w in "gu"]
        stage.append(stage[0])
        rstage = sb("rstage", [P, 2 * EXPERTS + KC * EXPERTS])
        route_gate_up = sb("route_gate_up", [P, 2, 2 * EXPERTS], F32R)
        route_down_w = sb("route_down_w", [P, KC, 2, EXPERTS], F32R)
        CHUNK = 1024
        CHUNKS = [(w, c) for c in range(4) for w in (0, 1)] + [(2, c) for c in range(4)]

        xn = sb("xn", [P, 2, DIM])
        xh = [sb(f"xh{i}", [P, P], F32R) for i in range(2)]
        xl = [sb(f"xl{i}", [P, P], F32R) for i in range(2)]
        logits = sb("logits", [P, 2, 16])
        top = sb("top", [P, 2, 2, 8])
        topi = sb("topi", [P, 2, 2, 8], U32)
        pick = sb("pick", [P, 2, 2, 2])
        gap = sb("gap", [P, 2, 2])
        prob = sb("prob", [P, 2, 2, 2])
        part = sb("part", [P, 2, 2, 2, EXPERTS])
        comb = sb("comb", [P, 2, 2, EXPERTS])
        dlogits = sb("dlogits", [P, 2, 8])
        dtop = sb("dtop", [P, 2, 8])
        dtopi = sb("dtopi", [P, 2, 8], U32)
        dpick = sb("dpick", [P, 2, 2])
        dgap = sb("dgap", [P, 2, 1])
        dprob = sb("dprob", [P, 2, 2])
        dhalf = sb("dhalf", [P, 2, 2])
        dpart = sb("dpart", [P, 2, 2, EXPERTS])
        dcomb = sb("dcomb", [P, 2, EXPERTS])
        acc = sb("acc", [P, 2, 2, INNER])
        sig = sb("sig", [P, 2, INNER])
        gated = sb("gated", [P, 2, INNER])
        inter = sb("inter", [P, 2, INNER])
        ih = [sb(f"ih{i}", [P, INNER], F32R) for i in range(2)]
        il = [sb(f"il{i}", [P, INNER], F32R) for i in range(2)]
        yacc = sb("yacc", [P, 2, DIM])
        stat6 = sb("stat6", [P, 2, 6])

        ps = [ctx.enter_context(nc.psum_tensor(f"{tag}_ps{i}", [P, HALF], F32)) for i in range(8)]
        expert_bank, a_bank, t_bank, y_bank = ps[0:4], ps[4], ps[5], ps[6:8]

        rstd_ready = sem("rstd_ready")
        xn_ready, xt_ready, xh_ready, xl_ready = sem("xn_ready"), sem("xt_ready"), sem("xh_ready"), sem("xl_ready")
        lg_ready, lg_copied, gap_ready, prob_ready, comb_ready = (
            sem("lg_ready"), sem("lg_copied"), sem("gap_ready"), sem("prob_ready"), sem("comb_ready"))
        prod_ready, first_used, prod_used = sem("prod_ready"), sem("first_used"), sem("prod_used")
        sig_ready, gated_ready, inter_ready = sem("sig_ready"), sem("gated_ready"), sem("inter_ready")
        it_ready, ih_ready, il_ready = sem("it_ready"), sem("ih_ready"), sem("il_ready")
        dlg_ready, dlg_copied, dgap_ready, dprob_ready, dcomb_ready = (
            sem("dlg_ready"), sem("dlg_copied"), sem("dgap_ready"), sem("dprob_ready"), sem("dcomb_ready"))
        y_ready, y_used = sem("y_ready"), sem("y_used")
        dve_a, dve_c, dve_y = sem("dve_a"), sem("dve_c"), sem("dve_y")
        pool_a, pool_c = sem("pool_a"), sem("pool_c")
        dve_pause, pool_pause = sem("dve_pause"), sem("pool_pause")
        aggr = sb("aggr", [P, 2, 2])

        ND = 2 * EXPERTS - 2
        w_in, r_in = [sem(f"w_in{k}") for k in range(len(CHUNKS))], sem("r_in")
        r_high, r_low, w_high, w_low = sem("r_high"), sem("r_low"), sem("w_high"), sem("w_low")
        if reads_input:
            x_in, c_in, input_stats = [sem(f"x_in{i}") for i in range(2)], sem("const_in"), sem("input_stats")
            stat6_all = sb("stat6_all", [P, TILES, 6])

        def exists(m):
            return not isinstance(m, int) or 0 <= m < TILES

        def tiles(eng, body):
            body(0, 0)
            body(1, 1)
            with eng.Fori(0, (TILES - 4) // 2) as i:
                for q in range(2):
                    body(i * 2 + (2 + q), q)
            for n in range(TILES - 2, TILES + 2):
                body(n, n % 2)

        with nc.Block() as block:
            @block.sync
            def _(sp):
                if reads_input:
                    read_input(sp, t, d, x_in, c_in)
                sp.dma_start(rstage[:, :], d["routers"]).then_inc(r_in, 16)
                for k, (w, c) in enumerate(CHUNKS):
                    cols = slice(c * CHUNK, (c + 1) * CHUNK)
                    if w == 2:
                        sp.wait_ge(w_low, 2 * c + 1)
                    sp.dma_start(stage[w][:, cols], d[("w_gate", "w_up", "w_down")[w]][:, cols]).then_inc(w_in[k], 16)
                load_ahead(sp)

            @block.tensor
            def _(pe):
                if reads_input:
                    pe.wait_ge(c_in, 16)
                for s in (xt_ready, lg_ready, prod_ready, it_ready, dlg_ready, y_ready):
                    pe.sem_inc(s, LEAD)

                def transpose_x(n, q):
                    pe.wait_ge(xn_ready, after(n))
                    pe.wait_ge(lg_copied, after(n - 1))
                    pe.transpose(a_bank[:, 0:P], xn[:, q, :], t.ident).then_inc(xt_ready, 1)

                def route_gu(n, q):
                    pe.wait_ge(xh_ready, after(n))
                    pe.wait_ge(xl_ready, after(n))
                    if isinstance(n, int) and n == 0:
                        pe.wait_ge(r_low, 1)
                    pe.matmul(a_bank[:, P:P + 32], xh[q][:, :], route_gate_up[:, :, :], start=True, stop=False, skip_group_check=True)
                    pe.matmul(a_bank[:, P:P + 16], xl[q][:, :], route_gate_up[:, 0, :], start=False, stop=True,
                              skip_group_check=True).then_inc(lg_ready, 1)

                def product(n, q, j):
                    if j < 4:
                        pe.wait_ge(prod_used, after(n * ND + (j - 4)))
                    elif j < 6:
                        pe.wait_ge(first_used, after(n * 2 + (j - 4)))
                    else:
                        pe.wait_ge(prod_used, after(n * ND + (j - 6)))
                    w, e = W[j % 2], j // 2
                    if isinstance(n, int) and n == 0 and j % 4 == 0:
                        pe.wait_ge(w_low, j // 2 + 2)
                    cols = slice(e * INNER, (e + 1) * INNER)
                    for k, (a, b) in enumerate(((xh, 0), (xh, 1), (xl, 0))):
                        last = pe.matmul(expert_bank[j % 4][:, :], a[q][:, :], w[b][:, cols], start=k == 0, stop=k == 2)
                    last.then_inc(prod_ready, 1)

                def transpose_inter(n, q):
                    pe.wait_ge(inter_ready, after(n))
                    pe.wait_ge(dlg_copied, after(n - 1))
                    for c in range(KC):
                        last = pe.transpose(t_bank[:, c * P:(c + 1) * P], inter[:, q, c * P:(c + 1) * P], t.ident)
                    last.then_inc(it_ready, 1)

                def route_down(n, q):
                    pe.wait_ge(ih_ready, after(n))
                    pe.wait_ge(il_ready, after(n))
                    for c in range(KC):
                        rows = slice(c * P, (c + 1) * P)
                        pe.matmul(t_bank[:, 0:2 * EXPERTS], ih[q][:, rows], route_down_w[:, c, :, :], start=c == 0, stop=False,
                                  skip_group_check=True)
                        last = pe.matmul(t_bank[:, 0:EXPERTS], il[q][:, rows], route_down_w[:, c, 0, :], start=False,
                                         stop=c == KC - 1, skip_group_check=True)
                    last.then_inc(dlg_ready, 1)

                def down(n, q, h, c):
                    if c == 0:
                        pe.wait_ge(ih_ready, after(n))
                        pe.wait_ge(il_ready, after(n))
                        pe.wait_ge(y_used, after((n - 1) * 2 + h))
                    if isinstance(n, int) and n == 0:
                        pe.wait_ge(w_low, 9 + c)
                    rows = slice(c * P, (c + 1) * P)
                    cols = slice(c * 1024 + h * HALF, c * 1024 + (h + 1) * HALF)
                    for k, (a, b) in enumerate(((ih, 0), (ih, 1), (il, 0))):
                        last = pe.matmul(y_bank[h][:, :], a[q][:, rows], W[2][b][:, cols],
                                         start=c == 0 and k == 0, stop=c == KC - 1 and k == 2)
                    if c == KC - 1:
                        last.then_inc(y_ready, 1)

                def body(n, q):
                    for j in range(16):
                        if exists(n):
                            product(n, q, j)
                        if j == 1 and exists(n + 1):
                            transpose_x(n + 1, 1 - q)
                        if j == 5 and exists(n - 1):
                            transpose_inter(n - 1, 1 - q)
                        if j == 6 and exists(n + 1):
                            route_gu(n + 1, 1 - q)
                        if j == 8 and exists(n - 1):
                            route_down(n - 1, 1 - q)
                        if j % 2 == 1 and j < 8 and exists(n - 2):
                            down(n - 2, q, 1, j // 2)
                        if j % 2 == 1 and j > 8 and exists(n - 1):
                            down(n - 1, 1 - q, 0, j // 2 - 4)

                transpose_x(0, 0)
                route_gu(0, 0)
                tiles(pe, body)

            @block.scalar
            def _(act):
                def high_weights(chunks):
                    for k in chunks:
                        w, c = CHUNKS[k]
                        cols = slice(c * CHUNK, (c + 1) * CHUNK)
                        act.wait_ge(w_in[k], 16)
                        act.activation(W[w][0][:, cols], stage[w][:, cols], ACT.Copy).then_inc(w_high, 1)

                if reads_input:
                    act.wait_ge(input_stats, 2 * TILES + 1)
                layernorm_scales(act, t, rstd_ready)
                act.wait_ge(r_in, 16)
                act.activation(route_gate_up[:, 0, :], rstage[:, 0:2 * EXPERTS], ACT.Copy)
                act.activation(route_down_w[:, :, 0, :], rstage[:, 2 * EXPERTS:].rearrange("p (c e) -> p c e", e=EXPERTS),
                               ACT.Copy).then_inc(r_high, 1)
                for s in (xh_ready, prob_ready, first_used, sig_ready, ih_ready, dprob_ready):
                    act.sem_inc(s, LEAD)

                def high_x(n, q):
                    act.wait_ge(xt_ready, after(n))
                    act.wait_ge(prod_ready, after((n - 2) * 16 + 15))
                    act.activation(xh[q][:, :], a_bank[:, 0:P], ACT.Copy).then_inc(xh_ready, 1)

                def probs(n, q):
                    act.wait_ge(gap_ready, after(n * 2 + 1))
                    act.wait_ge(comb_ready, after(n - 2))
                    act.activation(prob[:, q, :, 0], gap[:, q, :], ACT.Sigmoid)
                    act.activation(prob[:, q, :, 1], gap[:, q, :], ACT.Sigmoid, scale=-1.0).then_inc(prob_ready, 1)

                def first(n, q):
                    act.wait_ge(comb_ready, after(n))
                    act.wait_ge(inter_ready, after(n - 2))
                    for j in range(2):
                        act.wait_ge(prod_ready, after(n * 16 + j))
                        act.activation(acc[:, q, j, :], expert_bank[j][:, :], ACT.Copy,
                                       scale=comb[:, q, j, 0:1]).then_inc(first_used, 1)

                def sigmoid(n, q):
                    act.wait_ge(prod_used, after(n * ND + (ND - 2)))
                    act.wait_ge(gated_ready, after(n - 2))
                    act.activation(sig[:, q, :], acc[:, q, 0, :], ACT.Sigmoid).then_inc(sig_ready, 1)

                def high_inter(n, q):
                    act.wait_ge(it_ready, after(n))
                    act.wait_ge(y_ready, after((n - 2) * 2 + 1))
                    act.activation(ih[q][:, :], t_bank[:, :], ACT.Copy).then_inc(ih_ready, 1)

                def dprobs(n, q):
                    act.wait_ge(dgap_ready, after(n * 2 + 1))
                    act.wait_ge(dcomb_ready, after(n - 2))
                    act.activation(dprob[:, q, 0:1], dgap[:, q, :], ACT.Sigmoid)
                    act.activation(dprob[:, q, 1:2], dgap[:, q, :], ACT.Sigmoid, scale=-1.0).then_inc(dprob_ready, 1)

                def body(n, q):
                    if exists(n):
                        first(n, q)
                    if isinstance(n, int) and n == 0:
                        high_weights((2, 3))
                    if exists(n + 1):
                        high_x(n + 1, 1 - q)
                    if isinstance(n, int) and n == 0:
                        high_weights((4, 5, 6, 7))
                    if exists(n - 1):
                        high_inter(n - 1, 1 - q)
                    if isinstance(n, int) and n == 1:
                        high_weights((8, 9, 10, 11))
                    if exists(n + 1):
                        probs(n + 1, 1 - q)
                    if exists(n - 1):
                        dprobs(n - 1, 1 - q)
                    if exists(n):
                        sigmoid(n, q)

                high_x(0, 0)
                high_weights((0, 1))
                probs(0, 0)
                tiles(act, body)

            @block.gpsimd
            def _(pool):
                for s in (comb_ready, gated_ready, inter_ready, dcomb_ready, pool_a, pool_c):
                    pool.sem_inc(s, LEAD)
                own_a, own_c = Links(pool, pool_a, 1), Links(pool, pool_c, 2)

                def combine(n, q):
                    own_a.start(n)
                    pool.wait_ge(prob_ready, after(n))
                    pool.wait_ge(prod_used, after((n - 2) * ND + (ND - 1)))
                    pool.wait_ge(first_used, after((n - 2) * 2 + 1))
                    pool.sem_inc(pool_pause, 1)
                    for r in range(2):
                        for k in range(2):
                            ins = pool.tensor_scalar(part[:, q, r, k, :], t.iota8, pick[:, q, r, k:k + 1],
                                                     prob[:, q, r, k:k + 1], ALU.is_equal, ALU.mult)
                    own_a.mark(ins)
                    own_a.wait()
                    pool.tensor_tensor(comb[:, q, :, :], part[:, q, :, 0, :], part[:, q, :, 1, :], ALU.add).then_inc(comb_ready, 1)

                def dcombine(n, q):
                    own_c.start(n)
                    pool.wait_ge(dprob_ready, after(n))
                    pool.wait_ge(y_used, after((n - 2) * 2 + 1))
                    pool.sem_inc(pool_pause, 1)
                    own_c.mark(pool.tensor_scalar(dhalf[:, q, :], dprob[:, q, :], 0.5, None, ALU.mult))
                    own_c.wait()
                    pool.sem_inc(pool_pause, 1)
                    for k in range(2):
                        ins = pool.tensor_scalar(dpart[:, q, k, :], t.iota8, dpick[:, q, k:k + 1],
                                                 dhalf[:, q, k:k + 1], ALU.is_equal, ALU.mult)
                    own_c.mark(ins)
                    own_c.wait()
                    pool.tensor_tensor(dcomb[:, q, :], dpart[:, q, 0, :], dpart[:, q, 1, :], ALU.add).then_inc(dcomb_ready, 1)

                def gate(n, q):
                    pool.wait_ge(sig_ready, after(n))
                    pool.tensor_tensor(gated[:, q, :], acc[:, q, 0, :], sig[:, q, :], ALU.mult).then_inc(gated_ready, 1)
                    pool.wait_ge(gated_ready, after(n))
                    pool.wait_ge(prod_used, after(n * ND + (ND - 1)))
                    pool.wait_ge(it_ready, after(n - 2))
                    pool.tensor_tensor(inter[:, q, :], gated[:, q, :], acc[:, q, 1, :], ALU.mult).then_inc(inter_ready, 1)

                def body(n, q):
                    if exists(n + 1):
                        combine(n + 1, 1 - q)
                    if exists(n - 1):
                        dcombine(n - 1, 1 - q)
                    if exists(n):
                        gate(n, q)

                combine(0, 0)
                tiles(pool, body)

            @block.vector
            def _(dve):
                def low_weights(chunks):
                    for k in chunks:
                        w, c = CHUNKS[k]
                        cols = slice(c * CHUNK, (c + 1) * CHUNK)
                        dve.wait_ge(w_high, k + 1)
                        dve.tensor_tensor(W[w][1][:, cols], stage[w][:, cols], f32(W[w][0][:, cols]), ALU.subtract).then_inc(w_low, 1)

                if reads_input:
                    input_statistics(dve, t, stat6_all, x_in, c_in, input_stats)
                layernorm_reciprocals(dve, t, rstd_ready)
                dve.wait_ge(r_high, 1)
                dve.tensor_tensor(route_gate_up[:, 1, :], rstage[:, 0:2 * EXPERTS], f32(route_gate_up[:, 0, :]), ALU.subtract)
                dve.tensor_tensor(route_down_w[:, :, 1, :], rstage[:, 2 * EXPERTS:].rearrange("p (c e) -> p c e", e=EXPERTS),
                                  f32(route_down_w[:, :, 0, :]), ALU.subtract).then_inc(r_low, 1)
                for s in (xn_ready, xl_ready, lg_copied, gap_ready, prod_used, il_ready, dlg_copied, dgap_ready,
                          y_used, dve_a, dve_c, dve_y):
                    dve.sem_inc(s, LEAD)
                own_a, own_c, own_y = Links(dve, dve_a, 1), Links(dve, dve_c, 1), Links(dve, dve_y, EXPERTS)

                def normalise(n, q):
                    dve.wait_ge(xt_ready, after(n - 2))
                    dve.tensor_scalar(xn[:, q, :], t.X[:, at(n), :], t.stats[:, at(n), 0], t.rstd[:, at(n)],
                                      ALU.subtract, ALU.mult).then_inc(xn_ready, 1)

                def low_x(n, q):
                    dve.wait_ge(xh_ready, after(n))
                    dve.tensor_tensor(xl[q][:, :], a_bank[:, 0:P], f32(xh[q][:, :]), ALU.subtract).then_inc(xl_ready, 1)

                def best_gu(n, q, step):
                    if step == 0:
                        dve.wait_ge(lg_ready, after(n))
                        dve.reduce_sum(logits[:, q, :], a_bank[:, P:P + 32].rearrange("p (h e) -> p e h", h=2), AX.X).then_inc(lg_copied, 1)
                    if step == 1:
                        dve.wait_ge(lg_copied, after(n))
                        dve.sem_inc(dve_pause, 1)
                        own_a.start(n)
                        for r in range(2):
                            ins = dve.max(top[:, q, r, :], logits[:, q, 8 * r:8 * r + 8])
                        own_a.mark(ins)
                    if step == 2:
                        own_a.wait()
                        dve.wait_ge(comb_ready, after(n - 2))
                        dve.sem_inc(dve_pause, 1)
                        for r in range(2):
                            ins = dve.max_index(topi[:, q, r, :], top[:, q, r, :], logits[:, q, 8 * r:8 * r + 8])
                        ins.then_inc(gap_ready, 1)
                    if step == 3:
                        dve.wait_ge(gap_ready, after(n * 2))
                        dve.tensor_copy(pick[:, q, :, :], topi[:, q, :, 0:2])
                        dve.tensor_tensor(gap[:, q, :], top[:, q, :, 0], top[:, q, :, 1], ALU.subtract).then_inc(gap_ready, 1)

                def add(n, q, j):
                    dve.wait_ge(prod_ready, after(n * 16 + j))
                    if j < 4:
                        dve.wait_ge(first_used, after(n * 2 + (j - 2)))
                    else:
                        dve.wait_ge(prod_used, after(n * ND + (j - 4)))
                    r, e = j % 2, j // 2
                    dve.scalar_tensor_tensor(acc[:, q, r, :], expert_bank[j % 4][:, :], comb[:, q, r, e:e + 1],
                                             acc[:, q, r, :], ALU.mult, ALU.add).then_inc(prod_used, 1)

                def low_inter(n, q):
                    dve.wait_ge(ih_ready, after(n))
                    dve.tensor_tensor(il[q][:, :], t_bank[:, :], f32(ih[q][:, :]), ALU.subtract).then_inc(il_ready, 1)

                def best_down(n, q, step):
                    if step == 0:
                        dve.wait_ge(dlg_ready, after(n))
                        dve.reduce_sum(dlogits[:, q, :], t_bank[:, 0:2 * EXPERTS].rearrange("p (h e) -> p e h", h=2), AX.X).then_inc(dlg_copied, 1)
                    if step == 1:
                        dve.wait_ge(dlg_copied, after(n))
                        dve.sem_inc(dve_pause, 1)
                        own_c.start(n)
                        own_c.mark(dve.max(dtop[:, q, :], dlogits[:, q, :]))
                    if step == 2:
                        own_c.wait()
                        dve.wait_ge(dcomb_ready, after(n - 2))
                        dve.sem_inc(dve_pause, 1)
                        dve.max_index(dtopi[:, q, :], dtop[:, q, :], dlogits[:, q, :]).then_inc(dgap_ready, 1)
                    if step == 3:
                        dve.wait_ge(dgap_ready, after(n * 2))
                        dve.tensor_copy(dpick[:, q, :], dtopi[:, q, 0:2])
                        dve.tensor_tensor(dgap[:, q, :], dtop[:, q, 0:1], dtop[:, q, 1:2], ALU.subtract).then_inc(dgap_ready, 1)

                def add_down(n, q, e):
                    if e == 0:
                        own_y.start(n)
                        dve.wait_ge(dcomb_ready, after(n))
                    if e % 4 == 0:
                        dve.wait_ge(y_ready, after(n * 2 + e // 4))
                    if e == 4:
                        dve.wait_ge(y_used, after(n * 2))
                    elif e:
                        own_y.wait()
                    src = t.X[:, at(n), :] if e == 0 else yacc[:, q, :]
                    dst = t.X[:, at(n), :] if e == EXPERTS - 1 else yacc[:, q, :]
                    ins = dve.scalar_tensor_tensor(dst, y_bank[e // 4][:, (e % 4) * P:(e % 4 + 1) * P],
                                                   dcomb[:, q, e:e + 1], src, ALU.mult, ALU.add)
                    if e % 4 == 3:
                        ins.then_inc(y_used, 1)
                    else:
                        own_y.mark(ins)

                def statistics(n, q, step):
                    if step == 0:
                        dve.wait_ge(y_used, after(n * 2 + 1))
                        dve.sem_inc(dve_pause, 1)
                        own_y.mark(dve.bn_stats(stat6[:, q, :], t.X[:, at(n), :]))
                    else:
                        own_y.wait()
                        dve.sem_inc(dve_pause, 1)
                        if step == 1:
                            own_y.mark(dve.bn_aggr(aggr[:, q, :], stat6[:, q, :]))
                        else:
                            dve.tensor_copy(t.stats[:, at(n), :], aggr[:, q, :])

                def body(n, q):
                    for j in range(16):
                        if j >= 2 and exists(n):
                            add(n, q, j)
                        if isinstance(n, int) and n == 0 and j in (3, 7, 11):
                            low_weights((j // 2 + 1, j // 2 + 2))
                        if isinstance(n, int) and n == 1 and 8 <= j <= 11:
                            low_weights((j,))
                        if j == 3 and exists(n + 1):
                            low_x(n + 1, 1 - q)
                        if j == 7 and exists(n - 1):
                            low_inter(n - 1, 1 - q)
                        if 8 <= j <= 11 and exists(n + 1):
                            best_gu(n + 1, 1 - q, j - 8)
                        if 12 <= j and exists(n - 1):
                            best_down(n - 1, 1 - q, j - 12)
                        if exists(n - 2):
                            if j <= 3:
                                add_down(n - 2, q, j)
                            if 9 <= j <= 12:
                                add_down(n - 2, q, j - 5)
                            if 13 <= j:
                                statistics(n - 2, q, j - 13)
                    if exists(n + 2):
                        normalise(n + 2, q)

                normalise(0, 0)
                normalise(1, 1)
                low_x(0, 0)
                low_weights((0, 1))
                for step in range(4):
                    best_gu(0, 0, step)
                tiles(dve, body)
        sem.clear()


def ffn_phase(nc, t, tag):
    with ExitStack() as ctx:
        def sb(name, shape, dt=F32):
            return ctx.enter_context(nc.sbuf_tensor(f"{tag}_{name}", shape, dt))

        sem = Semaphores(ctx, nc, tag)

        w1, w2, small, w_in, s_in = t.w1, t.w2, t.ffn_small, t.ffn_in, t.ffn_small_in
        b1, b2, scale = small[:, 0:4], small[:, 4:5], small[0:8, 5:6]
        first_half, second_half = small[0:8, 8:12], small[0:8, 12:16]
        b2h = sb("b2h", [P, 1])
        xn = sb("xn", [P, BT, DIM])
        xT = sb("xT", [P, SEQ])
        even = sb("even", [8, DIM])
        odd = sb("odd", [8, DIM])
        evens = sb("evens", [8, DIM])
        odds = sb("odds", [8, KC, DIM])
        evenm = sb("evenm", [8, 4, 4, 32])
        w1e = sb("w1e", [P, INNER])
        w2e = sb("w2e", [P, INNER])
        hid = sb("hid", [P, 2, KC, HALF])
        oT = sb("oT", [P, 2, HALF])
        res = ResidualAdd(ctx, nc, sem, t, tag, 4)
        ps = [ctx.enter_context(nc.psum_tensor(f"{tag}_ps{i}", [P, HALF], F32)) for i in range(8)]
        x_bank, w_bank, h_bank, o_bank = ps[0:2], ps[2], ps[3:7], ps[7]

        rstd_ready, b2h_ready = sem("rstd_ready"), sem("b2h_ready")
        xn_ready, rows_in, pairs_ready = sem("xn_ready"), sem("rows_in"), sem("pairs_ready")
        xt_ready, xt_copied, wp_ready, we_ready = sem("xt_ready"), sem("xt_copied"), sem("wp_ready"), sem("we_ready")
        h_ready, hid_ready, o_ready, o_copied = sem("h_ready"), sem("hid_ready"), sem("o_ready"), sem("o_copied")
        ot_ready = sem("ot_ready")

        def pipeline(eng, start, run):
            start()
            with eng.Fori(0, BATCH - 1) as b:
                run(b, True)
            run(BATCH - 1, False)

        with nc.Block() as block:
            @block.sync
            def _(sp):
                with sp.Fori(0, BATCH) as b:
                    sp.wait_ge(xn_ready, after(b * BT))
                    sp.wait_ge(we_ready, after((b - 1) * 2 + 1))
                    sp.dma_start(even[:, :], xn[1:16:2, 0, :]).then_inc(rows_in, 16)
                    sp.dma_start(odd[:, :], xn[2:17:2, 0, :]).then_inc(rows_in, 16)

            @block.tensor
            def _(pe):
                for s in (xt_ready, wp_ready, h_ready, o_ready, ot_ready):
                    pe.sem_inc(s, LEAD)

                def transpose_x(b):
                    for s in range(2):
                        pe.wait_ge(xn_ready, after(b * BT + 4 * s + 3))
                        pe.wait_ge(res.xo_ready, after((b - 2) * 2 + s))
                        for j in range(4):
                            last = pe.transpose(x_bank[s][:, j * P:(j + 1) * P], xn[:, 4 * s + j, :], t.ident)
                        last.then_inc(xt_ready, 1)

                def pair_products(b, layer):
                    if layer == 0:
                        pe.wait_ge(pairs_ready, after(b * 3 + 2))
                        pe.wait_ge(we_ready, after((b - 1) * 2 + 1))
                        for p in range(KC):
                            last = pe.matmul(w_bank[:, p * P:(p + 1) * P], odds[:, p, :], even[:, :], start=True, stop=True)
                    else:
                        pe.wait_ge(we_ready, after(b * 2))
                        for c in range(KC):
                            last = pe.matmul(w_bank[:, c * P:(c + 1) * P], odd[:, :], evenm[:, c, :, :], start=True, stop=True)
                    last.then_inc(wp_ready, 1)

                def start():
                    transpose_x(0)
                    for layer in range(2):
                        pair_products(0, layer)

                def run(b, more):
                    for s in range(2):
                        pe.wait_ge(xt_copied, after(b * 2 + s))
                        pe.wait_ge(we_ready, after(b * 2))
                        for c in range(KC):
                            pe.wait_ge(hid_ready, after((b * 2 + s - 1) * KC + c))
                            pe.matmul(h_bank[c][:, :], w1e[:, c * P:(c + 1) * P], xT[:, s * HALF:(s + 1) * HALF],
                                      start=True, stop=True).then_inc(h_ready, 1)
                    if more:
                        transpose_x(b + 1)
                        pair_products(b + 1, 0)
                    pe.wait_ge(we_ready, after(b * 2 + 1))
                    for s in range(2):
                        pe.wait_ge(o_copied, after(b * 2 + s - 1))
                        for c in range(KC):
                            pe.wait_ge(hid_ready, after((b * 2 + s) * KC + c))
                            last = pe.matmul(o_bank[:, :], w2e[:, c * P:(c + 1) * P], hid[:, s, c, :], start=c == 0, stop=c == KC - 1)
                        last.then_inc(o_ready, 1)
                    if more:
                        pair_products(b + 1, 1)
                    for s in range(2):
                        pe.wait_ge(o_copied, after(b * 2 + s))
                        if more:
                            pe.wait_ge(xt_copied, after((b + 1) * 2 + s))
                        else:
                            pe.wait_ge(res.xo_ready, after((b - 1) * 2 + s))
                        for j in range(4):
                            last = pe.transpose(x_bank[s][:, j * P:(j + 1) * P], oT[:, s, j * P:(j + 1) * P], t.ident)
                        last.then_inc(ot_ready, 1)

                pipeline(pe, start, run)

            @block.scalar
            def _(act):
                layernorm_scales(act, t, rstd_ready)
                for s in (xt_copied, hid_ready, o_copied):
                    act.sem_inc(s, LEAD)
                act.wait_ge(b2h_ready, 1)

                def copy_x(b):
                    for s in range(2):
                        act.wait_ge(xt_ready, after(b * 2 + s))
                        act.wait_ge(h_ready, after((b - 1) * 2 * KC + (s + 1) * KC - 1))
                        act.activation(xT[:, s * HALF:(s + 1) * HALF], x_bank[s][:, :], ACT.Copy).then_inc(xt_copied, 1)

                def run(b, more):
                    for s in range(2):
                        for c in range(KC):
                            act.wait_ge(h_ready, after((b * 2 + s) * KC + c))
                            act.wait_ge(o_ready, after((b - 1) * 2 + s))
                            act.activation(hid[:, s, c, :], h_bank[c][:, :], ACT.Gelu, bias=b1[:, c:c + 1]).then_inc(hid_ready, 1)
                    if more:
                        copy_x(b + 1)
                    for s in range(2):
                        act.wait_ge(o_ready, after(b * 2 + s))
                        act.wait_ge(ot_ready, after((b - 1) * 2 + s))
                        act.activation(oT[:, s, :], o_bank[:, :], ACT.Identity, bias=b2h[:, :], scale=0.5).then_inc(o_copied, 1)

                pipeline(act, lambda: copy_x(0), run)

            @block.vector
            def _(dve):
                layernorm_reciprocals(dve, t, rstd_ready)
                for s in (xn_ready, pairs_ready, we_ready):
                    dve.sem_inc(s, LEAD)
                res.prime(dve)
                dve.wait_ge(s_in, 16)
                dve.tensor_scalar(b2h[:, :], b2, 0.5, None, ALU.mult).then_inc(b2h_ready, 1)
                dve.wait_ge(w_in, 32)

                def normalise(b):
                    for j in range(BT):
                        if j % 4 == 0:
                            dve.wait_ge(xt_ready, after((b - 1) * 2 + j // 4))
                            if j == 0:
                                dve.wait_ge(pairs_ready, after((b - 1) * 3 + 2))
                        n = b * BT + j
                        dve.tensor_scalar(xn[:, j, :], t.X[:, at(n), :], t.stats[:, at(n), 0], t.rstd[:, at(n)],
                                          ALU.subtract, ALU.mult).then_inc(xn_ready, 1)

                def pairs(b):
                    dve.wait_ge(rows_in, (b + 1) * 32)
                    dve.scalar_tensor_tensor(odds[:, :, :], odd[:, :].unsqueeze(1).to_broadcast([8, KC, DIM]), scale,
                                             first_half.unsqueeze(2).to_broadcast([8, KC, DIM]), ALU.mult, ALU.mult).then_inc(pairs_ready, 1)
                    dve.tensor_scalar(evens[:, :], even[:, :], scale, None, ALU.mult).then_inc(pairs_ready, 1)
                    dve.wait_ge(pairs_ready, after(b * 3 + 1))
                    ev = evens[:, :].rearrange("k (i r) -> k r i", r=4).unsqueeze(2).to_broadcast([8, 4, 4, 32])
                    sh = second_half.unsqueeze(1).unsqueeze(3).to_broadcast([8, 4, 4, 32])
                    dve.tensor_tensor(evenm[:, :, :, :], ev, sh, ALU.mult).then_inc(pairs_ready, 1)

                def element_weights(b, layer):
                    dve.wait_ge(wp_ready, after(b * 2 + layer))
                    if layer == 0:
                        dve.wait_ge(h_ready, after(b * 2 * KC - 1))
                        dve.tensor_tensor(w1e[:, :], w_bank[:, :], w1[:, :], ALU.add).then_inc(we_ready, 1)
                    else:
                        dve.wait_ge(o_ready, after(b * 2 - 1))
                        dve.tensor_tensor(w2e[:, :], w_bank[:, :], w2[:, :], ALU.add).then_inc(we_ready, 1)

                def prepare(b):
                    normalise(b)
                    pairs(b)
                    for layer in range(2):
                        element_weights(b, layer)

                def run(b, more):
                    if more:
                        prepare(b + 1)
                    for s in range(2):
                        dve.wait_ge(ot_ready, after(b * 2 + s))
                        res.add(dve, b * 2 + s, s, b * BT + 4 * s, x_bank[s][:, :])

                pipeline(dve, lambda: prepare(0), run)
        sem.clear()


FFN_SMALL = 16


def ffn_weights(ctx, nc, t):
    t.w1 = ctx.enter_context(nc.sbuf_tensor("ffn_w1", [P, INNER], F32))
    t.w2 = ctx.enter_context(nc.sbuf_tensor("ffn_w2", [P, INNER], F32))
    t.ffn_small = ctx.enter_context(nc.sbuf_tensor("ffn_small", [P, FFN_SMALL], F32))
    t.ffn_in, t.ffn_small_in = [ctx.enter_context(nc.semaphore(name)) for name in ("ffn_in", "ffn_small_in")]


def ffn_load(sp, t, d):
    sp.dma_start(t.w1[:, :], d["w1"]).then_inc(t.ffn_in, 16)
    sp.dma_start(t.w2[:, :], d["w2"]).then_inc(t.ffn_in, 16)
    sp.dma_start(t.ffn_small[:, :], d["ffn_small"]).then_inc(t.ffn_small_in, 16)


def ffn_laid_out(np, a, r):
    r["w1"] = a["L1_ffn_W1"].T
    r["w2"] = a["L1_ffn_W2"].reshape(DIM, KC, P).transpose(2, 1, 0).reshape(P, INNER)
    small = np.zeros((P, FFN_SMALL), np.float32)
    small[:, 0:4] = a["L1_ffn_b1"].reshape(KC, P).T
    small[:, 4] = a["L1_ffn_b2"]
    small[:, 5] = a["L1_ffn_scale"]
    small[0:4, 8:12] = np.eye(4)
    small[4:8, 12:16] = np.eye(4)
    r["ffn_small"] = small


GW = 3 * P
ROW = 32
SLOPE, SHIFT, DIVISOR = -0.01, 100.0, 1000.0
BOUND = 99.0


def attn0_phase(nc, t, tag):
    with ExitStack() as ctx:
        def sb(name, shape, dt=F32):
            return ctx.enter_context(nc.sbuf_tensor(f"{tag}_{name}", shape, dt))

        sem = Semaphores(ctx, nc, tag)

        w32, wp, small, w_in = t.attn0_w, t.attn0_wp, t.attn0_small, t.attn0_in
        w = [sb(f"w{i}", [P, GROUPS, GW], F32R) for i in range(2)]
        k_low, q_low, q_ones, head_mask = small[:, 0:1], small[:, 1:2], small[:, 2:3], small[:, 4:8]
        first_rows = small[:, 3:4]
        state_mask, kv_ones, seen = small[:, 8:136], small[:, 136:392], small[:, 392:904]
        xn = sb("xn", [P, BT, DIM])
        xT = [sb(f"xT{i}", [P, SEQ], F32R) for i in range(2)]
        low = sb("low", [P, 2, HALF], F32R)
        kS = sb("kS", [P, SEQ], F32R)
        kM = [sb(f"kM{q}", [P, GH, SEQ], F32R) for q in range(2)]
        qS = [sb(f"qS{q}", [P, SEQ], F32R) for q in range(2)]
        KV = [sb(f"KV{q}", [P, BT, 2 * P]) for q in range(2)]
        run = sb("run", [P, BT, P])
        runm = sb("runm", [P, BT, P])
        runl = sb("runl", [P, BT, P], F32R)
        S = [sb(f"S{q}", [P, BT, P], F32R) for q in range(2)]
        R = sb("R", [P, 2, GH, HALF])
        R2 = sb("R2", [P, 2, HALF])
        L = sb("L", [P, 2, GH, HALF])
        yS = sb("yS", [P, GROUPS, SEQ])
        bound = sb("bound", [P, 2, 3])
        peak = sb("peak", [1, 2])
        flag = sb("flag", [1, 2], mybir.dt.int32)
        res = ResidualAdd(ctx, nc, sem, t, tag, 4)
        ps = [ctx.enter_context(nc.psum_tensor(f"{tag}_ps{i}", [P, HALF], F32)) for i in range(8)]
        e_bank, a_bank, y_bank, x_bank = ps[0:4], ps[4:6], ps[6], ps[7]

        w_high, w_low, rstd_ready, zero_ready = sem("w_high"), sem("w_low"), sem("rstd_ready"), sem("zero_ready")
        xn_ready, xt_ready, xh_ready, xl_ready = sem("xn_ready"), sem("xt_ready"), sem("xh_ready"), sem("xl_ready")
        ap_ready, t_ready, av_ready, run_ready = sem("ap_ready"), sem("t_ready"), sem("av_ready"), sem("run_ready")
        km_ready, runm_ready, runl_ready, S_ready = sem("km_ready"), sem("runm_ready"), sem("runl_ready"), sem("S_ready")
        s_ready, r_ready, u_ready, up_ready, rp_ready, l_ready, g_ready = (
            sem("s_ready"), sem("r_ready"), sem("u_ready"), sem("up_ready"), sem("rp_ready"), sem("l_ready"), sem("g_ready"))
        pv_ready, y_ready, yc_ready, o_ready = sem("pv_ready"), sem("y_ready"), sem("yc_ready"), sem("o_ready")
        pe_pause, act_pause, dve_pause, pool_pause = sem("pe_pause"), sem("act_pause"), sem("vector_pause"), sem("pool_pause")
        bound_ready, peak_ready, top_ready, flag_ready = sem("bound_ready"), sem("peak_ready"), sem("top_ready"), sem("flag_ready")
        cs_ready, cl_ready, cm_ready, cc_ready, cv_ready, cy_ready = (
            sem("cs_ready"), sem("cl_ready"), sem("cm_ready"), sem("cc_ready"), sem("cv_ready"), sem("cy_ready"))

        units = [(s, u) for s in range(2) for u in key_units(s)]
        NU, NQ0 = len(units), len(key_units(0))
        US = NU * GH
        PRODUCTS = ((0, 0), (1, 0), (0, 1))
        POOLED = range(NU - 3, NU)

        def dve_heads(u):
            return GH - 1 if u in POOLED else GH

        UD = [sum(dve_heads(v) for v in range(u)) for u in range(NU + 1)]
        PREP = [("k", 0), ("k", 1), ("kv", 0), ("kv", 1), ("kv", 2), ("kv", 3), ("q", 0), ("q", 1), ("run", 0), ("run", 1)]
        KMASKS = (4, 5, 8, 9)
        LOWS = {0: 0, 1: 1, 6: 2, 7: 3}

        def width(u):
            pieces = units[u][1]
            return pieces[0][3] if len(pieces) == 1 else HALF

        def correct(eng, pause, m, q, body, totals):
            eng.wait_ge(flag_ready, after(m))
            eng.sem_inc(pause, 1)
            may_be_low = eng.value_load(flag[0:1, q:q + 1], min_val=0, max_val=1)
            with eng.If(may_be_low):
                nc.disable_value_cache = True
                body()
                nc.disable_value_cache = False
            with eng.Else():
                for s, n in totals:
                    eng.sem_inc(s, n)

        def pipeline(eng, open_element, prepare, attend, finish):
            def element(b, more):
                for g in range(GROUPS):
                    m, has_next = b * GROUPS + g, more or g + 1 < GROUPS
                    nxt = (lambda k: prepare(m + 1, (g + 1) % GROUPS, k)) if has_next else (lambda k: None)
                    attend(m, g, nxt, b, more)
                finish(b, more)

            open_element(0)
            for k in range(NU):
                prepare(0, 0, k)
            with eng.Fori(0, BATCH - 1) as b:
                element(b, True)
            element(BATCH - 1, False)

        with nc.Block() as block:
            @block.gpsimd
            def _(pool):
                for s in (runm_ready, runl_ready, S_ready, g_ready, up_ready):
                    pool.sem_inc(s, LEAD)
                pool.memset(run[:, 0, :], 0.0).then_inc(zero_ready, 1)
                pool.wait_ge(w_in, 48)

                def prepare(m, g, k):
                    q = g % 2
                    if k == NU - 1:
                        pool.wait_ge(av_ready, after(m * NU + NU - 1))
                        pool.wait_ge(y_ready, after((m - 1) * 2 - 1))
                        pool.tensor_tensor(runm[:, :, :], run[:, :, :], state_mask.unsqueeze(1).to_broadcast([P, BT, P]),
                                           ALU.mult).then_inc(runm_ready, 1)
                        pool.wait_ge(runm_ready, after(m))
                        pool.sem_inc(pool_pause, 1)
                        pool.tensor_tensor(runl[:, :, :], runm[:, :, :], k_low.unsqueeze(2).to_broadcast([P, BT, P]),
                                           ALU.mult).then_inc(runl_ready, 1)
                        pool.wait_ge(runl_ready, after(m))
                        pool.tensor_tensor(S[q][:, :, :], runm[:, :, :], f32(runl[:, :, :]), ALU.subtract).then_inc(S_ready, 1)

                def attend(m, g, nxt, b, more):
                    for u in range(NU):
                        if units[u][1][0][4]:
                            s = units[u][0]
                            for j in range(GH):
                                n = m * 2 * GH + (GH if u else 0) + j
                                pool.wait_ge(l_ready, after(n))
                                pool.tensor_tensor(L[:, s, j, :], L[:, s, j, :], seen, ALU.mult).then_inc(g_ready, 1)
                        if u in POOLED:
                            pool.wait_ge(rp_ready, after(m * len(POOLED) + POOLED.index(u)))
                            r = R[:, u % 2, 0, HALF - width(u):HALF]
                            pool.tensor_tensor(r, r, R2[:, u % 2, HALF - width(u):HALF], ALU.mult).then_inc(up_ready, 1)
                        nxt(u)

                pipeline(pool, lambda b: None, prepare, attend, lambda b, more: None)

            @block.tensor
            def _(pe):
                for s in (xt_ready, ap_ready, s_ready, pv_ready, y_ready, o_ready, peak_ready, cs_ready, cv_ready):
                    pe.sem_inc(s, LEAD)
                pe.wait_ge(w_in, 48)
                pe.wait_ge(w_low, 1)

                def open_element(b):
                    pe.wait_ge(av_ready, after(b * GROUPS * NU - 1))
                    for s in range(2):
                        pe.wait_ge(xn_ready, after(b * BT + 4 * s + 3))
                        for j in range(4):
                            last = pe.transpose(a_bank[s][:, j * P:(j + 1) * P], xn[:, 4 * s + j, :], t.ident)
                        last.then_inc(xt_ready, 1)
                    if isinstance(b, int):
                        pe.wait_ge(xl_ready, after(1))

                def prepare(m, g, k):
                    q = g % 2
                    kind, i = PREP[k]
                    bank = a_bank[k % 2]
                    pe.wait_ge(av_ready, after(m * NU + k - 2))
                    if kind in "kq":
                        off = P if kind == "k" else 0
                        for n, (a, b_) in enumerate(PRODUCTS):
                            last = pe.matmul(bank[:, :], w[b_][:, g, off:off + P], xT[a][:, i * HALF:(i + 1) * HALF],
                                             start=n == 0, stop=n == 2)
                    elif kind == "kv":
                        for h in range(2):
                            j = 2 * i + h
                            for n, (a, b_) in enumerate(PRODUCTS):
                                last = pe.matmul(bank[:, h * 2 * P:(h + 1) * 2 * P], xT[a][:, j * P:(j + 1) * P], w[b_][:, g, P:GW],
                                                 start=n == 0, stop=n == 2)
                    else:
                        pe.wait_ge(av_ready, after(m * NU + 5))
                        for h in range(4 if i == 0 else 3):
                            j = 4 * i + h
                            last = pe.matmul(bank[:, h * P:(h + 1) * P], KV[q][:, j, 0:P], KV[q][:, j, P:2 * P], start=True, stop=True)
                    last.then_inc(ap_ready, 1)

                def scores(m, g, u):
                    q = g % 2
                    s, pieces = units[u]
                    for j in range(GH):
                        pe.wait_ge(r_ready, after(m * US + (u - 1) * GH + j))
                        diagonal = pieces[0][4]
                        for k, (kt, at_, qc, n, _) in enumerate(pieces):
                            last = pe.matmul(e_bank[j][:, at_:at_ + n], kM[q][:, j, kt * P:(kt + 1) * P],
                                             qS[q][:, s * HALF + qc:s * HALF + qc + n], start=not diagonal or k == 0,
                                             stop=not diagonal, skip_group_check=diagonal)
                        if diagonal:
                            last = pe.matmul(e_bank[j][:, :], t.identb, t.neg_kq, start=False, stop=True, skip_group_check=True)
                        last.then_inc(s_ready, 1)

                def values(m, g, u):
                    q = g % 2
                    s, pieces = units[u]
                    first, end = u in (0, NQ0), u in (NQ0 - 1, NU - 1)
                    if first:
                        pe.wait_ge(yc_ready, after(m * 2 + s - 1))
                    pe.wait_ge(u_ready, after(m * UD[NU] + UD[u + 1] - 1))
                    if u in POOLED:
                        pe.wait_ge(up_ready, after(m * len(POOLED) + POOLED.index(u)))
                    for k, (kt, at_, qc, n, diagonal) in enumerate(pieces):
                        for j in range(GH):
                            rows = slice(j * ROW, (j + 1) * ROW)
                            last = pe.matmul(y_bank[rows, qc:qc + n], KV[q][:, kt, P + j * ROW:P + (j + 1) * ROW],
                                             R[:, u % 2, j, at_:at_ + n], start=first and k == 0, stop=False, skip_group_check=True)
                    last.then_inc(pv_ready, 1)
                    if end:
                        pe.wait_ge(g_ready, after((m * 2 + s) * GH + GH - 1))
                        for kt, at_, qc, n, _ in key_units(s)[0]:
                            for j in range(GH):
                                rows = slice(j * ROW, (j + 1) * ROW)
                                pe.matmul(y_bank[rows, qc:qc + n], KV[q][:, kt, P + j * ROW:P + (j + 1) * ROW],
                                          L[:, s, j, at_:at_ + n], start=False, stop=False, skip_group_check=True)
                        pe.wait_ge(S_ready, after(m))
                        chunks = [c for c in range(4 * s, 4 * s + 4) if c]
                        for c in chunks:
                            last = pe.matmul(y_bank[:, (c % 4) * P:(c % 4 + 1) * P], S[q][:, c, :], qS[q][:, c * P:(c + 1) * P],
                                             start=False, stop=c == chunks[-1], skip_group_check=True)
                        last.then_inc(y_ready, 1)

                def attend(m, g, nxt, b, more):
                    pe.wait_ge(km_ready, after(m * GH + GH - 1))
                    pe.wait_ge(av_ready, after(m * NU + NU - 1))
                    for u in range(NU):
                        scores(m, g, u)
                        if u == 0 and g == GROUPS - 1 and more:
                            pe.wait_ge(xl_ready, after(b * 2 + 3))
                        if u == 0 and g == 0:
                            pe.wait_ge(res.xo_ready, after(b * 2 - 1))
                        nxt(u)
                        if u == 4:
                            pe.wait_ge(bound_ready, after(m * 3 + 2))
                            pe.wait_ge(flag_ready, after(m - 1))
                            pe.matmul(x_bank[0:1, 0:GH], bound[:, g % 2, 2:3], head_mask, start=True, stop=True).then_inc(peak_ready, 1)
                        if u >= 1:
                            values(m, g, u - 1)
                    if more and g == GROUPS - 2:
                        open_element(b + 1)
                    values(m, g, NU - 1)
                    correct(pe, pe_pause, m, g % 2, lambda: low_scores(m, g), ((cs_ready, US), (cv_ready, NU)))

                def low_scores(m, g):
                    q = g % 2
                    for u in range(NU):
                        s, pieces = units[u]
                        for j in range(GH):
                            pe.wait_ge(cc_ready, after(m * US + (u - 1) * GH + j))
                            for kt, at_, qc, n, _ in pieces:
                                last = pe.matmul(e_bank[j][:, at_:at_ + n], kM[q][:, j, kt * P:(kt + 1) * P],
                                                 qS[q][:, s * HALF + qc:s * HALF + qc + n], start=True, stop=True)
                            last.then_inc(cs_ready, 1)
                        if u == 0:
                            pe.wait_ge(yc_ready, after(m * 2 + 1))
                        if u == NQ0:
                            pe.wait_ge(cy_ready, after(m * 2))
                        pe.wait_ge(cc_ready, after(m * US + u * GH + GH - 1))
                        for k, (kt, at_, qc, n, _) in enumerate(pieces):
                            for j in range(GH):
                                rows = slice(j * ROW, (j + 1) * ROW)
                                last = pe.matmul(y_bank[rows, qc:qc + n], KV[q][:, kt, P + j * ROW:P + (j + 1) * ROW],
                                                 R[:, 0, j, at_:at_ + n], start=u in (0, NQ0) and k == 0,
                                                 stop=u in (NQ0 - 1, NU - 1), skip_group_check=True)
                        last.then_inc(cv_ready, 1)
                    pe.wait_ge(cy_ready, after(m * 2 + 1))

                def finish(b, more):
                    pe.wait_ge(yc_ready, after((b + 1) * GROUPS * 2 - 1))
                    pe.wait_ge(cy_ready, after((b + 1) * GROUPS * 2 - 1))
                    pe.wait_ge(av_ready, after((b + 1) * GROUPS * NU + (NU - 1 if more else -1)))
                    for s in range(2):
                        for j in range(4):
                            for g in range(GROUPS):
                                c = s * HALF + j * P
                                last = pe.matmul(a_bank[s][:, j * P:(j + 1) * P], yS[:, g, c:c + P], wp[:, g * DIM:(g + 1) * DIM],
                                                 start=g == 0, stop=g == GROUPS - 1)
                        last.then_inc(o_ready, 1)

                pipeline(pe, open_element, prepare, attend, finish)

            @block.scalar
            def _(act):
                layernorm_scales(act, t, rstd_ready)
                for s in (xh_ready, t_ready, r_ready, rp_ready, l_ready, km_ready, yc_ready, cl_ready):
                    act.sem_inc(s, LEAD)
                act.wait_ge(w_in, 48)
                act.activation(w[0][:, :, 0:P], w32[:, :, 0:P], ACT.Copy, scale=SCORE_SCALE)
                act.activation(w[0][:, :, P:GW], w32[:, :, P:GW], ACT.Copy).then_inc(w_high, 1)

                def open_element(b):
                    for s in range(2):
                        act.wait_ge(xt_ready, after(b * 2 + s))
                        act.wait_ge(ap_ready, after(b * GROUPS * NU - 1))
                        act.activation(xT[0][:, s * HALF:(s + 1) * HALF], a_bank[s][:, :], ACT.Copy).then_inc(xh_ready, 1)

                def prepare(m, g, k):
                    if k in LOWS:
                        act.wait_ge(ap_ready, after(m * NU + k))
                        act.wait_ge(av_ready, after(m * NU + k - 2))
                        act.activation(low[:, k % 2, :], a_bank[k % 2][:, :], ACT.Copy,
                                       scale=k_low if PREP[k][0] == "k" else q_low).then_inc(t_ready, 1)
                    if k in KMASKS:
                        j = KMASKS.index(k)
                        if j == 0:
                            act.wait_ge(av_ready, after(m * NU + 1))
                            act.wait_ge(s_ready, after((m - 1) * US - 1))
                        act.activation(kM[g % 2][:, j, :], f32(kS[:, :]), ACT.Copy, scale=head_mask[:, j:j + 1]).then_inc(km_ready, 1)

                def copy_out(m, g, s):
                    act.wait_ge(y_ready, after(m * 2 + s))
                    act.activation(yS[:, g, s * HALF:(s + 1) * HALF], y_bank[:, :], ACT.Copy, scale=1.0 / DIVISOR).then_inc(yc_ready, 1)

                def attend(m, g, nxt, b, more):
                    for u in range(NU):
                        pieces, n = units[u][1], width(u)
                        for j in range(GH):
                            act.wait_ge(s_ready, after(m * US + u * GH + j))
                            if j == 0:
                                act.wait_ge(pv_ready, after(m * NU + u - 2))
                            if pieces[0][4]:
                                if j == 0:
                                    act.wait_ge(y_ready, after((m - 1) * 2 + units[u][0]))
                                act.activation(L[:, units[u][0], j, :], e_bank[j][:, :], ACT.Copy, bias=1.0, scale=SLOPE).then_inc(l_ready, 1)
                            act.activation(R[:, u % 2, j, HALF - n:HALF], e_bank[j][:, HALF - n:HALF], ACT.Relu).then_inc(r_ready, 1)
                            if j == 1 and u in POOLED:
                                act.wait_ge(r_ready, after(m * US + u * GH))
                                act.activation(R2[:, u % 2, HALF - n:HALF], R[:, u % 2, 0, HALF - n:HALF], ACT.Copy,
                                               bias=-SLOPE).then_inc(rp_ready, 1)
                        nxt(u)
                        if u == NQ0:
                            copy_out(m, g, 0)
                    if more and g == GROUPS - 2:
                        open_element(b + 1)
                    copy_out(m, g, 1)
                    correct(act, act_pause, m, g % 2, lambda: low_terms(m), ((cl_ready, US),))

                def low_terms(m):
                    for u in range(NU):
                        n = width(u)
                        for j in range(GH):
                            act.wait_ge(cs_ready, after(m * US + u * GH + j))
                            act.wait_ge(cc_ready, after(m * US + (u - 1) * GH + j))
                            act.activation(L[:, 0, j, HALF - n:HALF], e_bank[j][:, HALF - n:HALF], ACT.Copy, bias=-1.0,
                                           scale=-SLOPE).then_inc(cl_ready, 1)

                pipeline(act, open_element, prepare, attend, lambda b, more: None)

            @block.vector
            def _(dve):
                layernorm_reciprocals(dve, t, rstd_ready)
                for s in (xn_ready, xl_ready, av_ready, run_ready, u_ready, bound_ready, top_ready,
                          flag_ready, cm_ready, cc_ready, cy_ready):
                    dve.sem_inc(s, LEAD)
                res.prime(dve)
                dve.wait_ge(w_high, 1)
                dve.wait_ge(zero_ready, 1)
                dve.scalar_tensor_tensor(w[1][:, :, 0:P], w32[:, :, 0:P], SCORE_SCALE, f32(w[0][:, :, 0:P]), ALU.mult, ALU.subtract)
                dve.tensor_tensor(w[1][:, :, P:GW], w32[:, :, P:GW], f32(w[0][:, :, P:GW]), ALU.subtract).then_inc(w_low, 1)

                def normalise(b):
                    for j in range(BT):
                        if j % 4 == 0:
                            dve.wait_ge(xt_ready, after((b - 1) * 2 + j // 4))
                        n = b * BT + j
                        dve.tensor_scalar(xn[:, j, :], t.X[:, at(n), :], t.stats[:, at(n), 0], t.rstd[:, at(n)],
                                          ALU.subtract, ALU.mult).then_inc(xn_ready, 1)

                def open_element(b):
                    for s in range(2):
                        half = slice(s * HALF, (s + 1) * HALF)
                        dve.wait_ge(xh_ready, after(b * 2 + s))
                        dve.tensor_tensor(xT[1][:, half], a_bank[s][:, :], f32(xT[0][:, half]), ALU.subtract).then_inc(xl_ready, 1)

                def prepare(m, g, k):
                    q = g % 2
                    kind, i = PREP[k]
                    bank = a_bank[k % 2]
                    half = slice(i * HALF, (i + 1) * HALF)
                    if k in LOWS:
                        dve.wait_ge(t_ready, after(m * 4 + LOWS[k]))
                    else:
                        dve.wait_ge(ap_ready, after(m * NU + k))
                    if kind == "k":
                        dve.wait_ge(km_ready, after(m * GH - 1))
                        ins = dve.tensor_tensor(kS[:, half], bank[:, :], f32(low[:, k % 2, :]), ALU.subtract)
                    elif kind == "q":
                        dve.wait_ge(y_ready, after((m - 1) * 2 - 1))
                        ins = dve.scalar_tensor_tensor(qS[q][:, half], bank[:, :], q_ones, f32(low[:, k % 2, :]), ALU.add, ALU.subtract)
                    elif kind == "kv":
                        dve.wait_ge(y_ready, after((m - 1) * 2 - 1))
                        ins = dve.tensor_tensor(KV[q][:, 2 * i:2 * i + 2, :], bank[:, :].rearrange("p (j n) -> p j n", n=2 * P),
                                                kv_ones.unsqueeze(1).to_broadcast([P, 2, 2 * P]), ALU.add)
                    else:
                        dve.wait_ge(runm_ready, after(m - 1))
                        for h in range(4 if i == 0 else 3):
                            c = 4 * i + h
                            if c == 4:
                                dve.wait_ge(av_ready, after(m * NU + k - 1))
                            elif c:
                                dve.wait_ge(run_ready, after(m * 5 + c - 1 - (c > 4)))
                            ins = dve.tensor_tensor(run[:, c + 1, :], bank[:, h * P:(h + 1) * P], run[:, c, :], ALU.add)
                            if h != (3 if i == 0 else 2):
                                ins.then_inc(run_ready, 1)
                    ins.then_inc(av_ready, 1)
                    if k == 4:
                        dve.wait_ge(av_ready, after(m * NU + 1))
                        dve.reduce_max(bound[:, q, 0:1], f32(kS[:, :]), AX.X, apply_absolute_value=True).then_inc(bound_ready, 1)

                def bound_scores(m, q, u):
                    if u == 1:
                        dve.wait_ge(av_ready, after(m * NU + 7))
                        dve.reduce_max(bound[:, q, 1:2], f32(qS[q][:, :]), AX.X, apply_absolute_value=True).then_inc(bound_ready, 1)
                    if u == 2:
                        dve.wait_ge(bound_ready, after(m * 3 + 1))
                        dve.scalar_tensor_tensor(bound[:, q, 2:3], bound[:, q, 0:1], bound[:, q, 1:2], first_rows,
                                                 ALU.mult, ALU.mult).then_inc(bound_ready, 1)
                    if u == 6:
                        dve.wait_ge(peak_ready, after(m))
                        dve.reduce_max(peak[:, q:q + 1], x_bank[0:1, 0:GH], AX.X).then_inc(top_ready, 1)
                    if u == 7:
                        dve.wait_ge(top_ready, after(m))
                        dve.tensor_scalar(flag[:, q:q + 1], peak[:, q:q + 1], BOUND, None, ALU.is_ge).then_inc(flag_ready, 1)

                def attend(m, g, nxt, b, more):
                    for u in range(NU):
                        pieces, n = units[u][1], width(u)
                        for j in range(GH):
                            if j == 0 and u in POOLED:
                                continue
                            dve.wait_ge(r_ready, after(m * US + u * GH + j))
                            r = R[:, u % 2, j, HALF - n:HALF]
                            dve.scalar_tensor_tensor(r, r, -SLOPE, r, ALU.add, ALU.mult).then_inc(u_ready, 1)
                        nxt(u)
                        bound_scores(m, g % 2, u)
                        if more and g == GROUPS - 2 and u == NQ0:
                            normalise(b + 1)
                    if more and g == GROUPS - 2:
                        open_element(b + 1)
                    correct(dve, dve_pause, m, g % 2, lambda: low_weights(m, g), ((cc_ready, US), (cm_ready, 2 * GH), (cy_ready, 2)))

                def low_weights(m, g):
                    for u in range(NU):
                        n = width(u)
                        for j in range(GH):
                            dve.wait_ge(cl_ready, after(m * US + u * GH + j))
                            if j == 0:
                                dve.wait_ge(cv_ready, after(m * NU + u - 1))
                            c = R[:, 0, j, HALF - n:HALF]
                            ins = dve.scalar_tensor_tensor(c, e_bank[j][:, HALF - n:HALF], -SHIFT, L[:, 0, j, HALF - n:HALF],
                                                           ALU.is_lt, ALU.mult)
                            if units[u][1][0][4]:
                                ins.then_inc(cm_ready, 1)
                                dve.wait_ge(cm_ready, after(m * 2 * GH + (GH if u else 0) + j))
                                ins = dve.tensor_tensor(c, c, seen, ALU.mult)
                            ins.then_inc(cc_ready, 1)
                        if u in (NQ0 - 1, NU - 1):
                            s = units[u][0]
                            dve.wait_ge(cv_ready, after(m * NU + u))
                            y = yS[:, g, s * HALF:(s + 1) * HALF]
                            dve.scalar_tensor_tensor(y, y_bank[:, :], 1.0 / DIVISOR, y, ALU.mult, ALU.add).then_inc(cy_ready, 1)

                def finish(b, more):
                    for s in range(2):
                        dve.wait_ge(o_ready, after(b * 2 + s))
                        res.add(dve, b * 2 + s, s, b * BT + 4 * s, a_bank[s][:, :])

                normalise(0)
                pipeline(dve, open_element, prepare, attend, finish)
        sem.clear()


A0_SMALL = 904


def attn0_weights(ctx, nc, t):
    t.attn0_w = ctx.enter_context(nc.sbuf_tensor("attn0_w", [P, GROUPS, GW], F32))
    t.attn0_wp = ctx.enter_context(nc.sbuf_tensor("attn0_wp", [P, GROUPS * DIM], F32))
    t.attn0_small = ctx.enter_context(nc.sbuf_tensor("attn0_small", [P, A0_SMALL], F32))
    t.attn0_in = ctx.enter_context(nc.semaphore("attn0_in"))


def attn0_load(sp, t, d):
    sp.dma_start(t.attn0_w[:, :, :], d["wqkv"].rearrange("p (g n) -> p g n", g=GROUPS)).then_inc(t.attn0_in, 16)
    sp.dma_start(t.attn0_wp[:, :], d["wproj"]).then_inc(t.attn0_in, 16)
    sp.dma_start(t.attn0_small[:, :], d["attn0_small"]).then_inc(t.attn0_in, 16)


def attn0_laid_out(np, a, r):
    wqkv = a["L0_attn_W_attn"].reshape(DIM, 3, GROUPS, GH, HD)
    w = np.zeros((DIM, GROUPS, 3, GH, ROW), np.float32)
    for part in range(3):
        w[:, :, 0:2, :, part * HD:(part + 1) * HD] = wqkv[:, 0:2].transpose(0, 2, 1, 3, 4)
    w[:, :, 2, :, 0:HD] = wqkv[:, 2]
    r["wqkv"] = w.reshape(P, GROUPS * GW)
    wp = np.zeros((GROUPS, GH, ROW, DIM), np.float32)
    wp[:, :, 0:HD] = a["L0_attn_W_proj"].reshape(GROUPS, GH, HD, DIM)
    r["wproj"] = wp.transpose(1, 2, 0, 3).reshape(P, GROUPS * DIM)
    row, col = np.arange(P) % ROW, np.arange(P)
    small = np.zeros((P, A0_SMALL), np.float32)
    small[:, 0] = ((row >= HD) & (row < 2 * HD)) | (row == 25)
    small[:, 1] = (row >= 2 * HD) & (row < 3 * HD)
    small[:, 2] = (row == 24) | (row == 25)
    small[:, 3] = row < HD
    small[:, 4:8] = np.arange(P)[:, None] // ROW == np.arange(GH)
    same = (np.arange(P)[:, None] // ROW) == (col[None, :] // ROW)
    small[:, 8:136] = same * np.where(row < 24, SLOPE, 1.0)[:, None]
    small[:, 136:264] = ((row == 24) | (row == 25))[None, :]
    small[:, 392:904] = np.tile(np.triu(np.ones((P, P))), (1, 4))
    r["attn0_small"] = small


PAIRS = HEADS // 2
STACK = 3 * LAT
KROWS = STACK + 2
ZW = 5 * P
VW = 64
L1_COLS = 2 * LAT + 8 + 4 * HEADS


def key_units(s):
    k = 4 * s
    diagonal = [(k + i, i * P, i * P, P, True) for i in range(4)]
    split = [(k, P, P, 3 * P, False), (k + 2, 0, 3 * P, P, False)]
    half = [(k + 1, 2 * P, 2 * P, 2 * P, False)]
    return [diagonal, split, half] + [[(i, 0, 0, HALF, False)] for i in range(k)]


def attn1_phase(nc, t, tag):
    with ExitStack() as ctx:
        def sb(name, shape, dt=F32):
            return ctx.enter_context(nc.sbuf_tensor(f"{tag}_{name}", shape, dt))

        sem = Semaphores(ctx, nc, tag)

        wd32, lat32, wo, cols, w_in = t.wd, t.latent, t.wo, t.attn1_small, t.attn1_in
        wd = [sb(f"wd{i}", [P, HEADS * STACK], F32R) for i in range(2)]
        lat = [sb(f"lat{i}", [P, STACK], F32R) for i in range(2)]
        v_bias, k_bias, k_low, q_low = cols[:, 0:LAT], cols[0:STACK, 36:37], cols[0:STACK, 37:38], cols[0:STACK, 38:39]
        q_bias = cols[0:STACK, 40:40 + HEADS]
        k_lbias = sb("k_lbias", [STACK, 1])
        qb_low = sb("qb_low", [STACK, HEADS])
        xn = sb("xn", [P, BT, DIM])
        xT = [sb(f"xT{i}", [P, SEQ], F32R) for i in range(2)]
        kT = sb("kT", [STACK, 2, HALF], F32R)
        kS = sb("kS", [KROWS, SEQ], F32R)
        V = sb("V", [P, BT, VW])
        kN = sb("kN", [STACK, SEQ], F32R)
        VN = sb("VN", [P, BT, LAT])
        wcur = sb("wcur", [P, 2, 2 * STACK], F32R)
        bcur = sb("bcur", [STACK, 2, 2])
        qT = sb("qT", [STACK, 2, HALF], F32R)
        qS = [[sb(f"qS{q}{c}", [KROWS, SEQ], F32R) for c in range(2)] for q in range(2)]
        mx = sb("mx", [P, 2, 16])
        mh = sb("mh", [16, 2, P], F32R)
        ml = sb("ml", [16, 2, P], F32R)
        probs = sb("probs", [P, 2, 2, HALF])
        yT = sb("yT", [P, PAIRS, SEQ])
        rcp = sb("rcp", [P, 2, HEADS])
        z = sb("z", [P, 2, ZW])
        zT = sb("zT", [P, 2, ZW])
        res = ResidualAdd(ctx, nc, sem, t, tag, 1)
        m_all = ctx.enter_context(nc.psum_tensor(f"{tag}_psm", [P, 4 * HALF], F32))
        m_bank = [m_all[:, i * HALF:(i + 1) * HALF] for i in range(4)]
        e_bank = [ctx.enter_context(nc.psum_tensor(f"{tag}_pse{i}", [P, HALF], F32)) for i in range(2)]
        y_bank = ctx.enter_context(nc.psum_tensor(f"{tag}_psy", [P, HALF], F32))
        o_bank = ctx.enter_context(nc.psum_tensor(f"{tag}_pso", [P, HALF], F32))

        k_in, w_high, w_low, rstd_ready = sem("k_in"), sem("w_high"), sem("w_low"), sem("rstd_ready")
        minus = sb("minus", [2, SEQ], F32R)
        const_ready, minus_ready = sem("const_ready"), sem("minus_ready")
        xn_ready, xt_ready, xh_ready, xl_ready = sem("xn_ready"), sem("xt_ready"), sem("xh_ready"), sem("xl_ready")
        kp_ready, kt_ready, ks_ready, vp_ready, v_ready = (
            sem("kp_ready"), sem("kt_ready"), sem("ks_ready"), sem("vp_ready"), sem("v_ready"))
        wq_ready, qp_ready, qt_ready, qs_ready = sem("wq_ready"), sem("qp_ready"), sem("qt_ready"), sem("qs_ready")
        sm_ready, mx_ready, mt_ready, mh_ready, ml_ready, m_in = (
            sem("sm_ready"), sem("mx_ready"), sem("mt_ready"), sem("mh_ready"), sem("ml_ready"), sem("m_in"))
        s_ready, p_ready, pv_ready, y_ready, yc_ready = (
            sem("s_ready"), sem("p_ready"), sem("pv_ready"), sem("y_ready"), sem("yc_ready"))
        zt_ready, r_ready, z_ready, zz_ready, zc_ready, o_ready = (
            sem("zt_ready"), sem("r_ready"), sem("z_ready"), sem("zz_ready"), sem("zc_ready"), sem("o_ready"))
        kc_ready, act_pause, pool_pause = sem("kc_ready"), sem("act_pause"), sem("pool_pause")

        units = [(s, u) for s in range(2) for u in key_units(s)]
        NU = len(units)
        NQ0 = len(key_units(0))
        PRODUCTS = ((0, 0), (1, 0), (0, 1))

        def pipeline(eng, start, pair, finish):
            def element(b, more):
                with eng.Fori(0, PAIRS // 2 - 1) as i:
                    for q in range(2):
                        pair(b * PAIRS + i * 2 + q, q, i * 2 + q, b, (True, True))
                pair(b * PAIRS + PAIRS - 2, 0, PAIRS - 2, b, (True, more))
                pair(b * PAIRS + PAIRS - 1, 1, PAIRS - 1, b, (more, more))
                finish(b, more)

            start()
            with eng.Fori(0, BATCH - 1) as b:
                element(b, True)
            element(BATCH - 1, False)

        def opens(i, ahead):
            return isinstance(i, int) and i == PAIRS - 2 and ahead[1]

        MAXIMA = (range(0, 4), range(4, 6), range(6, 7), range(7, 9), range(9, 12), range(12, 14), range(14, 16))

        with nc.Block() as block:
            @block.sync
            def _(sp):
                sp.wait_ge(minus_ready, 1)
                sp.dma_start(f32(kS[STACK:KROWS, :]), f32(minus[:, :])).then_inc(k_in, 16)

                def maxima(m, q):
                    sp.wait_ge(ml_ready, after(m))
                    for c in range(2):
                        sp.dma_start(f32(qS[q][c][STACK:STACK + 1, :]), f32(mh[8 * c:8 * c + 8, q, :])).then_inc(m_in, 16)
                        sp.dma_start(f32(qS[q][c][STACK + 1:STACK + 2, :]), f32(ml[8 * c:8 * c + 8, q, :])).then_inc(m_in, 16)

                def pair(m, q, i, b, ahead):
                    if ahead[0]:
                        maxima(m + 1, 1 - q)

                pipeline(sp, lambda: maxima(0, 0), pair, lambda b, more: None)

            @block.gpsimd
            def _(pool):
                for s in (wq_ready, kc_ready):
                    pool.sem_inc(s, LEAD)
                pool.memset(V[:, :, LAT:VW], 0.0)
                pool.memset(z[:, :, HEADS * LAT:ZW], 0.0).then_inc(const_ready, 1)
                pool.wait_ge(const_ready, 1)
                pool.memset(V[:, :, LAT:LAT + 1], 1.0)
                pool.memset(z[:, :, HEADS * LAT:HEADS * LAT + 1], 1.0).then_inc(const_ready, 1)
                pool.wait_ge(w_low, 2)

                def weights(m, i):
                    pool.wait_ge(qs_ready, after(m * 4 - 1))
                    pool.sem_inc(pool_pause, 1)
                    for k in range(2):
                        pool.tensor_copy(wcur[:, k, :], wd[k][:, bass.ds(i * 2 * STACK, 2 * STACK)])
                    pool.tensor_copy(bcur[:, 0, :], q_bias[:, bass.ds(i * 2, 2)])
                    pool.tensor_copy(bcur[:, 1, :], qb_low[:, bass.ds(i * 2, 2)]).then_inc(wq_ready, 1)

                def take_over(b):
                    pool.wait_ge(ks_ready, after(b * 2 + 1))
                    pool.wait_ge(v_ready, after(b))
                    pool.wait_ge(s_ready, after(b * PAIRS * 2 * NU - 1))
                    pool.wait_ge(y_ready, after(b * PAIRS * 2 - 1))
                    pool.sem_inc(pool_pause, 1)
                    pool.tensor_copy(kS[0:STACK, :], kN[:, :])
                    pool.tensor_copy(V[:, :, 0:LAT], VN[:, :, :]).then_inc(kc_ready, 1)

                def start():
                    weights(0, 0)
                    weights(1, 1)
                    take_over(0)

                def pair(m, q, i, b, ahead):
                    if ahead[1]:
                        weights(m + 2, (i + 2) % PAIRS if isinstance(i, int) else i + 2)

                pipeline(pool, start, pair, lambda b, more: take_over(b + 1) if more else None)

            @block.tensor
            def _(pe):
                for s in (xt_ready, kp_ready, vp_ready, qp_ready, sm_ready, mt_ready, s_ready, pv_ready, y_ready,
                          zt_ready, zz_ready, o_ready):
                    pe.sem_inc(s, LEAD)
                pe.wait_ge(w_in, 64)
                pe.wait_ge(w_low, 2)
                pe.wait_ge(k_in, 16)
                pe.wait_ge(const_ready, 2)

                def transpose_x(b):
                    for s in range(2):
                        pe.wait_ge(xn_ready, after(b * BT + 4 * s + 3))
                        pe.wait_ge(mx_ready, after(b * PAIRS * 16 - 1))
                        for j in range(4):
                            last = pe.transpose(m_bank[s][:, j * P:(j + 1) * P], xn[:, 4 * s + j, :], t.ident)
                        last.then_inc(xt_ready, 1)

                def latents(b):
                    for s in range(2):
                        pe.wait_ge(xl_ready, after(b * 2 + s))
                        for k, (a, w) in enumerate(PRODUCTS):
                            last = pe.matmul(m_bank[2 + s][0:STACK, :], lat[w][:, :], xT[a][:, s * HALF:(s + 1) * HALF],
                                             start=k == 0, stop=k == 2)
                        last.then_inc(kp_ready, 1)

                def latent_rows(b):
                    pe.wait_ge(ml_ready, after(b * PAIRS - 1))
                    for j in range(BT):
                        for k, (a, w) in enumerate(PRODUCTS):
                            last = pe.matmul(o_bank[:, j * VW:j * VW + LAT], xT[a][:, j * P:(j + 1) * P], lat[w][:, 0:LAT],
                                             start=k == 0, stop=k == 2)
                    last.then_inc(vp_ready, 1)
                    pe.wait_ge(ks_ready, after(b * 2 + 1))

                def project(m, c):
                    pe.wait_ge(wq_ready, after(m))
                    pe.wait_ge(mx_ready, after((m - 1) * 16 + 15))
                    for s in range(2):
                        for k, (a, w) in enumerate(PRODUCTS):
                            last = pe.matmul(m_bank[2 * c + s][0:STACK, :], wcur[:, w, c * STACK:(c + 1) * STACK],
                                             xT[a][:, s * HALF:(s + 1) * HALF], start=k == 0, stop=k == 2)
                        last.then_inc(qp_ready, 1)

                def scores_max(m, q, v, keys):
                    c, j = v // 8, v % 8
                    if v < 2:
                        pe.wait_ge(qs_ready, after(m * 4 + 1 + 2 * v))
                    else:
                        pe.wait_ge(mx_ready, after(m * 16 + v - 2))
                    base = (v % 2) * 2 * HALF
                    for lo in range(0, (j + 1) * P, HALF):
                        hi = min(lo + HALF, (j + 1) * P)
                        pe.matmul(m_all[:, base + lo:base + hi], qS[q][c][0:STACK, j * P:(j + 1) * P], keys[0:STACK, lo:hi],
                                  start=True, stop=hi < (j + 1) * P)
                    pe.matmul(m_all[:, base + j * P:base + (j + 1) * P], t.identb, t.neg_qk, start=False, stop=True).then_inc(sm_ready, 1)

                def transpose_max(m, q):
                    pe.wait_ge(mx_ready, after(m * 16 + 15))
                    pe.wait_ge(ml_ready, after(m - 1))
                    pe.transpose(o_bank[0:16, 0:P], mx[:, q, :], t.ident).then_inc(mt_ready, 1)

                def scores(m, q, u):
                    s, pieces = units[u]
                    for c in range(2):
                        pe.wait_ge(p_ready, after(m * 2 * NU + 2 * (u - 1) + c))
                        diagonal = pieces[0][4]
                        for k, (kt, at_, qc, n, _) in enumerate(pieces):
                            last = pe.matmul(e_bank[c][:, at_:at_ + n], kS[:, kt * P:(kt + 1) * P],
                                             qS[q][c][:, s * HALF + qc:s * HALF + qc + n], start=True if not diagonal else k == 0,
                                             stop=not diagonal, skip_group_check=diagonal)
                        if diagonal:
                            last = pe.matmul(e_bank[c][:, :], t.identb, t.neg_kq, start=False, stop=True, skip_group_check=True)
                        last.then_inc(s_ready, 1)

                def values(m, q, u):
                    s, pieces = units[u]
                    first = u in (0, NQ0)
                    if first:
                        pe.wait_ge(yc_ready, after(m * 2 + s - 1))
                    pe.wait_ge(p_ready, after(m * 2 * NU + 2 * u + 1))
                    end = u in (NQ0 - 1, NU - 1)
                    for k, (kt, at_, qc, n, _) in enumerate(pieces):
                        for c in range(2):
                            last = pe.matmul(y_bank[VW * c:VW * (c + 1), qc:qc + n], V[:, kt, :], probs[:, u % 2, c, at_:at_ + n],
                                             start=first and k == 0, stop=end, skip_group_check=True)
                    last.then_inc(y_ready if end else pv_ready, 1)

                def start():
                    transpose_x(0)
                    latents(0)
                    latent_rows(0)
                    for c in range(2):
                        project(0, c)
                    for v in range(16):
                        scores_max(0, 0, v, kN)
                    pe.wait_ge(v_ready, after(0))
                    transpose_max(0, 0)
                    for c in range(2):
                        project(1, c)
                    pe.wait_ge(kc_ready, after(0))

                def pair(m, q, i, b, ahead):
                    last_pair = isinstance(i, int) and i == PAIRS - 1
                    pe.wait_ge(m_in, (m + 1) * 64)
                    for u in range(NU):
                        scores(m, q, u)
                        if ahead[0]:
                            for v in MAXIMA[u] if u < len(MAXIMA) else ():
                                scores_max(m + 1, 1 - q, v, kN if last_pair else kS)
                            if u == NU - 2:
                                if last_pair:
                                    pe.wait_ge(v_ready, after(b + 1))
                                transpose_max(m + 1, 1 - q)
                        if opens(i, ahead):
                            if u == NU - 2:
                                transpose_x(b + 1)
                            if u == NU - 1:
                                latents(b + 1)
                        if u == NU - 1 and ahead[1] and not opens(i, ahead):
                            project(m + 2, 1)
                        if u >= 1:
                            values(m, q, u - 1)
                        if opens(i, ahead) and u == NU - 1:
                            latent_rows(b + 1)
                        if ahead[1] and not opens(i, ahead) and u == NU - 2:
                            project(m + 2, 0)
                    if opens(i, ahead):
                        for c in range(2):
                            project(m + 2, c)
                    values(m, q, NU - 1)

                def finish(b, more):
                    def heads_out(j):
                        if j == 0:
                            pe.wait_ge(yc_ready, after((b + 1) * PAIRS * 2 - 1))
                            if more:
                                pe.wait_ge(qs_ready, after((b + 1) * PAIRS * 4 + 7))
                        pe.wait_ge(z_ready, after(b * BT + j - 2))
                        for i in range(PAIRS):
                            last = pe.transpose(m_all[:, (j % 2) * 2 * HALF + i * P:(j % 2) * 2 * HALF + (i + 1) * P],
                                                yT[:, i, j * P:(j + 1) * P], t.ident)
                        last.then_inc(zt_ready, 1)

                    def output(j):
                        pe.wait_ge(zc_ready, after((b * BT + j) * 2 + 1))
                        if j == 0:
                            pe.wait_ge(ml_ready, after((b + 1) * PAIRS - (0 if more else 1)))
                        pe.wait_ge(res.xo_ready, after(b * BT + j - 1))
                        for k in range(5):
                            last = pe.matmul(o_bank[:, 0:P], zT[:, j % 2, k * P:(k + 1) * P], wo[:, k * P:(k + 1) * P], start=k == 0, stop=k == 4)
                        last.then_inc(o_ready, 1)

                    heads_out(0)
                    for j in range(BT):
                        if j + 1 < BT:
                            heads_out(j + 1)
                        pe.wait_ge(z_ready, after(b * BT + j))
                        pe.wait_ge(zc_ready, after((b * BT + j - 1) * 2 + 1))
                        pe.wait_ge(p_ready, after((b + 1) * PAIRS * 2 * NU - 1))
                        for k in range(5):
                            last = pe.transpose(e_bank[k // 4][:, (k % 4) * P:(k % 4 + 1) * P], z[:, j % 2, k * P:(k + 1) * P], t.ident)
                        last.then_inc(zz_ready, 1)
                        if j >= 1:
                            output(j - 1)
                    output(BT - 1)
                    if more:
                        pe.wait_ge(kc_ready, after(b + 1))
                        pe.wait_ge(res.xo_ready, after(b * BT + BT - 1))

                pipeline(pe, start, pair, finish)

            @block.scalar
            def _(act):
                layernorm_scales(act, t, rstd_ready)
                for s in (xh_ready, kt_ready, qt_ready, mh_ready, p_ready, yc_ready, zc_ready):
                    act.sem_inc(s, LEAD)
                act.wait_ge(w_in, 64)
                act.activation(wd[0][:, :], wd32[:, :], ACT.Copy)
                act.activation(lat[0][:, :], lat32[:, :], ACT.Copy).then_inc(w_high, 1)
                act.wait_ge(w_low, 2)

                def high_x(b):
                    for s in range(2):
                        act.wait_ge(xt_ready, after(b * 2 + s))
                        act.wait_ge(qp_ready, after(b * PAIRS * 4 - 1))
                        act.activation(xT[0][:, s * HALF:(s + 1) * HALF], m_bank[s], ACT.Copy).then_inc(xh_ready, 1)

                def low_keys(b):
                    for s in range(2):
                        act.wait_ge(kp_ready, after(b * 2 + s))
                        act.wait_ge(ks_ready, after((b - 1) * 2 + s))
                        act.activation(kT[:, s, :], m_bank[2 + s][0:STACK, :], ACT.Identity, bias=k_lbias[:, :],
                                       scale=k_low).then_inc(kt_ready, 1)

                def start():
                    high_x(0)
                    low_keys(0)
                    for g in range(4):
                        low_query(0, g)
                    high_max(0, 0)
                    for g in range(4):
                        low_query(1, g)

                def low_query(m, g):
                    act.wait_ge(qp_ready, after(m * 4 + g))
                    act.wait_ge(qs_ready, after(m * 4 + g - 2))
                    act.activation(qT[:, g % 2, :], m_bank[g][0:STACK, :], ACT.Identity, bias=bcur[:, 1, g // 2:g // 2 + 1],
                                   scale=q_low).then_inc(qt_ready, 1)

                def high_max(m, q):
                    act.wait_ge(mt_ready, after(m))
                    act.activation(mh[:, q, :], o_bank[0:16, 0:P], ACT.Copy).then_inc(mh_ready, 1)

                def copy_out(m, i, s):
                    act.wait_ge(y_ready, after(m * 2 + s))
                    act.sem_inc(act_pause, 1)
                    act.activation(yT[:, at(i), s * HALF:(s + 1) * HALF], y_bank[:, :], ACT.Copy).then_inc(yc_ready, 1)

                def pair(m, q, i, b, ahead):
                    for u in range(NU):
                        for c in range(2):
                            act.wait_ge(s_ready, after(m * 2 * NU + 2 * u + c))
                            if c == 0:
                                if u in (0, 1):
                                    act.wait_ge(pv_ready if u == 0 else y_ready, after((m - 1) * (NU - 2) + NU - 3) if u == 0 else after(m * 2 - 1))
                                elif u - 2 == NQ0 - 1:
                                    act.wait_ge(y_ready, after(m * 2))
                                else:
                                    act.wait_ge(pv_ready, after(m * (NU - 2) + (u - 2) - (1 if u - 2 >= NQ0 else 0)))
                            n = 256 if len(units[u][1]) == 1 and units[u][1][0][3] == 256 else HALF
                            act.activation(probs[:, u % 2, c, HALF - n:HALF], e_bank[c][:, HALF - n:HALF], ACT.Exp,
                                           scale=SCORE_SCALE).then_inc(p_ready, 1)
                        if ahead[0] and u == NU - 2:
                            high_max(m + 1, 1 - q)
                        if opens(i, ahead):
                            if u == NU - 2:
                                high_x(b + 1)
                            if u == NU - 1:
                                low_keys(b + 1)
                        if u == NU - 2 and ahead[1] and not opens(i, ahead):
                            for g in range(2):
                                low_query(m + 2, g)
                        if u == NQ0:
                            copy_out(m, i, 0)
                    if ahead[1]:
                        for g in range(0 if opens(i, ahead) else 2, 4):
                            low_query(m + 2, g)
                    copy_out(m, i, 1)

                def finish(b, more):
                    for j in range(BT):
                        act.wait_ge(zz_ready, after(b * BT + j))
                        act.wait_ge(o_ready, after(b * BT + j - 2))
                        act.activation(zT[:, j % 2, 0:HALF], e_bank[0][:, :], ACT.Copy).then_inc(zc_ready, 1)
                        act.activation(zT[:, j % 2, HALF:ZW], e_bank[1][:, 0:P], ACT.Copy).then_inc(zc_ready, 1)

                pipeline(act, start, pair, finish)

            @block.vector
            def _(dve):
                layernorm_reciprocals(dve, t, rstd_ready)
                for s in (xn_ready, xl_ready, ks_ready, v_ready, qs_ready, mx_ready, ml_ready, r_ready, z_ready):
                    dve.sem_inc(s, LEAD)
                res.prime(dve)
                dve.memset(f32(minus[:, :]), -1.0).then_inc(minus_ready, 1)
                dve.wait_ge(w_in, 64)
                dve.tensor_scalar(k_lbias[:, :], k_bias, k_low, None, ALU.mult)
                dve.tensor_scalar(qb_low[:, :], q_bias, q_low, None, ALU.mult).then_inc(w_low, 1)
                dve.wait_ge(w_high, 1)
                dve.tensor_tensor(wd[1][:, :], wd32[:, :], f32(wd[0][:, :]), ALU.subtract)
                dve.tensor_tensor(lat[1][:, :], lat32[:, :], f32(lat[0][:, :]), ALU.subtract).then_inc(w_low, 1)
                dve.wait_ge(k_in, 16)
                dve.wait_ge(const_ready, 2)

                def normalise(b):
                    for j in range(BT):
                        if j % 4 == 0:
                            dve.wait_ge(xt_ready, after((b - 1) * 2 + j // 4))
                        n = b * BT + j
                        dve.tensor_scalar(xn[:, j, :], t.X[:, at(n), :], t.stats[:, at(n), 0], t.rstd[:, at(n)],
                                          ALU.subtract, ALU.mult).then_inc(xn_ready, 1)

                def low_x(b):
                    for s in range(2):
                        half = slice(s * HALF, (s + 1) * HALF)
                        dve.wait_ge(xh_ready, after(b * 2 + s))
                        dve.tensor_tensor(xT[1][:, half], m_bank[s], f32(xT[0][:, half]), ALU.subtract).then_inc(xl_ready, 1)

                def next_keys(b):
                    for s in range(2):
                        dve.wait_ge(kt_ready, after(b * 2 + s))
                        dve.wait_ge(kc_ready, after(b - 1))
                        dve.scalar_tensor_tensor(kN[:, s * HALF:(s + 1) * HALF], m_bank[2 + s][0:STACK, :], k_bias,
                                                 f32(kT[:, s, :]), ALU.add, ALU.subtract).then_inc(ks_ready, 1)
                    dve.wait_ge(vp_ready, after(b))
                    dve.tensor_tensor(VN[:, :, :], o_bank[:, :].rearrange("p (j v) -> p j v", v=VW)[:, :, 0:LAT],
                                      v_bias.unsqueeze(1).to_broadcast([P, BT, LAT]), ALU.add).then_inc(v_ready, 1)

                def start():
                    normalise(0)
                    low_x(0)
                    next_keys(0)
                    for g in range(4):
                        query(0, 0, g)
                    for v in range(16):
                        maximum(0, 0, v)
                    low_max(0, 0)
                    for g in range(4):
                        query(1, 1, g)

                def query(m, q, g):
                    c, s = g // 2, g % 2
                    dve.wait_ge(qt_ready, after(m * 4 + g))
                    dve.wait_ge(s_ready, after((m - 1) * 2 * NU - 1))
                    dve.scalar_tensor_tensor(qS[q][c][0:STACK, s * HALF:(s + 1) * HALF], m_bank[g][0:STACK, :],
                                             bcur[:, 0, c:c + 1], f32(qT[:, g % 2, :]), ALU.add, ALU.subtract).then_inc(qs_ready, 1)

                def maximum(m, q, v):
                    dve.wait_ge(sm_ready, after(m * 16 + v))
                    base = (v % 2) * 2 * HALF
                    dve.reduce_max(mx[:, q, v:v + 1], m_all[:, base:base + (v % 8 + 1) * P], AX.X).then_inc(mx_ready, 1)

                def low_max(m, q):
                    dve.wait_ge(mh_ready, after(m))
                    dve.tensor_tensor(ml[:, q, :], o_bank[0:16, 0:P], f32(mh[:, q, :]), ALU.subtract).then_inc(ml_ready, 1)

                def pair(m, q, i, b, ahead):
                    if ahead[0]:
                        for v in range(9):
                            maximum(m + 1, 1 - q, v)
                    if opens(i, ahead):
                        normalise(b + 1)
                    if ahead[0]:
                        for v in range(9, 16):
                            maximum(m + 1, 1 - q, v)
                        low_max(m + 1, 1 - q)
                    if opens(i, ahead):
                        low_x(b + 1)
                        next_keys(b + 1)
                    if ahead[1]:
                        for g in range(4):
                            query(m + 2, q, g)

                def finish(b, more):
                    for j in range(BT):
                        n = b * BT + j
                        heads = m_all[:, (j % 2) * 2 * HALF:(j % 2 + 1) * 2 * HALF].rearrange("p (h v) -> p h v", v=VW)
                        dve.wait_ge(zt_ready, after(n))
                        dve.reciprocal(rcp[:, j % 2, :], heads[:, :, LAT]).then_inc(r_ready, 1)
                        dve.wait_ge(r_ready, after(n))
                        dve.wait_ge(zz_ready, after(n - 2))
                        dve.tensor_tensor(z[:, j % 2, 0:HEADS * LAT].rearrange("p (h v) -> p h v", v=LAT), heads[:, :, 0:LAT],
                                          rcp[:, j % 2, :].unsqueeze(2).to_broadcast([P, HEADS, LAT]), ALU.mult).then_inc(z_ready, 1)
                        if j >= 2:
                            add_output(b * BT + j - 2, j % 2)
                    for j in range(BT - 2, BT):
                        add_output(b * BT + j, j % 2)

                def add_output(n, q):
                    dve.wait_ge(o_ready, after(n))
                    res.add(dve, n, q, n, o_bank[:, 0:P])

                pipeline(dve, start, pair, finish)
        sem.clear()


def attn1_weights(ctx, nc, t):
    t.wd = ctx.enter_context(nc.sbuf_tensor("attn1_wd", [P, HEADS * STACK], F32))
    t.latent = ctx.enter_context(nc.sbuf_tensor("attn1_latent", [P, STACK], F32))
    t.wo = ctx.enter_context(nc.sbuf_tensor("attn1_wo", [P, ZW], F32))
    t.attn1_small = ctx.enter_context(nc.sbuf_tensor("attn1_small", [P, L1_COLS], F32))
    t.attn1_in = ctx.enter_context(nc.semaphore("attn1_in"))


def attn1_load(sp, t, d):
    for tile, name in ((t.wd, "wd"), (t.latent, "latent"), (t.wo, "wo"), (t.attn1_small, "attn1_small")):
        sp.dma_start(tile[:, :], d[name]).then_inc(t.attn1_in, 16)


def attn1_laid_out(np, a, r):
    wd = np.repeat(a["L1_attn_Wd_w"].transpose(1, 0, 2)[:, :, None, :], 3, axis=2)
    r["wd"] = wd.reshape(P, HEADS * STACK)
    r["latent"] = np.tile(a["L1_attn_latent_w"], (1, 3))
    wo = np.zeros((ZW, DIM), np.float32)
    wo[0:HEADS * LAT] = a["L1_attn_out_w"]
    wo[HEADS * LAT] = a["L1_attn_out_b"]
    r["wo"] = wo.reshape(5, P, DIM).transpose(1, 0, 2).reshape(P, ZW)
    small = np.zeros((P, L1_COLS), np.float32)
    small[:, 0:LAT] = a["L1_attn_latent_b"]
    small[0:STACK, 36] = np.tile(a["L1_attn_latent_b"], 3)
    small[LAT:2 * LAT, 37] = 1.0
    small[2 * LAT:STACK, 38] = 1.0
    small[0:STACK, 40:40 + HEADS] = np.tile(a["L1_attn_Wd_b"].T, (3, 1))
    r["attn1_small"] = small


def macaron(nc, d, out):
    t = Shared()
    with ExitStack() as ctx:
        def sb(name, shape, dt=F32):
            return ctx.enter_context(nc.sbuf_tensor(name, shape, dt))

        t.X = sb("X", [P, TILES, DIM])
        t.stats = sb("stats", [P, TILES, 2])
        t.rstd = sb("rstd", [P, TILES])
        t.consts = sb("consts", [P, CONSTS])
        t.ident = t.consts[:, C_IDENT:C_IDENT + P]
        t.bconsts = sb("bconsts", [P, CONSTS - C_IDENT], BF16)
        t.identb = t.bconsts[:, 0:P]
        t.neg_qk = t.bconsts[:, C_NEG_QK - C_IDENT:C_NEG_KQ - C_IDENT]
        t.neg_kq = t.bconsts[:, C_NEG_KQ - C_IDENT:C_NEG_KQ - C_IDENT + HALF]
        t.iota8 = t.consts[:, C_IOTA:C_IOTA + EXPERTS]
        with ExitStack() as layer0:
            attn0_weights(layer0, nc, t)
            moe_phase(nc, t, d, "moe0", True, lambda sp: attn0_load(sp, t, d))
            attn0_phase(nc, t, "attn0")

        def load_ahead(sp):
            ffn_load(sp, t, d)
            attn1_load(sp, t, d)

        with ExitStack() as layer1:
            ffn_weights(layer1, nc, t)
            attn1_weights(layer1, nc, t)
            moe_phase(nc, t, d, "moe1", False, load_ahead)
            ffn_phase(nc, t, "ffn0")
            attn1_phase(nc, t, "attn1")
            ffn_phase(nc, t, "ffn1")
        store_phase(nc, t, out)


def store_phase(nc, t, out):
    with nc.semaphore("out_done") as out_done, nc.Block() as block:
        @block.sync
        def _(sp):
            sp.dma_start(out.rearrange("(n p) c -> p n c", p=P), t.X[:, :, :]).then_inc(out_done, 16)
            sp.wait_ge(out_done, 16)


C_EPS, C_IOTA, C_IDENT = 0, 8, 16
C_NEG_QK = C_IDENT + P
C_NEG_KQ = C_NEG_QK + P
CONSTS = C_NEG_KQ + HALF
NEG = -1e30


def constants(np):
    c = np.zeros((P, CONSTS), np.float32)
    c[:, C_EPS] = EPS
    c[:, C_IOTA:C_IOTA + EXPERTS] = np.arange(EXPERTS)
    c[:, C_IDENT:C_IDENT + P] = np.eye(P)
    c[:, C_NEG_QK:C_NEG_KQ] = NEG * np.triu(np.ones((P, P)), 1)
    c[:, C_NEG_KQ:] = np.tile(NEG * np.tril(np.ones((P, P)), -1), (1, 4))
    return c


def laid_out(inputs):
    import numpy as np

    a = {k: np.asarray(v) for k, v in inputs.items()}
    r = {}
    r["x"] = a["L0_attn_x"].reshape(BATCH * SEQ, DIM)
    r["w_gate"] = a["L0_ffn_w_gate"].transpose(2, 0, 1).reshape(P, EXPERTS * INNER)
    r["w_up"] = a["L0_ffn_w_up"].transpose(2, 0, 1).reshape(P, EXPERTS * INNER)
    r["w_down"] = a["L0_ffn_w_down"].reshape(EXPERTS, DIM, KC, P).transpose(3, 2, 0, 1).reshape(P, KC * EXPERTS * DIM)
    r["routers"] = np.concatenate([
        a["L0_ffn_router_gate"].T, a["L0_ffn_router_up"].T,
        a["L0_ffn_router_down"].reshape(EXPERTS, KC, P).transpose(2, 1, 0).reshape(P, KC * EXPERTS)], axis=1)
    r["consts"] = constants(np)
    attn0_laid_out(np, a, r)
    ffn_laid_out(np, a, r)
    attn1_laid_out(np, a, r)
    return {k: np.ascontiguousarray(v) for k, v in r.items()}


def kernel(**inputs):
    import concourse.bacc as bacc
    from concourse.bass_utils import run_bass_kernel_spmd

    nc = bacc.Bacc("TRN2", target_bir_lowering=False, num_devices=1)
    arrays = {f"in_{k}": v for k, v in laid_out(inputs).items()}
    d = {k[3:]: nc.dram_tensor(k, v.shape, mybir.dt.from_np(v.dtype), kind="ExternalInput").ap() for k, v in arrays.items()}
    out = nc.dram_tensor("out", (BATCH * SEQ, DIM), F32, kind="ExternalOutput").ap()
    macaron(nc, d, out)
    r = run_bass_kernel_spmd(nc, [arrays], core_ids=[0])
    return r.results[0]["out"].reshape(BATCH, SEQ, DIM)
```
